# Optimizing a Trainium2 kernel written in Bass

```python
import numpy as np
import jax
import jax.numpy as jnp

def _softmax(x, axis=-1):
    return jax.nn.softmax(x, axis=axis)

def _gelu(x):
    return jax.nn.gelu(x, approximate=True)

def _silu(x):
    return jax.nn.silu(x)

def _sigmoid(x):
    return jax.nn.sigmoid(x)

def _layernorm(x, axis=-1, eps=1e-05):
    m = jnp.mean(x, axis=axis, keepdims=True)
    v = jnp.var(x, axis=axis, keepdims=True)
    return (x - m) / jnp.sqrt(v + eps)

def _scatter_add(tgt, idx, src, axis=0):
    return tgt.at[idx].add(src)

def _segment_sum(src, seg, n):
    return jax.ops.segment_sum(src, seg, n)
kernel_name = 'mk_decoder_preln_d4_seqx_r8_5064a4'

def setup_inputs(seed: int=0):
    np.random.seed(seed)
    _w = jnp.asarray

    def _rec_inputs():
        import jax
        import jax.numpy as jnp
        _rk = jax.random.key(seed)
        x = -0.0003929 + 0.9999 * jax.random.normal(jax.random.fold_in(_rk, 1), (32, 56, 128), jnp.float32)
        _lenS = 56 - jax.random.randint(jax.random.fold_in(_rk, 7), (32,), 0, max(1, 56 // 4) + 1, jnp.int32)
        _lenS2 = 1500 - jax.random.randint(jax.random.fold_in(_rk, 8), (32,), 0, max(1, 1500 // 4) + 1, jnp.int32)
        _ctx_768P = jax.random.normal(jax.random.fold_in(_rk, 11), (32, 16, 96), jnp.float32)
        _ctx_768c = jax.random.dirichlet(jax.random.fold_in(_rk, 511), 0.3 * jnp.ones((16,), jnp.float32), (32, 1500))
        _ctx_768t = jnp.einsum('bsk,bkd->bsd', _ctx_768c, _ctx_768P)
        _ctx_768t = _ctx_768t * jax.lax.rsqrt(jnp.mean(jnp.square(_ctx_768t)) + 1e-12) * 0.953939
        ctx_768 = -7.36909e-05 + 0.999899 * (_ctx_768t + 0.3 * jax.random.normal(jax.random.fold_in(_rk, 611), (32, 1500, 96), jnp.float32))
        _validS = jnp.arange(56)[None, :] < _lenS[:, None]
        _validS2 = jnp.arange(1500)[None, :] < _lenS2[:, None]
        _causal = jnp.tril(jnp.ones((56, 56), dtype=bool))
        mask_BxS_bf1 = jnp.ones((32, 56), dtype=bool)
        mask_BxS2_bf1 = jnp.ones((32, 1500), dtype=bool)
        return (x, ctx_768, mask_BxS_bf1, mask_BxS2_bf1)
    x, ctx_768, mask_BxS_bf1, mask_BxS2_bf1 = _rec_inputs()

    def _L0_attn_setup():
        import jax, jax.numpy as jnp
        import numpy as np
        DIM = 128
        HEADS = 16
        DIM_HEAD = 64
        INNER = HEADS * DIM_HEAD
        SEQ = 512
        BATCH = 1
        key = jax.random.key(seed)
        ks = jax.random.split(key, 6)
        s = 0.02
        return {'x': jax.random.normal(ks[0], (BATCH, SEQ, DIM), dtype=jnp.float32), 'Wq': jax.random.normal(ks[1], (DIM, INNER), dtype=jnp.float32) * s, 'Wk': jax.random.normal(ks[2], (DIM, INNER), dtype=jnp.float32) * s, 'Wv': jax.random.normal(ks[3], (DIM, INNER), dtype=jnp.float32) * s, 'Wo': jax.random.normal(ks[4], (INNER, DIM), dtype=jnp.float32) * s, 'bo': jax.random.normal(ks[5], (DIM,), dtype=jnp.float32) * s}
    _L0_attn_all = _L0_attn_setup()
    _L0_attn_in = {k: v for k, v in _L0_attn_all.items() if k in ('Wq', 'Wk', 'Wv', 'Wo', 'bo')}
    del _L0_attn_all

    def _L0_xattn_setup():
        import jax, jax.numpy as jnp
        import numpy as np
        EPS = 1e-05

        def layernorm(x, g, b):
            mu = jnp.mean(x, axis=-1, keepdims=True)
            var = jnp.mean(jnp.square(x - mu), axis=-1, keepdims=True)
            return (x - mu) * jax.lax.rsqrt(var + EPS) * g + b
        key = jax.random.key(seed)
        ks = jax.random.split(key, 12)
        B, L1, L2 = (8, 256, 256)
        D1, D2, E = (128, 96, 128)
        s1, s2, se = (D1 ** (-0.5), D2 ** (-0.5), E ** (-0.5))
        return {'modality1': jax.random.normal(ks[0], (B, L1, D1), jnp.float32), 'modality2': jax.random.normal(ks[1], (B, L2, D2), jnp.float32), 'ln1_g': jnp.ones((D1,), jnp.float32), 'ln1_b': jnp.zeros((D1,), jnp.float32), 'ln2_g': jnp.ones((D2,), jnp.float32), 'ln2_b': jnp.zeros((D2,), jnp.float32), 'Wq': jax.random.normal(ks[2], (D1, E), jnp.float32) * s1, 'bq': jax.random.normal(ks[3], (E,), jnp.float32) * 0.01, 'Wk': jax.random.normal(ks[4], (D2, E), jnp.float32) * s2, 'bk': jax.random.normal(ks[5], (E,), jnp.float32) * 0.01, 'Wv': jax.random.normal(ks[6], (D2, E), jnp.float32) * s2, 'bv': jax.random.normal(ks[7], (E,), jnp.float32) * 0.01, 'Wo': jax.random.normal(ks[8], (E, D1), jnp.float32) * se, 'bo': jax.random.normal(ks[9], (D1,), jnp.float32) * 0.01}
    _L0_xattn_all = _L0_xattn_setup()
    _L0_xattn_in = {k: v for k, v in _L0_xattn_all.items() if k in ('ln1_g', 'ln1_b', 'ln2_g', 'ln2_b', 'Wq', 'bq', 'Wk', 'bk', 'Wv', 'bv', 'Wo', 'bo')}
    del _L0_xattn_all

    def _L0_ffn_setup():
        import jax, jax.numpy as jnp
        import numpy as np
        D = 128
        F = 4 * D
        E = 8
        NS = 2
        TOP_K = 2
        B, S = (2, 128)
        key = jax.random.key(seed)
        ks = jax.random.split(key, 7)
        w = 1.0 / np.sqrt(D)
        wf = 1.0 / np.sqrt(F)
        return {'x': jax.random.normal(ks[0], (B, S, D), jnp.float32), 'centroids': jax.random.normal(ks[1], (E, D), jnp.float32) * w, 'routing_bias': jnp.zeros((E,), jnp.float32), 'Wfc_r': jax.random.normal(ks[2], (E, F, D), jnp.float32) * w, 'Wproj_r': jax.random.normal(ks[3], (E, D, F), jnp.float32) * wf, 'Wfc_sh': jax.random.normal(ks[4], (NS, F, D), jnp.float32) * w, 'Wproj_sh': jax.random.normal(ks[5], (NS, D, F), jnp.float32) * wf}
    _L0_ffn_all = _L0_ffn_setup()
    _L0_ffn_in = {k: v for k, v in _L0_ffn_all.items() if k in ('centroids', 'routing_bias', 'Wfc_r', 'Wproj_r', 'Wfc_sh', 'Wproj_sh')}
    del _L0_ffn_all

    def _L1_attn_setup():
        import math
        import jax, jax.numpy as jnp
        import numpy as np
        B, T, D, H = (4, 128, 128, 8)
        HD = D // H

        def _trigram_dirs():
            t = np.array([[(i >> b & 1) * 2 - 1 for b in (2, 1, 0)] for i in range(8)], dtype=np.float32)
            return jnp.asarray(t / np.linalg.norm(t, axis=1, keepdims=True))
        key = jax.random.key(seed)
        k1, k2, k3, k4 = jax.random.split(key, 4)
        x = jax.random.normal(k1, (B, T, D), dtype=jnp.float32)
        Wqkv = jax.random.normal(k2, (D, 3 * D), dtype=jnp.float32) * 0.02
        Wout = jax.random.normal(k3, (D, D), dtype=jnp.float32) * 0.02
        head_scales = jax.random.normal(k4, (H,), dtype=jnp.float32) * 0.1
        head_dirs = _trigram_dirs()
        return {'x': x, 'Wqkv': Wqkv, 'Wout': Wout, 'head_scales': head_scales, 'head_dirs': head_dirs}
    _L1_attn_all = _L1_attn_setup()
    _L1_attn_in = {k: v for k, v in _L1_attn_all.items() if k in ('Wqkv', 'Wout', 'head_scales', 'head_dirs')}
    del _L1_attn_all

    def _L1_xattn_setup():
        import jax, jax.numpy as jnp
        import numpy as np
        HEADS = 8
        DIM_HEAD = 64
        SCALE = DIM_HEAD ** (-0.5)
        key = jax.random.key(seed)
        ks = jax.random.split(key, 7)
        B, Nq, Nc = (4, 256, 256)
        Dq, Dc = (128, 96)
        inner = HEADS * DIM_HEAD
        x = jax.random.normal(ks[0], (B, Nq, Dq), dtype=jnp.float32)
        context = jax.random.normal(ks[1], (B, Nc, Dc), dtype=jnp.float32)
        Wq = jax.random.normal(ks[2], (Dq, inner), dtype=jnp.float32) * Dq ** (-0.5)
        Wk = jax.random.normal(ks[3], (Dc, inner), dtype=jnp.float32) * Dc ** (-0.5)
        Wv = jax.random.normal(ks[4], (Dc, inner), dtype=jnp.float32) * Dc ** (-0.5)
        Wo = jax.random.normal(ks[5], (inner, Dq), dtype=jnp.float32) * inner ** (-0.5)
        bo = jax.random.normal(ks[6], (Dq,), dtype=jnp.float32) * 0.01
        return {'x': x, 'context': context, 'Wq': Wq, 'Wk': Wk, 'Wv': Wv, 'Wo': Wo, 'bo': bo}
    _L1_xattn_all = _L1_xattn_setup()
    _L1_xattn_in = {k: v for k, v in _L1_xattn_all.items() if k in ('Wq', 'Wk', 'Wv', 'Wo', 'bo')}
    del _L1_xattn_all

    def _L1_ffn_setup():
        import jax, jax.numpy as jnp
        import numpy as np
        B, T, C, E, K, CAP, H = (8, 256, 128, 8, 2, 512, 512)
        key = jax.random.key(seed)
        ks = jax.random.split(key, 6)
        s = 0.02
        return {'x': jax.random.normal(ks[0], (B, T, C), jnp.float32), 'rw1': s * jax.random.normal(ks[1], (C, H), jnp.float32), 'rb1': jnp.zeros((H,), jnp.float32), 'rw2': s * jax.random.normal(ks[2], (H, E), jnp.float32), 'rb2': jnp.zeros((E,), jnp.float32), 'ew1': s * jax.random.normal(ks[3], (E, C, H), jnp.float32), 'eb1': jnp.zeros((E, H), jnp.float32), 'ew2': s * jax.random.normal(ks[4], (E, H, C), jnp.float32), 'eb2': jnp.zeros((E, C), jnp.float32)}
    _L1_ffn_all = _L1_ffn_setup()
    _L1_ffn_in = {k: v for k, v in _L1_ffn_all.items() if k in ('rw1', 'rb1', 'rw2', 'rb2', 'ew1', 'eb1', 'ew2', 'eb2')}
    del _L1_ffn_all

    def _L2_attn_setup():
        import jax, jax.numpy as jnp
        import numpy as np
        B, S, D, H = (2, 256, 128, 16)
        DH = D // H
        EPS = 1e-05
        LAMBDA_INIT = 0.8
        key = jax.random.key(seed)
        ks = jax.random.split(key, 16)
        w_std = 1.0 / np.sqrt(D)
        lam_std = LAMBDA_INIT / np.sqrt(DH)
        return {'x': jax.random.normal(ks[0], (B, S, D), jnp.float32), 'Wq': jax.random.normal(ks[1], (D, D), jnp.float32) * w_std, 'bq': jax.random.normal(ks[2], (D,), jnp.float32) * 0.02, 'Wk': jax.random.normal(ks[3], (D, D), jnp.float32) * w_std, 'bk': jax.random.normal(ks[4], (D,), jnp.float32) * 0.02, 'Wv': jax.random.normal(ks[5], (D, D), jnp.float32) * w_std, 'bv': jax.random.normal(ks[6], (D,), jnp.float32) * 0.02, 'Wo': jax.random.normal(ks[7], (D, D), jnp.float32) * w_std, 'bo': jax.random.normal(ks[8], (D,), jnp.float32) * 0.02, 'lq1': jax.random.normal(ks[9], (H, DH), jnp.float32) * lam_std, 'lk1': jax.random.normal(ks[10], (H, DH), jnp.float32) * lam_std, 'lq2': jax.random.normal(ks[11], (H, DH), jnp.float32) * lam_std, 'lk2': jax.random.normal(ks[12], (H, DH), jnp.float32) * lam_std, 'gn_w': jnp.ones((H, DH), jnp.float32), 'gn_b': jnp.zeros((H, DH), jnp.float32)}
    _L2_attn_all = _L2_attn_setup()
    _L2_attn_in = {k: v for k, v in _L2_attn_all.items() if k in ('Wq', 'bq', 'Wk', 'bk', 'Wv', 'bv', 'Wo', 'bo', 'lq1', 'lk1', 'lq2', 'lk2', 'gn_w', 'gn_b')}
    del _L2_attn_all

    def _L2_xattn_setup():
        import jax, jax.numpy as jnp
        import numpy as np
        B, T, DT, G, DV = (16, 64, 128, 72, 96)
        H, DH = (4, 32)
        INNER = H * DH
        HID = 4 * DT
        N_STATE = 64
        K_TOP = 32

        def layernorm(x, g, b, eps=1e-05):
            m = x.mean(-1, keepdims=True)
            v = x.var(-1, keepdims=True)
            return (x - m) * jax.lax.rsqrt(v + eps) * g + b

        def s4d(x, log_dt, A_re, A_im, C_re, C_im, D_skip):
            Bb, L, D = x.shape
            dt = jnp.exp(log_dt)
            A = A_re + 1j * A_im
            C = C_re + 1j * C_im
            dtA = dt[:, None] * A
            dC = C * (jnp.exp(dtA) - 1.0) / A
            powers = jnp.exp(dtA[:, :, None] * jnp.arange(L))
            K = 2.0 * jnp.einsum('dn,dnl->dl', dC, powers).real
            n = 2 * L
            Kf = jnp.fft.rfft(K, n=n, axis=-1)
            xf = jnp.fft.rfft(x, n=n, axis=1)
            y = jnp.fft.irfft(xf * Kf.T[None], n=n, axis=1)[:, :L]
            return y + x * D_skip
        key = jax.random.key(seed)
        ks = jax.random.split(key, 16)
        s = 0.02
        inp = {'x_text': jax.random.normal(ks[0], (B, T, DT), jnp.float32), 'x_vision': jax.random.normal(ks[1], (B, G, DV), jnp.float32), 'text_mask': jnp.ones((B, T), bool), 'vision_mask': jnp.ones((B, G), bool), 'Wq': jax.random.normal(ks[2], (DT, INNER), jnp.float32) * s, 'Wk': jax.random.normal(ks[3], (DV, INNER), jnp.float32) * s, 'Wv': jax.random.normal(ks[4], (DV, DT), jnp.float32) * s, 'W_film_in': jax.random.normal(ks[5], (DT, 2 * DT), jnp.float32) * s, 'b_film_in': jnp.zeros((2 * DT,), jnp.float32), 'W_film_out': jax.random.normal(ks[6], (DT, 2 * DT), jnp.float32) * s, 'b_film_out': jnp.zeros((2 * DT,), jnp.float32), 'g_norm_in': jnp.ones((DT,), jnp.float32), 'b_norm_in': jnp.zeros((DT,), jnp.float32), 'g_norm_out': jnp.ones((DT,), jnp.float32), 'b_norm_out': jnp.zeros((DT,), jnp.float32), 'g_ffn': jnp.ones((DT,), jnp.float32), 'b_ffn': jnp.zeros((DT,), jnp.float32), 'W1': jax.random.normal(ks[7], (DT, HID), jnp.float32) * s, 'b1': jnp.zeros((HID,), jnp.float32), 'W2': jax.random.normal(ks[8], (HID, DT), jnp.float32) * s, 'b2': jnp.zeros((DT,), jnp.float32), 'log_dt': jnp.log(0.001) + jax.random.uniform(ks[9], (DT,), jnp.float32) * (jnp.log(0.1) - jnp.log(0.001)), 'A_re': -0.5 * jnp.ones((DT, N_STATE), jnp.float32), 'A_im': jnp.tile(jnp.pi * jnp.arange(N_STATE, dtype=jnp.float32), (DT, 1)), 'C_re': jax.random.normal(ks[10], (DT, N_STATE), jnp.float32) * 0.5 ** 0.5, 'C_im': jax.random.normal(ks[11], (DT, N_STATE), jnp.float32) * 0.5 ** 0.5, 'D_skip': jax.random.normal(ks[12], (DT,), jnp.float32), 'mod_gate': jnp.array(0.5, jnp.float32)}
        return inp
    _L2_xattn_all = _L2_xattn_setup()
    _L2_xattn_in = {k: v for k, v in _L2_xattn_all.items() if k in ('Wq', 'Wk', 'Wv', 'W_film_in', 'b_film_in', 'W_film_out', 'b_film_out', 'g_norm_in', 'b_norm_in', 'g_norm_out', 'b_norm_out', 'g_ffn', 'b_ffn', 'W1', 'b1', 'W2', 'b2', 'log_dt', 'A_re', 'A_im', 'C_re', 'C_im', 'D_skip', 'mod_gate')}
    del _L2_xattn_all

    def _L2_ffn_setup():
        import jax, jax.numpy as jnp
        import numpy as np
        B, L, D, E, H, TOP_K = (4, 256, 128, 8, 64, 2)
        key = jax.random.key(seed)
        k = jax.random.split(key, 6)
        x = jax.random.normal(k[0], (B, L, D), dtype=jnp.float32)
        gate_w = jax.random.normal(k[1], (D, E), dtype=jnp.float32) * 0.02
        gate_b = jnp.zeros((E,), jnp.float32)
        w1 = jax.random.normal(k[2], (E, D, H), dtype=jnp.float32) * 0.02
        b1 = jnp.zeros((E, H), jnp.float32)
        w2 = jax.random.normal(k[3], (E, H, D), dtype=jnp.float32) * 0.02
        b2 = jnp.zeros((E, D), jnp.float32)
        return {'x': x, 'gate_w': gate_w, 'gate_b': gate_b, 'w1': w1, 'b1': b1, 'w2': w2, 'b2': b2}
    _L2_ffn_all = _L2_ffn_setup()
    _L2_ffn_in = {k: v for k, v in _L2_ffn_all.items() if k in ('gate_w', 'gate_b', 'w1', 'b1', 'w2', 'b2')}
    del _L2_ffn_all

    def _L3_attn_setup():
        import jax, jax.numpy as jnp
        import numpy as np
        import math
        B, S, E = (2, 256, 128)
        H, DC, DR = (16, 32, 128)
        HD = E // H

        def _linear_params(key, din, dout):
            k1, k2 = jax.random.split(key)
            bound = 1.0 / math.sqrt(din)
            w = jax.random.uniform(k1, (din, dout), minval=-bound, maxval=bound, dtype=jnp.float32)
            b = jax.random.uniform(k2, (dout,), minval=-bound, maxval=bound, dtype=jnp.float32)
            return (w, b)

        def _gelu(x):
            return jax.nn.gelu(x, approximate=False)

        def _rope_cos_sin(seq_len, d_rope):
            inv_freq = 1.0 / 10000.0 ** (jnp.arange(0, d_rope, 2, dtype=jnp.float32) / d_rope)
            t = jnp.arange(seq_len, dtype=jnp.float32)
            freqs = t[:, None] * inv_freq[None, :]
            emb = jnp.concatenate([freqs, freqs], axis=-1)
            return (jnp.cos(emb), jnp.sin(emb))

        def _apply_rope(x, cos, sin):
            d = x.shape[-1]
            x1, x2 = (x[..., :d // 2], x[..., d // 2:])
            rot = jnp.concatenate([-x2, x1], axis=-1)
            return x * cos + rot * sin
        key = jax.random.key(seed)
        ks = jax.random.split(key, 10)
        x = jax.random.normal(ks[0], (B, S, E), dtype=jnp.float32)
        wq, bq = _linear_params(ks[1], E, DC)
        wqc, bqc = _linear_params(ks[2], DC, E - DR)
        wqr, bqr = _linear_params(ks[3], E, DR)
        wkv, bkv = _linear_params(ks[4], E, DC)
        wkr, bkr = _linear_params(ks[5], E, DR)
        wkc, bkc = _linear_params(ks[6], DC, E - DR)
        wv, bv = _linear_params(ks[7], DC, E)
        wo, bo = _linear_params(ks[8], E, E)
        return dict(x=x, wq=wq, bq=bq, wqc=wqc, bqc=bqc, wqr=wqr, bqr=bqr, wkv=wkv, bkv=bkv, wkr=wkr, bkr=bkr, wkc=wkc, bkc=bkc, wv=wv, bv=bv, wo=wo, bo=bo)
    _L3_attn_all = _L3_attn_setup()
    _L3_attn_in = {k: v for k, v in _L3_attn_all.items() if k in ('wq', 'bq', 'wqc', 'bqc', 'wqr', 'bqr', 'wkv', 'bkv', 'wkr', 'bkr', 'wkc', 'bkc', 'wv', 'bv', 'wo', 'bo')}
    del _L3_attn_all

    def _L3_xattn_setup():
        import jax, jax.numpy as jnp
        import numpy as np
        QUERY_DIM = 128
        CONTEXT_DIM = 96
        HEADS = 8
        DIM_HEAD = 64
        INNER = HEADS * DIM_HEAD
        key = jax.random.key(seed)
        ks = jax.random.split(key, 7)
        B, S, L = (8, 512, 77)
        x = jax.random.normal(ks[0], (B, S, QUERY_DIM), dtype=jnp.float32)
        context = jax.random.normal(ks[1], (B, L, CONTEXT_DIM), dtype=jnp.float32)
        Wq = jax.random.normal(ks[2], (QUERY_DIM, INNER), dtype=jnp.float32) * QUERY_DIM ** (-0.5)
        Wk = jax.random.normal(ks[3], (CONTEXT_DIM, INNER), dtype=jnp.float32) * CONTEXT_DIM ** (-0.5)
        Wv = jax.random.normal(ks[4], (CONTEXT_DIM, INNER), dtype=jnp.float32) * CONTEXT_DIM ** (-0.5)
        Wo = jax.random.normal(ks[5], (INNER, QUERY_DIM), dtype=jnp.float32) * INNER ** (-0.5)
        bo = jax.random.normal(ks[6], (QUERY_DIM,), dtype=jnp.float32) * 0.01
        return {'x': x, 'context': context, 'Wq': Wq, 'Wk': Wk, 'Wv': Wv, 'Wo': Wo, 'bo': bo}
    _L3_xattn_all = _L3_xattn_setup()
    _L3_xattn_in = {k: v for k, v in _L3_xattn_all.items() if k in ('Wq', 'Wk', 'Wv', 'Wo', 'bo')}
    del _L3_xattn_all

    def _L3_ffn_setup():
        import jax, jax.numpy as jnp
        import numpy as np
        TOP_K = 2
        key = jax.random.key(seed)
        ks = jax.random.split(key, 7)
        B_, S, D, F, E, R = (2, 256, 128, 512, 4, 4)
        x = jax.random.normal(ks[0], (B_, S, D), dtype=jnp.float32)
        Wg = jax.random.normal(ks[1], (E, D), dtype=jnp.float32) * (1.0 / np.sqrt(D))
        bg = jnp.zeros((E,), dtype=jnp.float32)
        Wi = jax.random.normal(ks[2], (F, D), dtype=jnp.float32) * (1.0 / np.sqrt(D))
        Wo = jax.random.normal(ks[3], (D, F), dtype=jnp.float32) * (1.0 / np.sqrt(F))
        A = jax.random.normal(ks[4], (E, R, D), dtype=jnp.float32) * (1.0 / np.sqrt(D))
        Bm = jax.random.normal(ks[5], (E, F, R), dtype=jnp.float32) * 0.01
        return {'x': x, 'Wg': Wg, 'bg': bg, 'Wi': Wi, 'Wo': Wo, 'A': A, 'B': Bm}
    _L3_ffn_all = _L3_ffn_setup()
    _L3_ffn_in = {k: v for k, v in _L3_ffn_all.items() if k in ('Wg', 'bg', 'Wi', 'Wo', 'A', 'B')}
    del _L3_ffn_all
    return {'x': x, 'ctx_768': ctx_768, 'mask_BxS_bf1': mask_BxS_bf1, 'mask_BxS2_bf1': mask_BxS2_bf1, 'L0_attn_Wq': _L0_attn_in['Wq'], 'L0_attn_Wk': _L0_attn_in['Wk'], 'L0_attn_Wv': _L0_attn_in['Wv'], 'L0_attn_Wo': _L0_attn_in['Wo'], 'L0_attn_bo': _L0_attn_in['bo'], 'L0_xattn_ln1_g': _L0_xattn_in['ln1_g'], 'L0_xattn_ln1_b': _L0_xattn_in['ln1_b'], 'L0_xattn_ln2_g': _L0_xattn_in['ln2_g'], 'L0_xattn_ln2_b': _L0_xattn_in['ln2_b'], 'L0_xattn_Wq': _L0_xattn_in['Wq'], 'L0_xattn_bq': _L0_xattn_in['bq'], 'L0_xattn_Wk': _L0_xattn_in['Wk'], 'L0_xattn_bk': _L0_xattn_in['bk'], 'L0_xattn_Wv': _L0_xattn_in['Wv'], 'L0_xattn_bv': _L0_xattn_in['bv'], 'L0_xattn_Wo': _L0_xattn_in['Wo'], 'L0_xattn_bo': _L0_xattn_in['bo'], 'L0_ffn_centroids': _L0_ffn_in['centroids'], 'L0_ffn_routing_bias': _L0_ffn_in['routing_bias'], 'L0_ffn_Wfc_r': _L0_ffn_in['Wfc_r'], 'L0_ffn_Wproj_r': _L0_ffn_in['Wproj_r'], 'L0_ffn_Wfc_sh': _L0_ffn_in['Wfc_sh'], 'L0_ffn_Wproj_sh': _L0_ffn_in['Wproj_sh'], 'L1_attn_Wqkv': _L1_attn_in['Wqkv'], 'L1_attn_Wout': _L1_attn_in['Wout'], 'L1_attn_head_scales': _L1_attn_in['head_scales'], 'L1_attn_head_dirs': _L1_attn_in['head_dirs'], 'L1_xattn_Wq': _L1_xattn_in['Wq'], 'L1_xattn_Wk': _L1_xattn_in['Wk'], 'L1_xattn_Wv': _L1_xattn_in['Wv'], 'L1_xattn_Wo': _L1_xattn_in['Wo'], 'L1_xattn_bo': _L1_xattn_in['bo'], 'L1_ffn_rw1': _L1_ffn_in['rw1'], 'L1_ffn_rb1': _L1_ffn_in['rb1'], 'L1_ffn_rw2': _L1_ffn_in['rw2'], 'L1_ffn_rb2': _L1_ffn_in['rb2'], 'L1_ffn_ew1': _L1_ffn_in['ew1'], 'L1_ffn_eb1': _L1_ffn_in['eb1'], 'L1_ffn_ew2': _L1_ffn_in['ew2'], 'L1_ffn_eb2': _L1_ffn_in['eb2'], 'L2_attn_Wq': _L2_attn_in['Wq'], 'L2_attn_bq': _L2_attn_in['bq'], 'L2_attn_Wk': _L2_attn_in['Wk'], 'L2_attn_bk': _L2_attn_in['bk'], 'L2_attn_Wv': _L2_attn_in['Wv'], 'L2_attn_bv': _L2_attn_in['bv'], 'L2_attn_Wo': _L2_attn_in['Wo'], 'L2_attn_bo': _L2_attn_in['bo'], 'L2_attn_lq1': _L2_attn_in['lq1'], 'L2_attn_lk1': _L2_attn_in['lk1'], 'L2_attn_lq2': _L2_attn_in['lq2'], 'L2_attn_lk2': _L2_attn_in['lk2'], 'L2_attn_gn_w': _L2_attn_in['gn_w'], 'L2_attn_gn_b': _L2_attn_in['gn_b'], 'L2_xattn_Wq': _L2_xattn_in['Wq'], 'L2_xattn_Wk': _L2_xattn_in['Wk'], 'L2_xattn_Wv': _L2_xattn_in['Wv'], 'L2_xattn_W_film_in': _L2_xattn_in['W_film_in'], 'L2_xattn_b_film_in': _L2_xattn_in['b_film_in'], 'L2_xattn_W_film_out': _L2_xattn_in['W_film_out'], 'L2_xattn_b_film_out': _L2_xattn_in['b_film_out'], 'L2_xattn_g_norm_in': _L2_xattn_in['g_norm_in'], 'L2_xattn_b_norm_in': _L2_xattn_in['b_norm_in'], 'L2_xattn_g_norm_out': _L2_xattn_in['g_norm_out'], 'L2_xattn_b_norm_out': _L2_xattn_in['b_norm_out'], 'L2_xattn_g_ffn': _L2_xattn_in['g_ffn'], 'L2_xattn_b_ffn': _L2_xattn_in['b_ffn'], 'L2_xattn_W1': _L2_xattn_in['W1'], 'L2_xattn_b1': _L2_xattn_in['b1'], 'L2_xattn_W2': _L2_xattn_in['W2'], 'L2_xattn_b2': _L2_xattn_in['b2'], 'L2_xattn_log_dt': _L2_xattn_in['log_dt'], 'L2_xattn_A_re': _L2_xattn_in['A_re'], 'L2_xattn_A_im': _L2_xattn_in['A_im'], 'L2_xattn_C_re': _L2_xattn_in['C_re'], 'L2_xattn_C_im': _L2_xattn_in['C_im'], 'L2_xattn_D_skip': _L2_xattn_in['D_skip'], 'L2_xattn_mod_gate': _L2_xattn_in['mod_gate'], 'L2_ffn_gate_w': _L2_ffn_in['gate_w'], 'L2_ffn_gate_b': _L2_ffn_in['gate_b'], 'L2_ffn_w1': _L2_ffn_in['w1'], 'L2_ffn_b1': _L2_ffn_in['b1'], 'L2_ffn_w2': _L2_ffn_in['w2'], 'L2_ffn_b2': _L2_ffn_in['b2'], 'L3_attn_wq': _L3_attn_in['wq'], 'L3_attn_bq': _L3_attn_in['bq'], 'L3_attn_wqc': _L3_attn_in['wqc'], 'L3_attn_bqc': _L3_attn_in['bqc'], 'L3_attn_wqr': _L3_attn_in['wqr'], 'L3_attn_bqr': _L3_attn_in['bqr'], 'L3_attn_wkv': _L3_attn_in['wkv'], 'L3_attn_bkv': _L3_attn_in['bkv'], 'L3_attn_wkr': _L3_attn_in['wkr'], 'L3_attn_bkr': _L3_attn_in['bkr'], 'L3_attn_wkc': _L3_attn_in['wkc'], 'L3_attn_bkc': _L3_attn_in['bkc'], 'L3_attn_wv': _L3_attn_in['wv'], 'L3_attn_bv': _L3_attn_in['bv'], 'L3_attn_wo': _L3_attn_in['wo'], 'L3_attn_bo': _L3_attn_in['bo'], 'L3_xattn_Wq': _L3_xattn_in['Wq'], 'L3_xattn_Wk': _L3_xattn_in['Wk'], 'L3_xattn_Wv': _L3_xattn_in['Wv'], 'L3_xattn_Wo': _L3_xattn_in['Wo'], 'L3_xattn_bo': _L3_xattn_in['bo'], 'L3_ffn_Wg': _L3_ffn_in['Wg'], 'L3_ffn_bg': _L3_ffn_in['bg'], 'L3_ffn_Wi': _L3_ffn_in['Wi'], 'L3_ffn_Wo': _L3_ffn_in['Wo'], 'L3_ffn_A': _L3_ffn_in['A'], 'L3_ffn_B': _L3_ffn_in['B']}

def reference(x, ctx_768, mask_BxS_bf1, mask_BxS2_bf1, L0_attn_Wq, L0_attn_Wk, L0_attn_Wv, L0_attn_Wo, L0_attn_bo, L0_xattn_ln1_g, L0_xattn_ln1_b, L0_xattn_ln2_g, L0_xattn_ln2_b, L0_xattn_Wq, L0_xattn_bq, L0_xattn_Wk, L0_xattn_bk, L0_xattn_Wv, L0_xattn_bv, L0_xattn_Wo, L0_xattn_bo, L0_ffn_centroids, L0_ffn_routing_bias, L0_ffn_Wfc_r, L0_ffn_Wproj_r, L0_ffn_Wfc_sh, L0_ffn_Wproj_sh, L1_attn_Wqkv, L1_attn_Wout, L1_attn_head_scales, L1_attn_head_dirs, L1_xattn_Wq, L1_xattn_Wk, L1_xattn_Wv, L1_xattn_Wo, L1_xattn_bo, L1_ffn_rw1, L1_ffn_rb1, L1_ffn_rw2, L1_ffn_rb2, L1_ffn_ew1, L1_ffn_eb1, L1_ffn_ew2, L1_ffn_eb2, L2_attn_Wq, L2_attn_bq, L2_attn_Wk, L2_attn_bk, L2_attn_Wv, L2_attn_bv, L2_attn_Wo, L2_attn_bo, L2_attn_lq1, L2_attn_lk1, L2_attn_lq2, L2_attn_lk2, L2_attn_gn_w, L2_attn_gn_b, L2_xattn_Wq, L2_xattn_Wk, L2_xattn_Wv, L2_xattn_W_film_in, L2_xattn_b_film_in, L2_xattn_W_film_out, L2_xattn_b_film_out, L2_xattn_g_norm_in, L2_xattn_b_norm_in, L2_xattn_g_norm_out, L2_xattn_b_norm_out, L2_xattn_g_ffn, L2_xattn_b_ffn, L2_xattn_W1, L2_xattn_b1, L2_xattn_W2, L2_xattn_b2, L2_xattn_log_dt, L2_xattn_A_re, L2_xattn_A_im, L2_xattn_C_re, L2_xattn_C_im, L2_xattn_D_skip, L2_xattn_mod_gate, L2_ffn_gate_w, L2_ffn_gate_b, L2_ffn_w1, L2_ffn_b1, L2_ffn_w2, L2_ffn_b2, L3_attn_wq, L3_attn_bq, L3_attn_wqc, L3_attn_bqc, L3_attn_wqr, L3_attn_bqr, L3_attn_wkv, L3_attn_bkv, L3_attn_wkr, L3_attn_bkr, L3_attn_wkc, L3_attn_bkc, L3_attn_wv, L3_attn_bv, L3_attn_wo, L3_attn_bo, L3_xattn_Wq, L3_xattn_Wk, L3_xattn_Wv, L3_xattn_Wo, L3_xattn_bo, L3_ffn_Wg, L3_ffn_bg, L3_ffn_Wi, L3_ffn_Wo, L3_ffn_A, L3_ffn_B):
    import jax
    import jax.numpy as jnp

    def _L0_attn_ref(x, Wq, Wk, Wv, Wo, bo):
        import jax, jax.numpy as jnp
        import numpy as np
        DIM = 128
        HEADS = 16
        DIM_HEAD = 64
        INNER = HEADS * DIM_HEAD
        SEQ = 512
        BATCH = 1
        b, n, _ = x.shape
        beta = 1.0 / jnp.sqrt(jnp.float32(DIM_HEAD))

        def split_heads(t):
            return t.reshape(b, n, HEADS, DIM_HEAD).transpose(0, 2, 1, 3)
        q = split_heads(x @ Wq)
        k = split_heads(x @ Wk)
        v = split_heads(x @ Wv)
        scores = jnp.einsum('bhid,bhjd->bhij', q * beta, k)
        mask_value = -jnp.finfo(scores.dtype).max
        causal = jnp.triu(jnp.ones((n, n), dtype=bool), k=1)
        scores = jnp.where(causal, mask_value, scores)
        attn = jax.nn.softmax(scores, axis=-1)
        out = jnp.einsum('bhij,bhjd->bhid', attn, v)
        out = out.transpose(0, 2, 1, 3).reshape(b, n, INNER)
        return out @ Wo + bo

    def _L0_xattn_ref(modality1, modality2, ln1_g, ln1_b, ln2_g, ln2_b, Wq, bq, Wk, bk, Wv, bv, Wo, bo):
        import jax, jax.numpy as jnp
        import numpy as np
        EPS = 1e-05

        def layernorm(x, g, b):
            mu = jnp.mean(x, axis=-1, keepdims=True)
            var = jnp.mean(jnp.square(x - mu), axis=-1, keepdims=True)
            return (x - mu) * jax.lax.rsqrt(var + EPS) * g + b
        E = Wq.shape[1]
        scaling = E ** (-0.5)
        x1 = layernorm(modality1, ln1_g, ln1_b)
        x2 = layernorm(modality2, ln2_g, ln2_b)
        q = x1 @ Wq + bq
        k = x2 @ Wk + bk
        v = x2 @ Wv + bv
        scores = jnp.einsum('bqe,bke->bqk', q, k) * scaling
        attn = jax.nn.softmax(scores, axis=-1)
        ctx = jnp.einsum('bqk,bke->bqe', attn, v)
        return ctx @ Wo + bo

    def _L0_ffn_ref(x, centroids, routing_bias, Wfc_r, Wproj_r, Wfc_sh, Wproj_sh):
        import jax, jax.numpy as jnp
        import numpy as np
        D = 128
        F = 4 * D
        E = 8
        NS = 2
        TOP_K = 2
        B, S = (2, 128)
        raw = jnp.einsum('bsd,ed->bse', x, centroids)
        routing_scores = jax.nn.sigmoid(raw)
        balanced = jax.nn.sigmoid(raw + routing_bias)
        _, top_idx = jax.lax.top_k(balanced, TOP_K)
        gathered = jnp.take_along_axis(routing_scores, top_idx, axis=-1)
        top_w = jax.nn.softmax(gathered, axis=-1)
        combine = jnp.sum(jax.nn.one_hot(top_idx, E, dtype=x.dtype) * top_w[..., None], axis=-2)
        h_sh = jax.nn.gelu(jnp.einsum('bsd,nfd->bsnf', x, Wfc_sh), approximate=False)
        shared_out = jnp.einsum('bsnf,ndf->bsd', h_sh, Wproj_sh)
        h_r = jax.nn.gelu(jnp.einsum('bsd,efd->bsef', x, Wfc_r), approximate=False)
        expert_out = jnp.einsum('bsef,edf->bsed', h_r, Wproj_r)
        routed_out = jnp.einsum('bsed,bse->bsd', expert_out, combine)
        return x + shared_out + routed_out

    def _L1_attn_ref(x, Wqkv, Wout, head_scales, head_dirs):
        import math
        import jax, jax.numpy as jnp
        import numpy as np
        B, T, D, H = (4, 128, 128, 8)
        HD = D // H

        def _trigram_dirs():
            t = np.array([[(i >> b & 1) * 2 - 1 for b in (2, 1, 0)] for i in range(8)], dtype=np.float32)
            return jnp.asarray(t / np.linalg.norm(t, axis=1, keepdims=True))
        b, t, d = x.shape
        scale = 1.0 / math.sqrt(HD)
        qkv = (x @ Wqkv).reshape(b, t, 3, H, HD)
        qkv = jnp.transpose(qkv, (2, 0, 3, 1, 4))
        q, k, v = (qkv[0], qkv[1], qkv[2])
        scores = jnp.einsum('bhqd,bhkd->bhqk', q, k) * scale
        q_proj = jnp.einsum('bhtd,hd->bht', q[..., :3], head_dirs)
        k_proj = jnp.einsum('bhtd,hd->bht', k[..., :3], head_dirs)
        geo_bias = q_proj[..., :, None] * k_proj[..., None, :]
        scores = scores + head_scales[None, :, None, None] * geo_bias
        causal = jnp.tril(jnp.ones((t, t), dtype=bool))
        scores = jnp.where(causal, scores, -jnp.inf)
        attn = jax.nn.softmax(scores, axis=-1)
        out = jnp.einsum('bhqk,bhkd->bhqd', attn, v)
        out = jnp.transpose(out, (0, 2, 1, 3)).reshape(b, t, d)
        return out @ Wout

    def _L1_xattn_ref(x, context, Wq, Wk, Wv, Wo, bo):
        import jax, jax.numpy as jnp
        import numpy as np
        HEADS = 8
        DIM_HEAD = 64
        SCALE = DIM_HEAD ** (-0.5)
        B, Nq, _ = x.shape
        q = (x @ Wq).reshape(B, Nq, HEADS, DIM_HEAD)
        k = (context @ Wk).reshape(B, context.shape[1], HEADS, DIM_HEAD)
        v = (context @ Wv).reshape(B, context.shape[1], HEADS, DIM_HEAD)
        sim = jnp.einsum('bihd,bjhd->bhij', q, k) * SCALE
        attn = jax.nn.softmax(sim, axis=-1)
        out = jnp.einsum('bhij,bjhd->bihd', attn, v)
        out = out.reshape(B, Nq, HEADS * DIM_HEAD)
        return out @ Wo + bo

    def _L1_ffn_ref(x, rw1, rb1, rw2, rb2, ew1, eb1, ew2, eb2):
        import jax, jax.numpy as jnp
        import numpy as np
        B, T, C, E, K, CAP, H = (8, 256, 128, 8, 2, 512, 512)
        Bx, Tx, Cx = x.shape
        N = Bx * Tx
        logits = jax.nn.relu(x @ rw1 + rb1) @ rw2 + rb2
        vals, ids = jax.lax.top_k(logits, K)
        probs = jax.nn.softmax(vals, axis=-1)
        ids_f = ids.reshape(N * K)
        probs_f = probs.reshape(N * K)
        xr = jnp.repeat(x.reshape(N, Cx), K, axis=0)
        m = jax.nn.one_hot(ids_f, E, dtype=jnp.int32)
        pos = jnp.cumsum(m, axis=0) - 1
        pos_tok = jnp.take_along_axis(pos, ids_f[:, None], axis=1)[:, 0]
        keep = (pos_tok < CAP).astype(x.dtype)
        pos_c = jnp.clip(pos_tok, 0, CAP - 1)
        disp = jnp.zeros((E, CAP, Cx), x.dtype).at[ids_f, pos_c].add(xr * keep[:, None])
        h = jax.nn.relu(jnp.einsum('enc,ech->enh', disp, ew1) + eb1[:, None, :])
        eo = jnp.einsum('enh,ehc->enc', h, ew2) + eb2[:, None, :]
        y = eo[ids_f, pos_c] * (probs_f * keep)[:, None]
        return y.reshape(Bx, Tx, K, Cx).sum(axis=2)

    def _L2_attn_ref(x, Wq, bq, Wk, bk, Wv, bv, Wo, bo, lq1, lk1, lq2, lk2, gn_w, gn_b):
        import jax, jax.numpy as jnp
        import numpy as np
        B, S, D, H = (2, 256, 128, 16)
        DH = D // H
        EPS = 1e-05
        LAMBDA_INIT = 0.8
        b, s, d = x.shape
        h, dh = lq1.shape
        scale = dh ** (-0.5)
        q = (x @ Wq + bq).reshape(b, s, h, dh)
        k = (x @ Wk + bk).reshape(b, s, h, dh)
        v = (x @ Wv + bv).reshape(b, s, h, dh)
        lam = jnp.exp((lq1 * lk1).sum(-1)) - jnp.exp((lq2 * lk2).sum(-1)) + LAMBDA_INIT
        scores = jnp.einsum('bihd,bjhd->bhij', q, k) * scale * lam[None, :, None, None]
        attn = jax.nn.softmax(scores, axis=-1)
        out = jnp.einsum('bhij,bjhd->bihd', attn, v)
        mean = out.mean(axis=(1, 3), keepdims=True)
        var = out.var(axis=(1, 3), keepdims=True)
        normed = (out - mean) * jax.lax.rsqrt(var + EPS)
        normed = normed * gn_w[None, None, :, :] + gn_b[None, None, :, :]
        y = normed.reshape(b, s, d) @ Wo + bo
        return y

    def _L2_xattn_ref(x_text, x_vision, text_mask, vision_mask, Wq, Wk, Wv, W_film_in, b_film_in, W_film_out, b_film_out, g_norm_in, b_norm_in, g_norm_out, b_norm_out, g_ffn, b_ffn, W1, b1, W2, b2, log_dt, A_re, A_im, C_re, C_im, D_skip, mod_gate):
        import jax, jax.numpy as jnp
        import numpy as np
        B, T, DT, G, DV = (16, 64, 128, 72, 96)
        H, DH = (4, 32)
        INNER = H * DH
        HID = 4 * DT
        N_STATE = 64
        K_TOP = 32

        def layernorm(x, g, b, eps=1e-05):
            m = x.mean(-1, keepdims=True)
            v = x.var(-1, keepdims=True)
            return (x - m) * jax.lax.rsqrt(v + eps) * g + b

        def s4d(x, log_dt, A_re, A_im, C_re, C_im, D_skip):
            Bb, L, D = x.shape
            dt = jnp.exp(log_dt)
            A = A_re + 1j * A_im
            C = C_re + 1j * C_im
            dtA = dt[:, None] * A
            dC = C * (jnp.exp(dtA) - 1.0) / A
            powers = jnp.exp(dtA[:, :, None] * jnp.arange(L))
            K = 2.0 * jnp.einsum('dn,dnl->dl', dC, powers).real
            n = 2 * L
            Kf = jnp.fft.rfft(K, n=n, axis=-1)
            xf = jnp.fft.rfft(x, n=n, axis=1)
            y = jnp.fft.irfft(xf * Kf.T[None], n=n, axis=1)[:, :L]
            return y + x * D_skip
        Bb, Tt, D = x_text.shape
        Gg = x_vision.shape[1]
        Q = (x_text @ Wq).reshape(Bb, Tt, H, DH)
        K = (x_vision @ Wk).reshape(Bb, Gg, H, DH)
        scores = jnp.einsum('bthd,bghd->bhtg', Q, K) / np.sqrt(DH).astype(np.float32)
        scores = jnp.where(vision_mask[:, None, None, :], scores, -jnp.inf)
        topv, topi = jax.lax.top_k(scores, K_TOP)
        probs = jax.nn.softmax(topv, axis=-1)
        bi = jnp.arange(Bb)[:, None, None, None]
        hi = jnp.arange(H)[None, :, None, None]
        ti = jnp.arange(Tt)[None, None, :, None]
        attn = jnp.zeros_like(scores).at[bi, hi, ti, topi].set(probs)
        attn_mean = attn.mean(axis=1)
        V = x_vision @ Wv
        c_t = jnp.einsum('btg,bgd->btd', attn_mean, V)
        c_t = c_t * text_mask[..., None]
        x = layernorm(x_text, g_norm_in, b_norm_in)
        scale_in, shift_in = jnp.split(c_t @ W_film_in + b_film_in, 2, axis=-1)
        x = x * (1.0 + mod_gate * scale_in) + mod_gate * shift_in
        y = s4d(x, log_dt, A_re, A_im, C_re, C_im, D_skip)
        scale_out, shift_out = jnp.split(c_t @ W_film_out + b_film_out, 2, axis=-1)
        y = y * (1.0 + mod_gate * scale_out) + mod_gate * shift_out
        xt = x_text + y
        h = layernorm(xt, g_ffn, b_ffn)
        h = jax.nn.gelu(h @ W1 + b1, approximate=False) @ W2 + b2
        xt = xt + h
        return layernorm(xt, g_norm_out, b_norm_out)

    def _L2_ffn_ref(x, gate_w, gate_b, w1, b1, w2, b2):
        import jax, jax.numpy as jnp
        import numpy as np
        B, L, D, E, H, TOP_K = (4, 256, 128, 8, 64, 2)
        b, l, d = x.shape
        e = gate_w.shape[1]
        xf = x.reshape(-1, d)
        t = xf.shape[0]
        logits = xf @ gate_w + gate_b
        top_vals, top_idx = jax.lax.top_k(logits, TOP_K)
        top_gates = jax.nn.softmax(top_vals, axis=-1)
        gates = jnp.zeros((t, e), x.dtype).at[jnp.arange(t)[:, None], top_idx].set(top_gates)
        h = jax.nn.gelu(jnp.einsum('td,edh->eth', xf, w1) + b1[:, None, :], approximate=False)
        eo = jnp.einsum('eth,ehd->etd', h, w2) + b2[:, None, :]
        out = jnp.einsum('te,etd->td', gates, eo)
        return out.reshape(b, l, d)

    def _L3_attn_ref(x, wq, bq, wqc, bqc, wqr, bqr, wkv, bkv, wkr, bkr, wkc, bkc, wv, bv, wo, bo):
        import jax, jax.numpy as jnp
        import numpy as np
        import math
        B, S, E = (2, 256, 128)
        H, DC, DR = (16, 32, 128)
        HD = E // H

        def _linear_params(key, din, dout):
            k1, k2 = jax.random.split(key)
            bound = 1.0 / math.sqrt(din)
            w = jax.random.uniform(k1, (din, dout), minval=-bound, maxval=bound, dtype=jnp.float32)
            b = jax.random.uniform(k2, (dout,), minval=-bound, maxval=bound, dtype=jnp.float32)
            return (w, b)

        def _gelu(x):
            return jax.nn.gelu(x, approximate=False)

        def _rope_cos_sin(seq_len, d_rope):
            inv_freq = 1.0 / 10000.0 ** (jnp.arange(0, d_rope, 2, dtype=jnp.float32) / d_rope)
            t = jnp.arange(seq_len, dtype=jnp.float32)
            freqs = t[:, None] * inv_freq[None, :]
            emb = jnp.concatenate([freqs, freqs], axis=-1)
            return (jnp.cos(emb), jnp.sin(emb))

        def _apply_rope(x, cos, sin):
            d = x.shape[-1]
            x1, x2 = (x[..., :d // 2], x[..., d // 2:])
            rot = jnp.concatenate([-x2, x1], axis=-1)
            return x * cos + rot * sin
        b, s, _ = x.shape
        cq = _gelu(x @ wq + bq)
        q_c = cq @ wqc + bqc
        q_r = x @ wqr + bqr
        ckv = _gelu(x @ wkv + bkv)
        k_r = x @ wkr + bkr
        k_c = ckv @ wkc + bkc
        v = (ckv @ wv + bv).reshape(b, s, H, HD).transpose(0, 2, 1, 3)
        cos, sin = _rope_cos_sin(s, DR)
        q_r = _apply_rope(q_r, cos, sin)
        k_r = _apply_rope(k_r, cos, sin)
        q = _gelu(jnp.concatenate([q_c, q_r], axis=-1)).reshape(b, s, H, HD).transpose(0, 2, 1, 3)
        k = _gelu(jnp.concatenate([k_c, k_r], axis=-1)).reshape(b, s, H, HD).transpose(0, 2, 1, 3)
        scale = 1.0 / math.sqrt(HD)
        scores = jnp.einsum('bhqd,bhkd->bhqk', q, k) * scale
        causal = jnp.triu(jnp.ones((s, s), dtype=bool), k=1)
        scores = jnp.where(causal[None, None], -jnp.inf, scores)
        attn = jax.nn.softmax(scores, axis=-1)
        out = jnp.einsum('bhqk,bhkd->bhqd', attn, v)
        out = out.transpose(0, 2, 1, 3).reshape(b, s, E)
        return out @ wo + bo

    def _L3_xattn_ref(x, context, Wq, Wk, Wv, Wo, bo):
        import jax, jax.numpy as jnp
        import numpy as np
        QUERY_DIM = 128
        CONTEXT_DIM = 96
        HEADS = 8
        DIM_HEAD = 64
        INNER = HEADS * DIM_HEAD
        B, S, _ = x.shape
        L = context.shape[1]
        scale = DIM_HEAD ** (-0.5)
        q = (x @ Wq).reshape(B, S, HEADS, DIM_HEAD).transpose(0, 2, 1, 3)
        k = (context @ Wk).reshape(B, L, HEADS, DIM_HEAD).transpose(0, 2, 1, 3)
        v = (context @ Wv).reshape(B, L, HEADS, DIM_HEAD).transpose(0, 2, 1, 3)
        attn = jnp.einsum('bhsd,bhld->bhsl', q, k) * scale
        attn = jax.nn.softmax(attn, axis=-1)
        out = jnp.einsum('bhsl,bhld->bhsd', attn, v)
        out = out.transpose(0, 2, 1, 3).reshape(B, S, INNER)
        return out @ Wo + bo

    def _L3_ffn_ref(x, Wg, bg, Wi, Wo, A, B):
        import jax, jax.numpy as jnp
        import numpy as np
        TOP_K = 2
        E = Wg.shape[0]
        logits = jnp.einsum('bsd,ed->bse', x, Wg) + bg
        scores = jax.nn.softmax(logits, axis=-1)
        topv, topi = jax.lax.top_k(scores, TOP_K)
        w = jnp.sum(jax.nn.one_hot(topi, E, dtype=x.dtype) * topv[..., None], axis=-2)
        base = jnp.einsum('bsd,fd->bsf', x, Wi)
        lora_low = jnp.einsum('bsd,erd->bser', x, A)
        lora = jnp.einsum('bser,efr->bsef', lora_low, B)
        h = jax.nn.relu(base[:, :, None, :] + lora)
        expert_out = jnp.einsum('bsef,df->bsed', h, Wo)
        out = jnp.einsum('bse,bsed->bsd', w, expert_out)
        return out
    x = x + _L0_attn_ref(_layernorm(x, axis=-1), L0_attn_Wq, L0_attn_Wk, L0_attn_Wv, L0_attn_Wo, L0_attn_bo)
    x = x + _L0_xattn_ref(_layernorm(x, axis=-1), ctx_768, L0_xattn_ln1_g, L0_xattn_ln1_b, L0_xattn_ln2_g, L0_xattn_ln2_b, L0_xattn_Wq, L0_xattn_bq, L0_xattn_Wk, L0_xattn_bk, L0_xattn_Wv, L0_xattn_bv, L0_xattn_Wo, L0_xattn_bo)
    x = x + _L0_ffn_ref(_layernorm(x, axis=-1), L0_ffn_centroids, L0_ffn_routing_bias, L0_ffn_Wfc_r, L0_ffn_Wproj_r, L0_ffn_Wfc_sh, L0_ffn_Wproj_sh)
    x = x + _L1_attn_ref(_layernorm(x, axis=-1), L1_attn_Wqkv, L1_attn_Wout, L1_attn_head_scales, L1_attn_head_dirs)
    x = x + _L1_xattn_ref(_layernorm(x, axis=-1), ctx_768, L1_xattn_Wq, L1_xattn_Wk, L1_xattn_Wv, L1_xattn_Wo, L1_xattn_bo)
    x = x + _L1_ffn_ref(_layernorm(x, axis=-1), L1_ffn_rw1, L1_ffn_rb1, L1_ffn_rw2, L1_ffn_rb2, L1_ffn_ew1, L1_ffn_eb1, L1_ffn_ew2, L1_ffn_eb2)
    x = x + _L2_attn_ref(_layernorm(x, axis=-1), L2_attn_Wq, L2_attn_bq, L2_attn_Wk, L2_attn_bk, L2_attn_Wv, L2_attn_bv, L2_attn_Wo, L2_attn_bo, L2_attn_lq1, L2_attn_lk1, L2_attn_lq2, L2_attn_lk2, L2_attn_gn_w, L2_attn_gn_b)
    x = x + _L2_xattn_ref(_layernorm(x, axis=-1), ctx_768, mask_BxS_bf1, mask_BxS2_bf1, L2_xattn_Wq, L2_xattn_Wk, L2_xattn_Wv, L2_xattn_W_film_in, L2_xattn_b_film_in, L2_xattn_W_film_out, L2_xattn_b_film_out, L2_xattn_g_norm_in, L2_xattn_b_norm_in, L2_xattn_g_norm_out, L2_xattn_b_norm_out, L2_xattn_g_ffn, L2_xattn_b_ffn, L2_xattn_W1, L2_xattn_b1, L2_xattn_W2, L2_xattn_b2, L2_xattn_log_dt, L2_xattn_A_re, L2_xattn_A_im, L2_xattn_C_re, L2_xattn_C_im, L2_xattn_D_skip, L2_xattn_mod_gate)
    x = x + _L2_ffn_ref(_layernorm(x, axis=-1), L2_ffn_gate_w, L2_ffn_gate_b, L2_ffn_w1, L2_ffn_b1, L2_ffn_w2, L2_ffn_b2)
    x = x + _L3_attn_ref(_layernorm(x, axis=-1), L3_attn_wq, L3_attn_bq, L3_attn_wqc, L3_attn_bqc, L3_attn_wqr, L3_attn_bqr, L3_attn_wkv, L3_attn_bkv, L3_attn_wkr, L3_attn_bkr, L3_attn_wkc, L3_attn_bkc, L3_attn_wv, L3_attn_bv, L3_attn_wo, L3_attn_bo)
    x = x + _L3_xattn_ref(_layernorm(x, axis=-1), ctx_768, L3_xattn_Wq, L3_xattn_Wk, L3_xattn_Wv, L3_xattn_Wo, L3_xattn_bo)
    x = x + _L3_ffn_ref(_layernorm(x, axis=-1), L3_ffn_Wg, L3_ffn_bg, L3_ffn_Wi, L3_ffn_Wo, L3_ffn_A, L3_ffn_B)
    return x

_drawn_inputs = setup_inputs


def setup_inputs(seed=0):
    import zlib

    import numpy as np

    out = dict(_drawn_inputs(seed))
    spreads = {'L0_xattn_ln1_g': (1.0, 0.2),
     'L0_xattn_ln1_b': (0.0, 0.1),
     'L0_xattn_ln2_g': (1.0, 0.2),
     'L0_xattn_ln2_b': (0.0, 0.1),
     'L0_ffn_routing_bias': (0.0, 0.1),
     'L1_ffn_rb1': (0.0, 0.8),
     'L1_ffn_rb2': (0.0, 0.1),
     'L1_ffn_eb1': (0.0, 0.8),
     'L1_ffn_eb2': (0.0, 0.498),
     'L2_attn_gn_w': (1.0, 0.2),
     'L2_attn_gn_b': (0.0, 0.1),
     'L2_xattn_b_film_in': (0.0, 0.535),
     'L2_xattn_b_film_out': (0.0, 0.563),
     'L2_xattn_g_norm_in': (1.0, 0.2),
     'L2_xattn_b_norm_in': (0.0, 0.298),
     'L2_xattn_g_norm_out': (1.0, 0.2),
     'L2_xattn_b_norm_out': (0.0, 0.295),
     'L2_xattn_g_ffn': (1.0, 0.6),
     'L2_xattn_b_ffn': (0.0, 0.8),
     'L2_xattn_b1': (0.0, 0.8),
     'L2_xattn_b2': (0.0, 0.456),
     'L2_xattn_A_re': (-0.5, 0.6),
     'L2_ffn_gate_b': (0.0, 0.544),
     'L2_ffn_b1': (0.0, 0.8),
     'L2_ffn_b2': (0.0, 0.393),
     'L3_ffn_bg': (0.0, 0.8)}
    factors = {'L0_attn_Wq': 8.0,
     'L0_attn_Wk': 8.0,
     'L0_xattn_bq': 6.771,
     'L0_xattn_bk': 64.0,
     'L0_xattn_bo': 3.162,
     'L1_attn_Wqkv': 4.208,
     'L1_attn_Wout': 4.118,
     'L1_attn_head_scales': 8.0,
     'L1_attn_head_dirs': 8.0,
     'L1_xattn_bo': 8.0,
     'L1_ffn_rw1': 8.0,
     'L1_ffn_rw2': 4.344,
     'L1_ffn_ew1': 5.977,
     'L1_ffn_ew2': 4.459,
     'L2_attn_bq': 8.0,
     'L2_attn_bk': 64.0,
     'L2_attn_bv': 2.967,
     'L2_attn_bo': 7.16,
     'L2_xattn_Wq': 8.0,
     'L2_xattn_Wk': 8.0,
     'L2_xattn_Wv': 8.0,
     'L2_xattn_W_film_in': 8.0,
     'L2_xattn_W_film_out': 8.0,
     'L2_xattn_W1': 5.955,
     'L2_xattn_W2': 5.532,
     'L2_ffn_gate_w': 3.372,
     'L2_ffn_w1': 8.0,
     'L2_ffn_w2': 8.0,
     'L3_attn_wqr': 8.0,
     'L3_attn_bqr': 36.506,
     'L3_attn_wkv': 2.869,
     'L3_attn_bkv': 8.0,
     'L3_attn_wkr': 8.0,
     'L3_attn_bkr': 45.083,
     'L3_attn_bv': 2.978,
     'L3_attn_bo': 4.16,
     'L3_xattn_bo': 8.0,
     'L3_ffn_Wg': 3.115,
     'L3_ffn_A': 8.0,
     'L3_ffn_B': 8.0}
    for name, (base, spread) in spreads.items():
        noise = np.random.default_rng([zlib.crc32(name.encode()), seed]).standard_normal(out[name].shape)
        drawn = base * np.exp(spread * noise) if base else spread * noise
        out[name] = jnp.asarray(drawn.astype(out[name].dtype))
    for name, factor in factors.items():
        out[name] = (out[name] * factor).astype(out[name].dtype)
    return out
```

```python
from contextlib import ExitStack, contextmanager

import concourse.bass as bass
from concourse import mybir

FIRST_SUBLAYER, LAST_SUBLAYER = 0, 12

F32 = mybir.dt.float32
U8 = mybir.dt.uint8
ALU = mybir.AluOpType
ACT = mybir.ActivationFunctionType
AX_X = mybir.AxisListType.X

B, S, D = 32, 56, 128
TB = 2
P = TB * S
T = B // TB
N = T * P
BT = 4
NB = T // BT
W = BT * P
L, DC = 1500, 96
LC, LP = 12, 125
EPS = 1e-5
NEG = -1e30


class Chip:
    pass


class Heads:

    def __init__(self, sb, name, dv, mask_q, mask_k, head, value, query=None, key=None):
        self.diag = sb(f"{name}_diag", [P, 2, GH, P])
        self.probs = sb(f"{name}_probs", [P, 2, GH, P])
        self.negmax = sb(f"{name}_negmax", [P, 2, GH])
        self.over_sum = sb(f"{name}_over_sum", [P, 4, GH])
        self.dv, self.mask_q, self.mask_k = dv, mask_q, mask_k
        self.head, self.value, self.query, self.key, self.query_group = head, value, query, key, None


class Routing:

    def __init__(self, sb, name, E):
        self.logits, self.kept_logits = sb(f"{name}_logits", [P, T, E]), sb(f"{name}_kept_logits", [P, T, E])
        self.first, self.second = sb(f"{name}_first", [P, T, E]), sb(f"{name}_second", [P, T, E])
        self.rank, self.combine = sb(f"{name}_rank", [P, T, E]), sb(f"{name}_combine", [P, T, E])
        self.score, self.bias = sb(f"{name}_score", [P, T, E]), sb(f"{name}_bias", [P, E])
        self.top, self.lead = sb(f"{name}_top", [P, 2, T]), sb(f"{name}_lead", [P, T])
        self.a, self.b = sb(f"{name}_a", [P, T]), sb(f"{name}_b", [P, T])


class Expert:

    def __init__(self, up, down, out_bias=None, gate=None):
        self.up, self.down, self.out_bias, self.gate = up, down, out_bias, gate


@contextmanager
def stage(nc, name, *signals):
    sems = {s: nc.alloc_semaphore(f"{name}_{s}") for s in signals}
    with nc.Block() as block:
        yield block, sems
    nc.clear_and_free_semaphores(list(sems.values()))
    nc.all_engine_barrier()


def in_order(eng, sem):
    count = [0]

    def link(ins):
        count[0] += 1
        ins.then_inc(sem, 1)
        eng.wait_ge(sem, count[0])

    return link


def over(ap, n):
    return ap.unsqueeze(2).to_broadcast([ap.shape[0], ap.shape[1], n])


def under(ap, n):
    return ap.unsqueeze(1).to_broadcast([ap.shape[0], n, ap.shape[1]])


def column(ap):
    return ap.rearrange("(p a) -> p a", a=1)


def row(ap):
    return ap.rearrange("(a n) -> a n", a=1)


def rows(ap, p):
    return row(ap).to_broadcast([p, ap.shape[0]])


def build_constants(nc, g):
    with stage(nc, "const", "filled", "cut", "kept") as (block, s):
        @block.gpsimd
        def _(pool):
            link = in_order(pool, s["cut"])
            nc.gpsimd.memset(g.ones[:], 1.0).then_inc(s["filled"], 1)
            link(nc.gpsimd.memset(g.ident[:], 0.0))
            link(nc.gpsimd.affine_select(out=g.ident[:], in_=g.ident[:], compare_op=ALU.not_equal, fill=1.0,
                                         base=0, pattern=[[-1, 128]], channel_multiplier=1))
            link(nc.gpsimd.memset(g.last_row[:], 0.0))
            link(nc.gpsimd.memset(g.last_row[:, DC:DC + 1], 1.0))
            for mask in (g.mask_any, g.mask_q, g.mask_k):
                link(nc.gpsimd.memset(mask[:], 0.0))
                link(nc.gpsimd.affine_select(out=mask[:, :, 0:S], in_=mask[:, :, 0:S], compare_op=ALU.is_ge,
                                             fill=NEG, base=S - 1, pattern=[[0, BT], [0, S]],
                                             channel_multiplier=-1))
                link(nc.gpsimd.affine_select(out=mask[:, :, S:P], in_=mask[:, :, S:P], compare_op=ALU.is_ge,
                                             fill=NEG, base=-S, pattern=[[0, BT], [0, S]],
                                             channel_multiplier=1))
            link(nc.gpsimd.affine_select(out=g.mask_q[:], in_=g.mask_q[:], compare_op=ALU.is_ge, fill=NEG,
                                         base=0, pattern=[[0, BT], [-1, P]], channel_multiplier=1))
            link(nc.gpsimd.affine_select(out=g.mask_k[:], in_=g.mask_k[:], compare_op=ALU.is_ge, fill=NEG,
                                         base=0, pattern=[[0, BT], [1, P]], channel_multiplier=-1))


def load_all(eng, arrived, loads):
    for dst, src in loads:
        eng.dma_start(dst, src).then_inc(arrived, 16)
    if loads:
        eng.wait_ge(arrived, 16 * len(loads))


def normalize(nc, g, name, src, loads=(), turn=True, dst=None):
    dst = g.xn if dst is None else dst
    half = len(loads) // 2
    with stage(nc, name, "load_a", "load_b", "steps", "centred", "squared", "spread", "pool_steps", "rstd",
               "normal", "turned", "kept") as (block, s):
        @block.sync
        def _(sp):
            load_all(sp, s["load_a"], loads[half:])

        @block.vector
        def _(dve):
            link = in_order(dve, s["steps"])
            link(nc.vector.tensor_reduce(g.stat[:, 0, :], src[:], AX_X, ALU.add))
            link(nc.vector.tensor_scalar(g.stat[:, 1, :], g.stat[:, 0, :], -1.0 / D, None, ALU.mult))
            nc.vector.tensor_tensor(dst[:], src[:], over(g.stat[:, 1, :], D), ALU.add).then_inc(s["centred"], 1)
            dve.wait_ge(s["squared"], 1)
            nc.vector.tensor_reduce(g.stat[:, 2, :], g.square[:], AX_X, ALU.add).then_inc(s["spread"], 1)
            dve.wait_ge(s["rstd"], 1)
            nc.vector.tensor_tensor(dst[:], dst[:], over(g.stat[:, 3, :], D), ALU.mult).then_inc(s["normal"], 1)
            if turn:
                for b in range(1, NB, 2):
                    dve.wait_ge(s["turned"], b + 1)
                    nc.vector.tensor_copy(g.xnT[:, b * W:(b + 1) * W], g.ps[:, b, 0:W]).then_inc(s["kept"], 1)

        @block.gpsimd
        def _(pool):
            link = in_order(pool, s["pool_steps"])
            pool.wait_ge(s["spread"], 1)
            link(nc.gpsimd.tensor_scalar(g.stat[:, 2, :], g.stat[:, 2, :], 1.0 / D, EPS, ALU.mult, ALU.add))
            nc.gpsimd.tensor_tensor(g.stat[:, 3, :], g.stat[:, 2, :], g.minus_half[:], ALU.pow).then_inc(s["rstd"], 1)

        @block.scalar
        def _(act):
            for dst_, src_ in loads[:half]:
                act.dma_start(dst_, src_).then_inc(s["load_b"], 16)
            act.wait_ge(s["centred"], 1)
            nc.scalar.activation(g.square[:], dst[:], ACT.Square).then_inc(s["squared"], 1)
            if turn:
                for b in range(0, NB, 2):
                    act.wait_ge(s["turned"], b + 1)
                    nc.scalar.copy(g.xnT[:, b * W:(b + 1) * W], g.ps[:, b, 0:W]).then_inc(s["kept"], 1)
            if half:
                act.wait_ge(s["load_b"], 16 * half)

        @block.tensor
        def _(pe):
            if turn:
                pe.wait_ge(s["normal"], 1)
                turn_tiles(nc, g, dst, s["turned"])


def turn_tiles(nc, g, src, turned):
    for b in range(NB):
        for j in range(BT):
            last = nc.tensor.transpose(g.ps[:, b, j * P:(j + 1) * P], src[:, b * BT + j, :], g.ident[0:P, 0:P])
        last.then_inc(turned, 1)


def turn_and_project(nc, g, name, src, wo, bo4, add_to):
    with stage(nc, name, "turned", "kept", "projected", "added") as (block, s):
        @block.tensor
        def _(pe):
            turn_tiles(nc, g, src, s["turned"])
            for b in range(NB):
                pe.wait_ge(s["kept"], b + 1)
                bank = g.ps[0:P, NB + b, :]
                if bo4 is not None:
                    nc.tensor.matmul(bank, g.ones[0:1, 0:P], bo4[0:1, :], start=True, stop=False,
                                     skip_group_check=True)
                for j in range(BT):
                    t = b * BT + j
                    last = nc.tensor.matmul(bank[:, j * D:(j + 1) * D], g.workT[:, t * P:(t + 1) * P], wo[:],
                                            start=bo4 is None, stop=True, skip_group_check=True)
                last.then_inc(s["projected"], 1)

        @block.scalar
        def _(act):
            for b in range(NB):
                act.wait_ge(s["turned"], b + 1)
                nc.scalar.copy(g.workT[:, b * W:(b + 1) * W], g.ps[:, b, 0:W]).then_inc(s["kept"], 1)

        @block.vector
        def _(dve):
            for b in range(NB):
                dve.wait_ge(s["projected"], b + 1)
                part = add_to[:, b * BT:(b + 1) * BT, :]
                nc.vector.tensor_tensor(part, part, g.ps[0:P, NB + b, :].rearrange("p (j d) -> p j d", j=BT),
                                        ALU.add).then_inc(s["added"], 1)


GH = 4


def attend_groups(nc, g, a, s, i, groups, pe):
    def scores(k):
        n = i * groups + k
        if k >= 2:
            pe.wait_ge(s["max_taken"], n - 1)
        bank = g.ps[0:P, k % 2, 0:W]
        nc.tensor.matmul(bank, g.ident[0:P, 0:P], a.mask_q[:].rearrange("p a b -> p (a b)"),
                         start=True, stop=False, skip_group_check=True)
        for h in range(GH):
            q, kk = a.query(a.head(k, h)), a.key(a.head(k, h))
            last = nc.tensor.matmul(bank[:, h * P:(h + 1) * P], q, kk, start=False, stop=(h == GH - 1),
                                    skip_group_check=True)
        last.then_inc(s["scores"], 1)

    def scores_turned(k):
        n = i * groups + k
        pe.wait_ge(s["diag"], n + 1)
        if k >= 2:
            pe.wait_ge(s["probs"], n - 1)
        bank = g.ps[0:P, 2 + k % 2, 0:W]
        nc.tensor.matmul(bank, g.ident[0:P, 0:P], a.mask_k[:].rearrange("p a b -> p (a b)"),
                         start=True, stop=False, skip_group_check=True)
        nc.tensor.matmul(bank, g.ones[0:P, 0:P], a.diag[:, k % 2, :, :].rearrange("p a b -> p (a b)"),
                         start=False, stop=False, skip_group_check=True)
        if a.query_group is None:
            for h in range(GH):
                q, kk = a.query(a.head(k, h)), a.key(a.head(k, h))
                last = nc.tensor.matmul(bank[:, h * P:(h + 1) * P], kk, q, start=False, stop=(h == GH - 1),
                                        skip_group_check=True)
        else:
            last = nc.tensor.matmul(bank, a.key(0), a.query_group(k), start=False, stop=True,
                                    skip_group_check=True)
        last.then_inc(s["turned_scores"], 1)

    def mix(k):
        n = i * groups + k
        pe.wait_ge(s["probs"], n + 1)
        if k >= 2:
            pe.wait_ge(s["mixed_kept"], n - 1)
        bank = g.ps[0:P, 4 + k % 2, :]
        for h in range(GH):
            last = nc.tensor.matmul(bank[:, h * a.dv:(h + 1) * a.dv], a.probs[:, k % 2, h, :],
                                    a.value(i, a.head(k, h)), start=True, stop=True, skip_group_check=True)
        last.then_inc(s["mixed"], 1)

    for k in range(groups + 3):
        if k < groups:
            scores(k)
        if 0 <= k - 1 < groups:
            scores_turned(k - 1)
        if 0 <= k - 2 < groups:
            mix(k - 2)


def attend_vector(nc, g, a, s, i, groups, dve, out):
    def maxima(k):
        n = i * groups + k
        dve.wait_ge(s["scores"], n + 1)
        if k >= 2:
            dve.wait_ge(s["diag"], n - 1)
        nc.vector.tensor_reduce(a.negmax[:, k % 2, :], g.ps[0:P, k % 2, 0:W].rearrange("p (h q) -> p h q", h=GH),
                                AX_X, ALU.max, negate=True).then_inc(s["max_taken"], 1)

    def keep(k):
        n = i * groups + k
        dve.wait_ge(s["mixed"], n + 1)
        bank = g.ps[0:P, 4 + k % 2, 0:GH * a.dv].rearrange("p (h d) -> p h d", h=GH)
        nc.vector.reciprocal(a.over_sum[:, k, :], bank[:, :, a.dv - 1]).then_inc(s["inverse"], 1)
        dve.wait_ge(s["inverse"], n + 1)
        nc.vector.tensor_tensor(out(i, k), bank[:, :, 0:a.dv - 1], over(a.over_sum[:, k, :], a.dv - 1),
                                ALU.mult).then_inc(s["mixed_kept"], 1)

    for k in range(groups + 3):
        if k < groups:
            maxima(k)
        if 0 <= k - 3 < groups:
            keep(k - 3)


def attend_diagonals(nc, g, a, s, i, groups, pool):
    for k in range(groups):
        n = i * groups + k
        pool.wait_ge(s["max_taken"], n + 1)
        if k >= 2:
            pool.wait_ge(s["turned_scores"], n - 1)
        nc.gpsimd.tensor_tensor(a.diag[:, k % 2, :, :], under(g.ident[0:P, 0:P], GH),
                                over(a.negmax[:, k % 2, :], P), ALU.mult).then_inc(s["diag"], 1)


def attend_exponentials(nc, g, a, s, i, groups, act):
    for k in range(groups):
        n = i * groups + k
        act.wait_ge(s["turned_scores"], n + 1)
        if k >= 2:
            act.wait_ge(s["mixed"], n - 1)
        nc.scalar.activation(a.probs[:, k % 2, :, :], g.ps[0:P, 2 + k % 2, 0:W].rearrange("p (h q) -> p h q", h=GH),
                             ACT.Exp).then_inc(s["probs"], 1)


ATTEND = ("scores", "max_taken", "diag", "turned_scores", "probs", "mixed", "inverse", "mixed_kept")


def wide_attention(nc, g, w, sb):
    H, DH = 16, 64
    INNER = H * DH
    C = INNER // 128
    groups = H // GH
    wq, wk, wv = (sb(f"a0_{n}", [D, INNER]) for n in ("wq", "wk", "wv"))
    wo = sb("a0_wo", [128, C, D])
    bo = sb("a0_bo", [1, D])
    normalize(nc, g, "a0_norm", g.x, [
        (wq[:], w["L0_attn_Wq"]), (wk[:], w["L0_attn_Wk"]), (wv[:], w["L0_attn_Wv"]),
        (wo[:], w["L0_attn_Wo"].rearrange("(c p) d -> p c d", p=128)), (bo[:], row(w["L0_attn_bo"]))])
    xt = sb("a0_xt", [D, P])
    qT, kT = (sb(f"a0_{n}", [128, C, P]) for n in ("qT", "kT"))
    v = sb("a0_v", [P, H, DH + 1])
    on = sb("a0_on", [P, INNER])
    onT = sb("a0_onT", [128, C, P])
    a = Heads(
        sb, "a0", DH + 1, g.mask_q, g.mask_k,
        head=lambda k, h: 8 * (k // 2) + 2 * h + k % 2,
        query=lambda h: qT[DH * (h % 2):DH * (h % 2) + DH, h // 2, :],
        key=lambda h: kT[DH * (h % 2):DH * (h % 2) + DH, h // 2, :],
        value=lambda i, h: v[:, h, :])
    with stage(nc, "a0", "ones_set", "xt", "q", "k", "v", "q_kept", "k_kept", "v_kept", "on_turned", "onT_kept",
               "projected", "added", *ATTEND) as (block, s):
        @block.tensor
        def _(pe):
            pe.wait_ge(s["ones_set"], 1)
            with pe.Fori(0, T) as i:
                pe.wait_ge(s["xt"], i + 1)
                for c in range(C):
                    last = nc.tensor.matmul(g.ps[:, c // 4, (c % 4) * P:(c % 4) * P + P],
                                            wq[:, c * 128:(c + 1) * 128], xt[:], start=True, stop=True)
                    if c % 4 == 3:
                        last.then_inc(s["q"], 1)
                for c in range(C):
                    last = nc.tensor.matmul(g.ps[:, 2 + c // 4, (c % 4) * P:(c % 4) * P + P],
                                            wk[:, c * 128:(c + 1) * 128], xt[:], start=True, stop=True)
                    if c % 4 == 3:
                        last.then_inc(s["k"], 1)
                for c in range(2):
                    nc.tensor.matmul(g.ps[0:P, 4 + c, :], xt[:], wv[:, c * 512:(c + 1) * 512],
                                     start=True, stop=True).then_inc(s["v"], 1)
                pe.wait_ge(s["q_kept"], 2 * i + 2)
                pe.wait_ge(s["k_kept"], 2 * i + 2)
                pe.wait_ge(s["v_kept"], 2 * i + 2)
                attend_groups(nc, g, a, s, i, groups, pe)
                pe.wait_ge(s["mixed_kept"], groups * i + groups)
                for c in range(C):
                    last = nc.tensor.transpose(g.ps[:, 6 + c // 4, (c % 4) * P:(c % 4) * P + P],
                                               on[:, c * 128:(c + 1) * 128], g.ident[0:P, 0:P])
                    if c % 4 == 3:
                        last.then_inc(s["on_turned"], 1)
                pe.wait_ge(s["onT_kept"], 2 * i + 2)
                nc.tensor.matmul(g.ps[0:P, 6, 0:D], g.ones[0:1, 0:P], bo[:], start=True, stop=False)
                for c in range(C):
                    last = nc.tensor.matmul(g.ps[0:P, 6, 0:D], onT[:, c, :], wo[:, c, :], start=False,
                                            stop=(c == C - 1))
                last.then_inc(s["projected"], 1)

        @block.gpsimd
        def _(pool):
            nc.gpsimd.memset(v[:, :, DH:DH + 1], 1.0).then_inc(s["ones_set"], 1)
            with pool.Fori(0, T) as i:
                attend_diagonals(nc, g, a, s, i, groups, pool)

        @block.scalar
        def _(act):
            nc.scalar.copy(xt[:], g.xnT[:, 0:P]).then_inc(s["xt"], 1)
            with act.Fori(0, T) as i:
                for c in range(2):
                    act.wait_ge(s["q"], 2 * i + c + 1)
                    nc.scalar.mul(qT[:, 4 * c:4 * c + 4, :], g.ps[:, c, 0:W].rearrange("p (c t) -> p c t", c=4),
                                  DH ** -0.5).then_inc(s["q_kept"], 1)
                act.wait_ge(s["v"], 2 * i + 1)
                nc.scalar.copy(v[:, 0:H // 2, 0:DH], g.ps[0:P, 4, :].rearrange("p (h d) -> p h d", d=DH))\
                    .then_inc(s["v_kept"], 1)
                act.wait_ge(s["v"], 2 * i + 2)
                nc.scalar.copy(xt[:], g.next_tile(g.xnT, i)).then_inc(s["xt"], 1)
                attend_exponentials(nc, g, a, s, i, groups, act)
                for c in range(2):
                    act.wait_ge(s["on_turned"], 2 * i + c + 1)
                    nc.scalar.copy(onT[:, 4 * c:4 * c + 4, :], g.ps[:, 6 + c, 0:W].rearrange("p (c t) -> p c t", c=4))\
                        .then_inc(s["onT_kept"], 1)

        @block.vector
        def _(dve):
            dve.wait_ge(s["ones_set"], 1)
            with dve.Fori(0, T) as i:
                for c in range(2):
                    dve.wait_ge(s["k"], 2 * i + c + 1)
                    nc.vector.tensor_copy(kT[:, 4 * c:4 * c + 4, :],
                                          g.ps[:, 2 + c, 0:W].rearrange("p (c t) -> p c t", c=4))\
                        .then_inc(s["k_kept"], 1)
                dve.wait_ge(s["v"], 2 * i + 2)
                nc.vector.tensor_copy(v[:, H // 2:H, 0:DH], g.ps[0:P, 5, :].rearrange("p (h d) -> p h d", d=DH))\
                    .then_inc(s["v_kept"], 1)
                attend_vector(nc, g, a, s, i, groups, dve,
                              lambda i, k: on[:, (k // 2) * 2 * GH * DH:(k // 2 + 1) * 2 * GH * DH].rearrange(
                                  "p (h two d) -> p two h d", two=2, d=DH)[:, k % 2, :, :])
                dve.wait_ge(s["projected"], i + 1)
                nc.vector.tensor_tensor(g.x[:, i, :], g.x[:, i, :], g.ps[0:P, 6, 0:D], ALU.add)\
                    .then_inc(s["added"], 1)


def narrow_attention(nc, g, sb, name, v, qT, kT, head_scale, H, DH, masks, out):
    groups = H // GH
    qm = sb(f"{name}_qm", [128, 2, H, P])
    kt = sb(f"{name}_kt", [128, 2, P])
    a = Heads(sb, name, DH + 1, masks[0], masks[1], head=lambda k, h: GH * k + h,
              value=lambda i, h: v[:, i, h, :])
    tiles = lambda x, i: x[:].rearrange("p (t c) -> p t c", c=P)[:, i, :]
    with stage(nc, name, "kt", "qm", *ATTEND) as (block, s):
        @block.tensor
        def _(pe):
            with pe.Fori(0, T) as i:
                b = 0
                pe.wait_ge(s["kt"], i + 1)
                pe.wait_ge(s["qm"], i + 1)
                a.query, a.key = (lambda h: qm[:, b, h, :]), (lambda h: kt[:, b, :])
                a.query_group = lambda k: qm[:, b, GH * k:GH * k + GH, :].rearrange("p h t -> p (h t)")
                attend_groups(nc, g, a, s, i, groups, pe)

        @block.gpsimd
        def _(pool):
            with pool.Fori(0, T) as i:
                attend_diagonals(nc, g, a, s, i, groups, pool)

        @block.scalar
        def _(act):
            nc.scalar.copy(kt[:, 0, :], kT[:, 0:P]).then_inc(s["kt"], 1)
            with act.Fori(0, T) as i:
                attend_exponentials(nc, g, a, s, i, groups, act)
                nc.scalar.copy(kt[:, 0, :], g.next_tile(kT, i)).then_inc(s["kt"], 1)

        @block.vector
        def _(dve):
            nc.vector.tensor_tensor(qm[:, 0, :, :], under(qT[:, 0:P], H), over(head_scale, P), ALU.mult)\
                .then_inc(s["qm"], 1)
            with dve.Fori(0, T) as i:
                attend_vector(nc, g, a, s, i, groups, dve, out)
                nc.vector.tensor_tensor(qm[:, 0, :, :], under(g.next_tile(qT, i), H), over(head_scale, P),
                                        ALU.mult).then_inc(s["qm"], 1)


def project_values(nc, g, name, lhs, wv, bias, v, H, DH):
    with stage(nc, name, "v", "ones", "kept") as (block, s):
        @block.tensor
        def _(pe):
            for b in range(NB):
                for j in range(BT):
                    t = b * BT + j
                    bank = g.ps[0:P, b, j * D:(j + 1) * D]
                    if bias is not None:
                        nc.tensor.matmul(bank, g.ones[0:1, 0:P], bias[:], start=True, stop=False)
                    last = nc.tensor.matmul(bank, lhs[:, t * P:(t + 1) * P], wv, start=bias is None, stop=True)
                last.then_inc(s["v"], 1)

        @block.gpsimd
        def _(pool):
            nc.gpsimd.memset(v[:, :, :, DH:DH + 1], 1.0).then_inc(s["ones"], 1)

        @block.vector
        def _(dve):
            for b in range(NB):
                dve.wait_ge(s["v"], b + 1)
                for j in range(BT):
                    last = nc.vector.tensor_copy(
                        v[:, b * BT + j, :, 0:DH],
                        g.ps[0:P, b, j * D:(j + 1) * D].rearrange("p (h d) -> p h d", h=H))
                last.then_inc(s["kept"], 1)


def head_features(nc, link, mask, H, DH):
    link(nc.gpsimd.memset(mask[:], 1.0))
    link(nc.gpsimd.affine_select(out=mask[:], in_=mask[:], compare_op=ALU.is_ge, fill=0.0, base=0,
                                 pattern=[[-DH, H]], channel_multiplier=1))
    link(nc.gpsimd.affine_select(out=mask[:], in_=mask[:], compare_op=ALU.is_ge, fill=0.0, base=DH - 1,
                                 pattern=[[DH, H]], channel_multiplier=-1))


def biased_attention(nc, g, w, sb):
    H, DH = 8, 16
    wqT, wkv, wo = sb("a1_wqT", [D, D]), sb("a1_wkv", [D, 2, D]), sb("a1_wo", [D, D])
    scale_col, dir_row = sb("a1_scale_col", [D, 1]), sb("a1_dir_row", [1, D])
    normalize(nc, g, "a1_norm", g.x, [
        (wqT[:], w["L1_attn_WqT"]), (wkv[:], w["L1_attn_Wkv"].rearrange("d (a e) -> d a e", a=2)),
        (wo[:], w["L1_attn_Wout"]), (scale_col[:], column(w["L1_attn_head_scales_row"])),
        (dir_row[:], row(w["L1_attn_head_dirs_row"]))])
    same, mix, wq = sb("a1_same", [D, D]), sb("a1_mix", [D, D]), sb("a1_wq", [D, D])
    heads, v = sb("a1_heads", [D, H]), sb("a1_v", [P, T, H, DH + 1])
    qT, kT = g.workT, g.keyT
    with stage(nc, "a1_weights", "cut", "outer", "steps", "mixed", "wq", "wq_kept", "qk", "kept") as (block, s):
        @block.gpsimd
        def _(pool):
            link = in_order(pool, s["cut"])
            head_features(nc, link, heads, H, DH)
            link(nc.gpsimd.tensor_copy(same[:].rearrange("p (h d) -> p h d", h=H), over(heads[:], DH)))

        @block.tensor
        def _(pe):
            nc.tensor.matmul(g.ps[:, 0, 0:D], dir_row[:], dir_row[:], start=True, stop=True).then_inc(s["outer"], 1)
            pe.wait_ge(s["mixed"], 1)
            nc.tensor.matmul(g.ps[:, 1, 0:D], wqT[:], mix[:], start=True, stop=True).then_inc(s["wq"], 1)
            pe.wait_ge(s["wq_kept"], 1)
            for b in range(NB):
                nc.tensor.matmul(g.ps[:, b, 0:W], wq[:], g.xnT[:, b * W:(b + 1) * W], start=True, stop=True)
                nc.tensor.matmul(g.ps[:, NB + b, 0:W], wkv[:, 0, :], g.xnT[:, b * W:(b + 1) * W], start=True,
                                 stop=True).then_inc(s["qk"], 1)

        @block.vector
        def _(dve):
            link = in_order(dve, s["steps"])
            dve.wait_ge(s["cut"], 4)
            dve.wait_ge(s["outer"], 1)
            link(nc.vector.scalar_tensor_tensor(out=mix[:], in0=g.ps[:, 0, 0:D], scalar=scale_col[:, 0:1],
                                                in1=same[:], op0=ALU.mult, op1=ALU.mult))
            nc.vector.scalar_tensor_tensor(out=mix[:], in0=g.ident[:], scalar=DH ** -0.5, in1=mix[:],
                                           op0=ALU.mult, op1=ALU.add).then_inc(s["mixed"], 1)
            dve.wait_ge(s["wq"], 1)
            nc.vector.tensor_copy(wq[:], g.ps[:, 1, 0:D]).then_inc(s["wq_kept"], 1)
            for b in range(NB):
                dve.wait_ge(s["qk"], b + 1)
                nc.vector.tensor_copy(kT[:, b * W:(b + 1) * W], g.ps[:, NB + b, 0:W]).then_inc(s["kept"], 1)

        @block.scalar
        def _(act):
            for b in range(NB):
                act.wait_ge(s["qk"], b + 1)
                nc.scalar.copy(qT[:, b * W:(b + 1) * W], g.ps[:, b, 0:W]).then_inc(s["kept"], 1)
    project_values(nc, g, "a1_values", g.xnT, wkv[:, 1, :], None, v, H, DH)
    narrow_attention(nc, g, sb, "a1", v, qT, kT, heads[:], H, DH, (g.mask_q, g.mask_k),
                     lambda i, k: g.work[:, i, k * GH * DH:(k + 1) * GH * DH].rearrange("p (h d) -> p h d", h=GH))
    turn_and_project(nc, g, "a1_out", g.work, wo, None, g.x)


def scaled_attention(nc, g, w, sb):
    H, DH = 16, 8
    wq, wk, wv, wo = (sb(f"a2_{n}", [D, D]) for n in ("wq", "wk", "wv", "wo"))
    cols = sb("a2_cols", [D, 6])
    bv, bo4 = sb("a2_bv", [1, D]), sb("a2_bo4", [1, 4 * D])
    gains = sb("a2_gains", [P, 2, D])
    names = ("bq", "bk", "lq1", "lk1", "lq2", "lk2")
    flat = lambda ap: ap if len(ap.shape) == 1 else ap.rearrange("h d -> (h d)")
    normalize(nc, g, "a2_norm", g.x, [
        (wq[:], w["L2_attn_Wq"]), (wk[:], w["L2_attn_Wk"]), (wv[:], w["L2_attn_Wv"]), (wo[:], w["L2_attn_Wo"]),
        *[(cols[:, n:n + 1], column(flat(w[f"L2_attn_{name}"]))) for n, name in enumerate(names)],
        (bv[:], row(w["L2_attn_bv"])), (bo4[:], row(w["L2_attn_bo4"])),
        (gains[:, 0, :], rows(flat(w["L2_attn_gn_w"]), P)), (gains[:, 1, :], rows(flat(w["L2_attn_gn_b"]), P))])
    heads, same, v = sb("a2_heads", [D, H]), sb("a2_same", [D, D]), sb("a2_v", [P, T, H, DH + 1])
    dots, lams, scale = sb("a2_dots", [D, 2]), sb("a2_lams", [D, 3]), sb("a2_scale", [D, H])
    qT, kT = g.workT, g.keyT
    with stage(nc, "a2_weights", "cut", "steps", "dots", "sums", "exps", "qk", "kept") as (block, s):
        @block.gpsimd
        def _(pool):
            link = in_order(pool, s["cut"])
            head_features(nc, link, heads, H, DH)
            link(nc.gpsimd.tensor_copy(same[:].rearrange("p (h d) -> p h d", h=H), over(heads[:], DH)))

        @block.tensor
        def _(pe):
            for b in range(NB):
                if b == 2:
                    pe.wait_ge(s["dots"], 2)
                    pe.wait_ge(s["cut"], 4)
                    nc.tensor.matmul(g.ps[:, 7, 0:2], same[:], dots[:], start=True, stop=True).then_inc(s["sums"], 1)
                    pe.wait_ge(s["exps"], 1)
                nc.tensor.matmul(g.ps[:, b, 0:W], wq[:], g.xnT[:, b * W:(b + 1) * W], start=True, stop=True)
                nc.tensor.matmul(g.ps[:, NB + b, 0:W], wk[:], g.xnT[:, b * W:(b + 1) * W], start=True,
                                 stop=True).then_inc(s["qk"], 1)

        @block.vector
        def _(dve):
            link = in_order(dve, s["steps"])
            nc.vector.tensor_tensor(dots[:, 0:1], cols[:, 2:3], cols[:, 3:4], ALU.mult).then_inc(s["dots"], 1)
            nc.vector.tensor_tensor(dots[:, 1:2], cols[:, 4:5], cols[:, 5:6], ALU.mult).then_inc(s["dots"], 1)
            dve.wait_ge(s["exps"], 1)
            link(nc.vector.tensor_tensor(lams[:, 2:3], lams[:, 0:1], lams[:, 1:2], ALU.subtract))
            link(nc.vector.tensor_scalar(lams[:, 2:3], lams[:, 2:3], 0.8, DH ** -0.5, ALU.add, ALU.mult))
            dve.wait_ge(s["cut"], 4)
            link(nc.vector.tensor_scalar(scale[:], heads[:], lams[:, 2:3], None, ALU.mult))
            for b in range(NB):
                dve.wait_ge(s["qk"], b + 1)
                nc.vector.tensor_scalar(kT[:, b * W:(b + 1) * W], g.ps[:, NB + b, 0:W], cols[:, 1:2], None,
                                        ALU.add).then_inc(s["kept"], 1)

        @block.scalar
        def _(act):
            act.wait_ge(s["sums"], 1)
            nc.scalar.activation(lams[:, 0:2], g.ps[:, 7, 0:2], ACT.Exp).then_inc(s["exps"], 1)
            for b in range(NB):
                act.wait_ge(s["qk"], b + 1)
                nc.scalar.activation(qT[:, b * W:(b + 1) * W], g.ps[:, b, 0:W], ACT.Identity,
                                     bias=cols[:, 0:1]).then_inc(s["kept"], 1)
    project_values(nc, g, "a2_values", g.xnT, wv[:], bv, v, H, DH)
    narrow_attention(nc, g, sb, "a2", v, qT, kT, scale[:], H, DH, (g.mask_any, g.mask_any),
                     lambda i, k: g.work[:, i, k * GH * DH:(k + 1) * GH * DH].rearrange("p (h d) -> p h d", h=GH))
    both = sb("a2_both", [P, P])
    sums, mean, rstd = (sb(f"a2_{n}", [P, T * H]) for n in ("sums", "mean", "rstd"))
    half = sb("a2_half", [P, T * H])
    wide = g.work[:].rearrange("p t (h d) -> p (t h) d", d=DH)
    square = g.xn[:].rearrange("p t (h d) -> p (t h) d", d=DH)
    share = 1.0 / (S * DH)
    with stage(nc, "a2_gn", "cut", "sums", "steps", "total", "centred", "squared", "spread", "rstd") as (block, s):
        @block.gpsimd
        def _(pool):
            link = in_order(pool, s["cut"])
            link(nc.gpsimd.memset(half[:], -0.5))
            link(nc.gpsimd.tensor_scalar(both[:], g.mask_any[:, 0, :], 0.0, None, ALU.is_ge))
            pool.wait_ge(s["spread"], 1)
            nc.gpsimd.tensor_tensor(rstd[:], sums[:], half[:], ALU.pow).then_inc(s["rstd"], 1)

        @block.tensor
        def _(pe):
            pe.wait_ge(s["cut"], 2)
            for n in range(2):
                pe.wait_ge(s["sums"], n + 1)
                nc.tensor.matmul(g.ps[0:P, n, 0:T * H], both[:], sums[:], start=True, stop=True).then_inc(s["total"], 1)

        @block.scalar
        def _(act):
            act.wait_ge(s["centred"], 1)
            nc.scalar.activation(square, wide, ACT.Square).then_inc(s["squared"], 1)

        @block.vector
        def _(dve):
            link = in_order(dve, s["steps"])
            nc.vector.tensor_reduce(sums[:], wide, AX_X, ALU.add).then_inc(s["sums"], 1)
            dve.wait_ge(s["total"], 1)
            link(nc.vector.tensor_scalar(mean[:], g.ps[0:P, 0, 0:T * H], -share, None, ALU.mult))
            nc.vector.tensor_tensor(wide, wide, over(mean[:], DH), ALU.add).then_inc(s["centred"], 1)
            dve.wait_ge(s["squared"], 1)
            nc.vector.tensor_reduce(sums[:], square, AX_X, ALU.add).then_inc(s["sums"], 1)
            dve.wait_ge(s["total"], 2)
            nc.vector.tensor_scalar(sums[:], g.ps[0:P, 1, 0:T * H], share, EPS, ALU.mult, ALU.add)\
                .then_inc(s["spread"], 1)
            dve.wait_ge(s["rstd"], 1)
            link(nc.vector.tensor_tensor(wide, wide, over(rstd[:], DH), ALU.mult))
            link(nc.vector.tensor_tensor(g.work[:], g.work[:], under(gains[:, 0, :], T), ALU.mult))
            link(nc.vector.tensor_tensor(g.work[:], g.work[:], under(gains[:, 1, :], T), ALU.add))
    turn_and_project(nc, g, "a2_out", g.work, wo, bo4, g.x)


def rotary_attention(nc, g, w, sb):
    H, DH, DV = 16, 8, 32
    wqk = sb("a3_wqk", [D, 4, D])
    bqk = sb("a3_bqk", [D, 4])
    cs = sb("a3_cs", [D, 2, P])
    wkv, bkv = sb("a3_wkv", [D, DV]), sb("a3_bkv", [DV, 1])
    wv, bv, wo, bo4 = sb("a3_wv", [DV, D]), sb("a3_bv", [1, D]), sb("a3_wo", [D, D]), sb("a3_bo4", [1, 4 * D])
    names = ("wqr", "wqr_swapped", "wkr", "wkr_swapped")
    normalize(nc, g, "a3_norm", g.x, [
        *[(wqk[:, n, :], w[f"L3_attn_{name}"]) for n, name in enumerate(names)],
        *[(bqk[:, n:n + 1], column(w[f"L3_attn_{name.replace('w', 'b', 1)}"])) for n, name in enumerate(names)],
        (cs[:], w["rotary"].rearrange("a d t -> d a t")), (wkv[:], w["L3_attn_wkv"]),
        (bkv[:], column(w["L3_attn_bkv"])), (wv[:], w["L3_attn_wv"]), (bv[:], row(w["L3_attn_bv"])),
        (wo[:], w["L3_attn_wo"]), (bo4[:], row(w["L3_attn_bo4"]))])
    heads, v, cT = sb("a3_heads", [D, H]), sb("a3_v", [P, T, H, DH + 1]), sb("a3_cT", [DV, N])
    ra, rb = sb("a3_ra", [D, 2, W]), sb("a3_rb", [D, 2, W])
    outs = (g.workT, g.keyT)
    with stage(nc, "a3_qk", "cut", "c", "c_kept", "pair", "turned", "summed", "kept") as (block, s):
        @block.gpsimd
        def _(pool):
            link = in_order(pool, s["cut"])
            head_features(nc, link, heads, H, DH)
            link(nc.gpsimd.tensor_scalar(heads[:], heads[:], DH ** -0.5, None, ALU.mult))

        @block.tensor
        def _(pe):
            for b in range(NB):
                nc.tensor.matmul(g.ps[0:DV, b, 0:W], wkv[:], g.xnT[:, b * W:(b + 1) * W], start=True,
                                 stop=True).then_inc(s["c"], 1)
            pe.wait_ge(s["c_kept"], NB)
            for n in range(2 * NB):
                which, b = n // NB, n % NB
                if n >= 2:
                    pe.wait_ge(s["turned"], 2 * (n - 1))
                for m in range(2):
                    last = nc.tensor.matmul(g.ps[:, 2 * (n % 2) + m, 0:W], wqk[:, 2 * which + m, :],
                                            g.xnT[:, b * W:(b + 1) * W], start=True, stop=True)
                last.then_inc(s["pair"], 1)

        @block.vector
        def _(dve):
            for n in range(2 * NB):
                which = n // NB
                dve.wait_ge(s["pair"], n + 1)
                if n >= 2:
                    dve.wait_ge(s["kept"], n - 1)
                for m, r in enumerate((ra, rb)):
                    nc.vector.scalar_tensor_tensor(
                        out=r[:, n % 2, :].rearrange("p (j t) -> p j t", j=BT),
                        in0=g.ps[:, 2 * (n % 2) + m, 0:W].rearrange("p (j t) -> p j t", j=BT),
                        scalar=bqk[:, 2 * which + m:2 * which + m + 1], in1=under(cs[:, m, :], BT),
                        op0=ALU.add, op1=ALU.mult).then_inc(s["turned"], 1)
                dve.wait_ge(s["turned"], 2 * n + 2)
                nc.vector.tensor_tensor(ra[:, n % 2, :], ra[:, n % 2, :], rb[:, n % 2, :], ALU.add)\
                    .then_inc(s["summed"], 1)

        @block.scalar
        def _(act):
            for b in range(NB):
                act.wait_ge(s["c"], b + 1)
                nc.scalar.activation(cT[:, b * W:(b + 1) * W], g.ps[0:DV, b, 0:W], ACT.Gelu, bias=bkv[:, 0:1])\
                    .then_inc(s["c_kept"], 1)
            for n in range(2 * NB):
                which, b = n // NB, n % NB
                act.wait_ge(s["summed"], n + 1)
                nc.scalar.activation(outs[which][:, b * W:(b + 1) * W], ra[:, n % 2, :], ACT.Gelu)\
                    .then_inc(s["kept"], 1)
    project_values(nc, g, "a3_values", cT, wv[:], bv, v, H, DH)
    narrow_attention(nc, g, sb, "a3", v, outs[0], outs[1], heads[:], H, DH, (g.mask_q, g.mask_k),
                     lambda i, k: g.work[:, i, k * GH * DH:(k + 1) * GH * DH].rearrange("p (h d) -> p h d", h=GH))
    turn_and_project(nc, g, "a3_out", g.work, wo, bo4, g.x)


def best_two(nc, g, link, logits, E, r):
    for n, pick in enumerate((r.first, r.second)):
        link(nc.vector.tensor_reduce(r.top[:, n, :], logits[:], AX_X, ALU.max))
        link(nc.vector.tensor_tensor(pick[:], logits[:], over(r.top[:, n, :], E), ALU.is_equal))
        link(nc.vector.tensor_tensor(pick[:], pick[:], r.rank[:], ALU.mult))
        link(nc.vector.tensor_reduce(r.lead[:], pick[:], AX_X, ALU.max))
        link(nc.vector.tensor_tensor(pick[:], r.rank[:], over(r.lead[:], E), ALU.is_equal))
        if n == 0:
            link(nc.vector.scalar_tensor_tensor(out=logits[:], in0=pick[:], scalar=NEG, in1=logits[:],
                                                op0=ALU.mult, op1=ALU.add))


def rank_experts(nc, link, rank, E):
    for e in range(E):
        link(nc.gpsimd.memset(rank[:, :, e:e + 1], float(E - e)))


def token_logits(nc, g, wg, E, done):
    for t in range(T):
        last = nc.tensor.matmul(g.ps[0:P, 0, t * E:(t + 1) * E], g.xnT[:, t * P:(t + 1) * P], wg, start=True,
                                stop=True)
    last.then_inc(done, 1)


def experts(nc, g, name, sb, jobs, act_func, out, add_xn=False):
    hT = sb(f"{name}_hT", [128, 2, 4, W])
    part = sb(f"{name}_part", [P, 2, BT, D])
    J = len(jobs)
    ups = sum(len(j.up) for j in jobs)
    assert all(len(j.up) <= 4 for j in jobs)
    first_up = [sum(len(j.up) for j in jobs[:n]) for n in range(J)]
    with stage(nc, name, "up", "hidden", "down", "gated", "added") as (block, s):
        @block.tensor
        def _(pe):
            with pe.Fori(0, NB) as i:
                def up(n):
                    for m, (wt, _, extra) in enumerate(jobs[n].up):
                        u = first_up[n] + m
                        if u >= 2:
                            pe.wait_ge(s["hidden"], ups * i + u - 1)
                        bank = g.ps[:, u % 2, 0:W]
                        rows_ = wt.shape[1]
                        last = nc.tensor.matmul(bank[0:rows_], wt, g.block_of(g.xnT, i), start=True,
                                                stop=extra is None)
                        if extra is not None:
                            last = nc.tensor.matmul(bank[0:rows_], extra[0], extra[1](i), start=False, stop=True)
                        last.then_inc(s["up"], 1)

                def down(n):
                    job = jobs[n]
                    pe.wait_ge(s["hidden"], ups * i + first_up[n] + len(job.up))
                    if n >= 2:
                        pe.wait_ge(s["gated"], J * i + n - 1)
                    for j in range(BT):
                        bank = g.ps[0:P, 4 + n % 2, j * D:(j + 1) * D]
                        if job.out_bias is not None:
                            nc.tensor.matmul(bank, g.ones[0:1, 0:P], job.out_bias, start=True, stop=False,
                                             skip_group_check=True)
                        for m, wt in enumerate(job.down):
                            last = nc.tensor.matmul(bank, hT[:, n % 2, m, j * P:(j + 1) * P], wt,
                                                    start=(m == 0 and job.out_bias is None),
                                                    stop=(m == len(job.down) - 1), skip_group_check=True)
                    last.then_inc(s["down"], 1)

                up(0)
                for n in range(J):
                    if n + 1 < J:
                        up(n + 1)
                    down(n)
                pe.wait_ge(s["gated"], J * i + J)

        @block.scalar
        def _(act):
            with act.Fori(0, NB) as i:
                for n, job in enumerate(jobs):
                    if n >= 2:
                        act.wait_ge(s["down"], J * i + n - 1)
                    for m, (wt, bias, _) in enumerate(job.up):
                        u = first_up[n] + m
                        act.wait_ge(s["up"], ups * i + u + 1)
                        nc.scalar.activation(hT[0:wt.shape[1], n % 2, m, :], g.ps[0:wt.shape[1], u % 2, 0:W],
                                             act_func, bias=0.0 if bias is None else bias).then_inc(s["hidden"], 1)

        @block.vector
        def _(dve):
            with dve.Fori(0, NB) as i:
                target = g.tiles_of(out, i)
                if add_xn:
                    nc.vector.tensor_tensor(target, target, g.tiles_of(g.xn, i), ALU.add).then_inc(s["added"], 1)
                for n, job in enumerate(jobs):
                    dve.wait_ge(s["down"], J * i + n + 1)
                    bank = g.ps[0:P, 4 + n % 2, :].rearrange("p (j d) -> p j d", j=BT)
                    if job.gate is None:
                        nc.vector.tensor_copy(part[:, n % 2, :, :], bank).then_inc(s["gated"], 1)
                    else:
                        nc.vector.tensor_tensor(part[:, n % 2, :, :], bank, over(g.block_gate(job.gate, i), D),
                                                ALU.mult).then_inc(s["gated"], 1)
                    dve.wait_ge(s["gated"], J * i + n + 1)
                    if add_xn or n:
                        dve.wait_ge(s["added"], (J + int(add_xn)) * i + n + int(add_xn))
                    nc.vector.tensor_tensor(target, target, part[:, n % 2, :, :], ALU.add).then_inc(s["added"], 1)
                dve.wait_ge(s["added"], (J + int(add_xn)) * i + J + int(add_xn))


def shared_and_routed(nc, g, w, sb):
    E, F = 8, 4 * D
    FB = F // 128
    A = E + 2
    w1, w2 = sb("f0_w1", [D, A, F]), sb("f0_w2", [128, A, FB, D])
    wg, r = sb("f0_wg", [D, E]), Routing(sb, "f0", E)
    normalize(nc, g, "f0_norm", g.x, [
        (wg[:], w["L0_ffn_centroidsT"]), (r.bias[:], rows(w["L0_ffn_routing_bias"], P)),
        *[(w1[:, e, :], w["L0_ffn_WfcT"][e]) for e in range(A)],
        *[(w2[:, e, :, :], w["L0_ffn_WprojT"][e].rearrange("(c p) d -> p c d", p=128)) for e in range(A)]])
    with stage(nc, "f0_route", "ranked", "logits", "steps", "raw", "score", "gap", "exp") as (block, s):
        @block.gpsimd
        def _(pool):
            rank_experts(nc, in_order(pool, s["ranked"]), r.rank, E)

        @block.tensor
        def _(pe):
            token_logits(nc, g, wg[:], E, s["logits"])

        @block.scalar
        def _(act):
            act.wait_ge(s["logits"], 1)
            nc.scalar.activation(r.score[:], g.ps[0:P, 0, 0:T * E].rearrange("p (t e) -> p t e", t=T), ACT.Sigmoid)\
                .then_inc(s["score"], 1)
            act.wait_ge(s["gap"], 1)
            nc.scalar.activation(g.stat[:, 0, :], g.stat[:, 0, :], ACT.Exp).then_inc(s["exp"], 1)

        @block.vector
        def _(dve):
            link = in_order(dve, s["steps"])
            dve.wait_ge(s["logits"], 1)
            dve.wait_ge(s["ranked"], E)
            dve.wait_ge(s["score"], 1)
            link(nc.vector.tensor_tensor(r.logits[:], g.ps[0:P, 0, 0:T * E].rearrange("p (t e) -> p t e", t=T),
                                         under(r.bias[:], T), ALU.add))
            best_two(nc, g, link, r.logits, E, r)
            dve.wait_ge(s["score"], 1)
            for n, pick in enumerate((r.first, r.second)):
                link(nc.vector.tensor_tensor(r.combine[:], pick[:], r.score[:], ALU.mult))
                link(nc.vector.tensor_reduce(r.top[:, n, :], r.combine[:], AX_X, ALU.add))
            link(nc.vector.tensor_tensor(r.a[:], r.top[:, 0, :], r.top[:, 1, :], ALU.max))
            link(nc.vector.tensor_tensor(r.b[:], r.top[:, 0, :], r.top[:, 1, :], ALU.min))
            nc.vector.tensor_tensor(g.stat[:, 0, :], r.b[:], r.a[:], ALU.subtract).then_inc(s["gap"], 1)
            dve.wait_ge(s["exp"], 1)
            link(nc.vector.tensor_scalar(r.a[:], g.stat[:, 0, :], 1.0, None, ALU.add))
            link(nc.vector.reciprocal(r.a[:], r.a[:]))
            link(nc.vector.tensor_tensor(r.b[:], g.stat[:, 0, :], r.a[:], ALU.mult))
            link(nc.vector.tensor_tensor(r.lead[:], r.top[:, 0, :], r.top[:, 1, :], ALU.is_ge))
            link(nc.vector.tensor_tensor(g.stat[:, 1, :], r.a[:], r.b[:], ALU.subtract))
            link(nc.vector.tensor_tensor(g.stat[:, 1, :], g.stat[:, 1, :], r.lead[:], ALU.mult))
            link(nc.vector.tensor_tensor(g.stat[:, 2, :], g.stat[:, 1, :], r.b[:], ALU.add))
            link(nc.vector.tensor_tensor(g.stat[:, 3, :], r.a[:], g.stat[:, 1, :], ALU.subtract))
            link(nc.vector.tensor_tensor(r.first[:], r.first[:], over(g.stat[:, 2, :], E), ALU.mult))
            link(nc.vector.tensor_tensor(r.second[:], r.second[:], over(g.stat[:, 3, :], E), ALU.mult))
            link(nc.vector.tensor_tensor(r.combine[:], r.first[:], r.second[:], ALU.add))
    jobs = [Expert([(w1[:, e, m * 128:(m + 1) * 128], None, None) for m in range(FB)],
                   [w2[:, e, m, :] for m in range(FB)], gate=None if e < 2 else r.combine[:, :, e - 2])
            for e in range(A)]
    experts(nc, g, "f0", sb, jobs, ACT.Gelu, g.x, add_xn=True)


def capped_experts(nc, g, w, sb):
    E, F, CAP = 8, 512, 512
    FB = F // 128
    w1, w2 = sb("f1_w1", [D, E, F]), sb("f1_w2", [128, E, FB, D])
    b1, b2 = sb("f1_b1", [128, E, FB]), sb("f1_b2", [1, E, D])
    rw1, rb1, rw2 = sb("f1_rw1", [D, F]), sb("f1_rb1", [128, FB]), sb("f1_rw2", [128, FB, E])
    r = Routing(sb, "f1", E)
    normalize(nc, g, "f1_norm", g.x, [
        (rw1[:], w["L1_ffn_rw1"]), (rb1[:], w["L1_ffn_rb1_cols"]),
        (rw2[:], w["L1_ffn_rw2"].rearrange("(m p) e -> p m e", p=128)), (r.bias[:], rows(w["L1_ffn_rb2"], P)),
        (b1[:], w["L1_ffn_eb1_cols"]),
        (b2[:], w["L1_ffn_eb2"].rearrange("(a e) d -> a e d", a=1)),
        *[(w1[:, e, :], w["L1_ffn_ew1"][e]) for e in range(E)],
        *[(w2[:, e, :, :], w["L1_ffn_ew2"][e].rearrange("(c p) d -> p c d", p=128)) for e in range(E)]])
    hT = sb("f1_router_hT", [128, FB, W])
    earlier = sb("f1_earlier", [P, P])
    chosen, before, total = (sb(f"f1_{n}", [P, T, E]) for n in ("chosen", "before", "total"))
    with stage(nc, "f1_route", "ranked", "up", "hidden", "logits", "logits_kept", "steps", "gap", "exp", "chosen",
               "counts") as (block, s):
        @block.gpsimd
        def _(pool):
            link = in_order(pool, s["ranked"])
            rank_experts(nc, link, r.rank, E)
            link(nc.gpsimd.memset(earlier[:], 1.0))
            link(nc.gpsimd.affine_select(out=earlier[:], in_=earlier[:], compare_op=ALU.is_ge, fill=0.0,
                                         base=-1, pattern=[[1, P]], channel_multiplier=-1))

        @block.tensor
        def _(pe):
            for b in range(NB):
                for m in range(FB):
                    if b:
                        pe.wait_ge(s["hidden"], FB * (b - 1) + m + 1)
                    nc.tensor.matmul(g.ps[:, m, 0:W], rw1[:, m * 128:(m + 1) * 128], g.xnT[:, b * W:(b + 1) * W],
                                     start=True, stop=True).then_inc(s["up"], 1)
                pe.wait_ge(s["hidden"], FB * (b + 1))
                for j in range(BT):
                    for m in range(FB):
                        last = nc.tensor.matmul(g.ps[0:P, 4 + b % 2, j * E:(j + 1) * E], hT[:, m, j * P:(j + 1) * P],
                                                rw2[:, m, :], start=(m == 0), stop=(m == FB - 1))
                last.then_inc(s["logits"], 1)
                if b % 2:
                    pe.wait_ge(s["logits_kept"], b + 1)
            pe.wait_ge(s["chosen"], 1)
            nc.tensor.matmul(g.ps[0:P, 6, 0:T * E], earlier[:], chosen[:].rearrange("p t e -> p (t e)"),
                             start=True, stop=True)
            nc.tensor.matmul(g.ps[0:P, 7, 0:T * E], g.ones[0:P, 0:P], chosen[:].rearrange("p t e -> p (t e)"),
                             start=True, stop=True).then_inc(s["counts"], 1)

        @block.scalar
        def _(act):
            for b in range(NB):
                if b:
                    act.wait_ge(s["logits"], b)
                for m in range(FB):
                    act.wait_ge(s["up"], FB * b + m + 1)
                    nc.scalar.activation(hT[:, m, :], g.ps[:, m, 0:W], ACT.Relu, bias=rb1[:, m:m + 1])\
                        .then_inc(s["hidden"], 1)
            act.wait_ge(s["gap"], 1)
            nc.scalar.activation(r.a[:], g.stat[:, 0, :], ACT.Exp).then_inc(s["exp"], 1)

        @block.vector
        def _(dve):
            link = in_order(dve, s["steps"])
            for b in range(NB):
                dve.wait_ge(s["logits"], b + 1)
                nc.vector.tensor_tensor(r.logits[:, b * BT:(b + 1) * BT, :],
                                        g.ps[0:P, 4 + b % 2, 0:BT * E].rearrange("p (t e) -> p t e", t=BT),
                                        under(r.bias[:], BT), ALU.add).then_inc(s["logits_kept"], 1)
            dve.wait_ge(s["logits_kept"], NB)
            dve.wait_ge(s["ranked"], E + 2)
            best_two(nc, g, link, r.logits, E, r)
            nc.vector.tensor_tensor(chosen[:], r.first[:], r.second[:], ALU.add).then_inc(s["chosen"], 1)
            nc.vector.tensor_tensor(g.stat[:, 0, :], r.top[:, 1, :], r.top[:, 0, :], ALU.subtract)\
                .then_inc(s["gap"], 1)
            dve.wait_ge(s["exp"], 1)
            weigh_two(nc, link, r, E)
            dve.wait_ge(s["counts"], 1)
            link(nc.vector.tensor_copy(total[:], g.ps[0:P, 7, 0:T * E].rearrange("p (t e) -> p t e", t=T)))
            link(nc.vector.memset(before[:, 0:1, :], 0.0))
            for t in range(1, T):
                link(nc.vector.tensor_tensor(before[:, t, :], before[:, t - 1, :], total[:, t - 1, :], ALU.add))
            link(nc.vector.tensor_tensor(before[:], before[:],
                                         g.ps[0:P, 6, 0:T * E].rearrange("p (t e) -> p t e", t=T), ALU.add))
            link(nc.vector.scalar_tensor_tensor(out=r.combine[:], in0=before[:], scalar=float(CAP),
                                                in1=r.combine[:], op0=ALU.is_lt, op1=ALU.mult))
    jobs = [Expert([(w1[:, e, m * 128:(m + 1) * 128], b1[:, e, m:m + 1], None) for m in range(FB)],
                   [w2[:, e, m, :] for m in range(FB)], out_bias=b2[0:1, e, :], gate=r.combine[:, :, e])
            for e in range(E)]
    experts(nc, g, "f1", sb, jobs, ACT.Relu, g.x)


def weigh_two(nc, link, r, E):
    link(nc.vector.tensor_scalar(r.b[:], r.a[:], 1.0, None, ALU.add))
    link(nc.vector.reciprocal(r.b[:], r.b[:]))
    link(nc.vector.tensor_tensor(r.a[:], r.a[:], r.b[:], ALU.mult))
    link(nc.vector.tensor_tensor(r.first[:], r.first[:], over(r.b[:], E), ALU.mult))
    link(nc.vector.tensor_tensor(r.second[:], r.second[:], over(r.a[:], E), ALU.mult))
    link(nc.vector.tensor_tensor(r.combine[:], r.first[:], r.second[:], ALU.add))


def small_experts(nc, g, w, sb):
    E, F = 8, 64
    w1, w2 = sb("f2_w1", [D, E * F]), sb("f2_w2", [128, E // 2, D])
    b1, b2 = sb("f2_b1", [128, E // 2]), sb("f2_b2", [1, E, D])
    wg, r = sb("f2_wg", [D, E]), Routing(sb, "f2", E)
    normalize(nc, g, "f2_norm", g.x, [
        (wg[:], w["L2_ffn_gate_w"]), (r.bias[:], rows(w["L2_ffn_gate_b"], P)),
        (w1[:].rearrange("d (e f) -> d e f", e=E), w["L2_ffn_w1"].rearrange("e d f -> d e f")),
        (w2[:], w["L2_ffn_w2"].rearrange("(c a) f d -> (a f) c d", a=2)),
        (b1[:], w["L2_ffn_b1_cols"]),
        (b2[:], w["L2_ffn_b2"].rearrange("(a e) d -> a e d", a=1))])
    with stage(nc, "f2_route", "ranked", "logits", "steps", "gap", "exp") as (block, s):
        @block.gpsimd
        def _(pool):
            rank_experts(nc, in_order(pool, s["ranked"]), r.rank, E)

        @block.tensor
        def _(pe):
            token_logits(nc, g, wg[:], E, s["logits"])

        @block.scalar
        def _(act):
            act.wait_ge(s["gap"], 1)
            nc.scalar.activation(r.a[:], g.stat[:, 0, :], ACT.Exp).then_inc(s["exp"], 1)

        @block.vector
        def _(dve):
            link = in_order(dve, s["steps"])
            dve.wait_ge(s["logits"], 1)
            dve.wait_ge(s["ranked"], E)
            link(nc.vector.tensor_tensor(r.logits[:], g.ps[0:P, 0, 0:T * E].rearrange("p (t e) -> p t e", t=T),
                                         under(r.bias[:], T), ALU.add))
            best_two(nc, g, link, r.logits, E, r)
            nc.vector.tensor_tensor(g.stat[:, 0, :], r.top[:, 1, :], r.top[:, 0, :], ALU.subtract)\
                .then_inc(s["gap"], 1)
            dve.wait_ge(s["exp"], 1)
            weigh_two(nc, link, r, E)
    jobs = [Expert([(w1[:, c * 128:(c + 1) * 128], b1[:, c:c + 1], None)], []) for c in range(E // 2)]
    paired_experts(nc, g, "f2", sb, jobs, w2, b2, r, E, F)


def paired_experts(nc, g, name, sb, jobs, w2, b2, r, E, F):
    hT = sb(f"{name}_hT", [128, 2, W])
    part = sb(f"{name}_part", [P, 2, BT, D])
    C = E // 2
    with stage(nc, name, "up", "hidden", "down", "gated", "added") as (block, s):
        @block.tensor
        def _(pe):
            with pe.Fori(0, NB) as i:
                def up(c):
                    if c >= 2:
                        pe.wait_ge(s["hidden"], C * i + c - 1)
                    nc.tensor.matmul(g.ps[:, c % 2, 0:W], jobs[c].up[0][0], g.block_of(g.xnT, i), start=True,
                                     stop=True).then_inc(s["up"], 1)

                up(0)
                for c in range(C):
                    if c + 1 < C:
                        up(c + 1)
                    pe.wait_ge(s["hidden"], C * i + c + 1)
                    for half in range(2):
                        e = 2 * c + half
                        if e >= 4:
                            pe.wait_ge(s["gated"], E * i + e - 3)
                        for j in range(BT):
                            bank = g.ps[0:P, 4 + 2 * half + c % 2, j * D:(j + 1) * D]
                            nc.tensor.matmul(bank, g.ones[0:1, 0:P], b2[0:1, e, :], start=True, stop=False,
                                             skip_group_check=True)
                            last = nc.tensor.matmul(bank, hT[F * half:F * half + F, c % 2, j * P:(j + 1) * P],
                                                    w2[F * half:F * half + F, c, :], start=False, stop=True,
                                                    skip_group_check=True)
                        last.then_inc(s["down"], 1)
                pe.wait_ge(s["gated"], E * i + E)

        @block.scalar
        def _(act):
            with act.Fori(0, NB) as i:
                for c in range(C):
                    if c >= 2:
                        act.wait_ge(s["down"], E * i + 2 * c - 2)
                    act.wait_ge(s["up"], C * i + c + 1)
                    nc.scalar.activation(hT[:, c % 2, :], g.ps[:, c % 2, 0:W], ACT.Gelu, bias=jobs[c].up[0][1])\
                        .then_inc(s["hidden"], 1)

        @block.vector
        def _(dve):
            with dve.Fori(0, NB) as i:
                target = g.tiles_of(g.x, i)
                for e in range(E):
                    dve.wait_ge(s["down"], E * i + e + 1)
                    bank = g.ps[0:P, 4 + 2 * (e % 2) + e // 2 % 2, :].rearrange("p (j d) -> p j d", j=BT)
                    nc.vector.tensor_tensor(part[:, e % 2, :, :], bank, over(g.block_gate(r.combine[:, :, e], i), D),
                                            ALU.mult).then_inc(s["gated"], 1)
                    dve.wait_ge(s["gated"], E * i + e + 1)
                    if e:
                        dve.wait_ge(s["added"], E * i + e)
                    nc.vector.tensor_tensor(target, target, part[:, e % 2, :, :], ALU.add).then_inc(s["added"], 1)
                dve.wait_ge(s["added"], E * i + E)


def adapted_experts(nc, g, w, sb):
    E, F, R = 4, 512, 4
    FB = F // 128
    wi, wo = sb("f3_wi", [D, F]), sb("f3_wo", [128, FB, D])
    low, high = sb("f3_low", [D, E, R]), sb("f3_high", [R, E, F])
    wg, r = sb("f3_wg", [D, E]), Routing(sb, "f3", E)
    normalize(nc, g, "f3_norm", g.x, [
        (wg[:], w["L3_ffn_WgT"]), (r.bias[:], rows(w["L3_ffn_bg"], P)), (wi[:], w["L3_ffn_WiT"]),
        (wo[:], w["L3_ffn_WoT"].rearrange("(c p) d -> p c d", p=128)),
        (low[:], w["L3_ffn_AT"].rearrange("d (e r) -> d e r", e=E)),
        (high[:], w["L3_ffn_BT"].rearrange("r (e f) -> r e f", e=E))])
    lowT = sb("f3_lowT", [R, E, N])
    with stage(nc, "f3_route", "ranked", "logits", "low", "low_kept", "steps", "gap", "exp") as (block, s):
        @block.gpsimd
        def _(pool):
            rank_experts(nc, in_order(pool, s["ranked"]), r.rank, E)

        @block.tensor
        def _(pe):
            token_logits(nc, g, wg[:], E, s["logits"])
            for e in range(E):
                for b in range(NB):
                    n = e * NB + b
                    if n >= 2:
                        pe.wait_ge(s["low_kept"], n - 1)
                    nc.tensor.matmul(g.ps[0:R, 1 + n % 2, 0:W], low[:, e, :], g.xnT[:, b * W:(b + 1) * W],
                                     start=True, stop=True).then_inc(s["low"], 1)

        @block.scalar
        def _(act):
            for e in range(E):
                for b in range(NB):
                    n = e * NB + b
                    act.wait_ge(s["low"], n + 1)
                    nc.scalar.copy(lowT[:, e, b * W:(b + 1) * W], g.ps[0:R, 1 + n % 2, 0:W]).then_inc(s["low_kept"], 1)
            act.wait_ge(s["gap"], 1)
            nc.scalar.activation(r.score[:], r.score[:], ACT.Exp).then_inc(s["exp"], 1)

        @block.vector
        def _(dve):
            link = in_order(dve, s["steps"])
            dve.wait_ge(s["logits"], 1)
            dve.wait_ge(s["ranked"], E)
            link(nc.vector.tensor_tensor(r.logits[:], g.ps[0:P, 0, 0:T * E].rearrange("p (t e) -> p t e", t=T),
                                         under(r.bias[:], T), ALU.add))
            link(nc.vector.tensor_copy(r.kept_logits[:], r.logits[:]))
            best_two(nc, g, link, r.logits, E, r)
            nc.vector.tensor_tensor(r.score[:], r.kept_logits[:], over(r.top[:, 0, :], E), ALU.subtract)\
                .then_inc(s["gap"], 1)
            dve.wait_ge(s["exp"], 1)
            link(nc.vector.tensor_reduce(r.a[:], r.score[:], AX_X, ALU.add))
            link(nc.vector.reciprocal(r.a[:], r.a[:]))
            link(nc.vector.tensor_tensor(r.score[:], r.score[:], over(r.a[:], E), ALU.mult))
            link(nc.vector.tensor_tensor(r.first[:], r.first[:], r.second[:], ALU.add))
            link(nc.vector.tensor_tensor(r.combine[:], r.first[:], r.score[:], ALU.mult))
    jobs = [Expert([(wi[:, m * 128:(m + 1) * 128], None,
                     (high[:, e, m * 128:(m + 1) * 128], lambda i, e=e: g.block_of(lowT[:, e, :], i)))
                    for m in range(FB)],
                   [wo[:, m, :] for m in range(FB)], gate=r.combine[:, :, e]) for e in range(E)]
    experts(nc, g, "f3", sb, jobs, ACT.Relu, g.x)


RING = 4


def cross_attend(nc, g, w, sb, name, H, wqk, wvo, out_row, context_norm=False, q_row=None):
    R = H * S
    RG = min(R, P)
    G, KJ = R // RG, 3
    LJ = L // KJ
    M = G * KJ
    KQ = wqk(0).shape[1]
    HB = min(H, GH)
    kT = sb(f"{name}_kT", [DC + 1, 2, LC, LP])
    tok = sb(f"{name}_tok", [LP, 2, LC, DC + 1])
    raw = sb(f"{name}_raw", [LP, 2, LC, DC + 1]) if context_norm else tok
    qa = sb(f"{name}_qa", [DC + 1, 2, R])
    maxima, negmax = sb(f"{name}_maxima", [RG, 2, G, KJ]), sb(f"{name}_negmax", [RG, 2, G])
    diag = sb(f"{name}_diag", [RG, 2, G, RG])
    probs = sb(f"{name}_probs", [LP, RING, R])
    inverse, spread = sb(f"{name}_inverse", [DC + 1, 2, R]), sb(f"{name}_spread", [DC, 2, R])
    oT = sb(f"{name}_oT", [DC + 1, H, 2, S])
    extra = ("sum", "centred", "squared", "variance", "deviation", "rstd", "pool_steps", "normal", "turned",
             "kT_kept", "context_steps") if context_norm else ()
    if context_norm:
        cstat = sb(f"{name}_cstat", [LP, 2, 4, LC])
        square = sb(f"{name}_square", [LP, 2, LC, DC])
        half = sb(f"{name}_half", [LP, LC])
    with stage(nc, name, "context_0", "context_1", "set", "q", "q_kept", "scores", "max_taken", "negmax", "diag",
               "row", "row_kept", "turned_scores", "probs", "mixed", "inverse", "spread", "spread_kept", "normal_o",
               "projected", "added", *extra) as (block, s):
        context = (s["context_0"], s["context_1"])

        @block.sync
        def _(sp):
            def load(i, b):
                n = TB * i + b
                if not context_norm:
                    sp.dma_start(kT[:, b, :, :], g.ctxT[n, :, :, :]).then_inc(context[b], 16)
                sp.dma_start(raw[:, b, :, :], g.ctx[n, :, :, :]).then_inc(context[b], 16)

            for b in range(TB):
                load(0, b)
            with sp.Fori(0, T - 1) as i:
                for b in range(TB):
                    if context_norm:
                        sp.wait_ge(s["normal"], TB * i + b + 1)
                    else:
                        sp.wait_ge(s["mixed"], LC * (TB * i + b + 1))
                    load(i + 1, b)

        loads = 16 if context_norm else 32

        @block.tensor
        def _(pe):
            pe.wait_ge(s["set"], 1)
            with pe.Fori(0, T) as i:
                def queries():
                    for h in range(H):
                        last = nc.tensor.matmul(g.ps[0:KQ, 5 + h // GH, (h % GH) * P:(h % GH + 1) * P], wqk(h),
                                                g.tile_of(g.xnT, i), start=True, stop=q_row is None)
                        if q_row is not None:
                            last = nc.tensor.matmul(g.ps[0:KQ, 5, 0:P], q_row[:], g.ones[0:1, 0:P], start=False,
                                                    stop=True)
                        if h % GH == HB - 1:
                            last.then_inc(s["q"], 1)

                def turn_context(b):
                    seq = TB * i + b
                    pe.wait_ge(s["normal"], seq + 1)
                    if b:
                        pe.wait_ge(s["max_taken"], M * seq)
                    for j in range(KJ):
                        for c in range(LC // KJ):
                            last = nc.tensor.transpose(g.ps[0:DC + 1, j, c * LP:(c + 1) * LP],
                                                       tok[:, b, j * (LC // KJ) + c, :], g.ident[0:LP, 0:LP])
                        last.then_inc(s["turned"], 1)
                    pe.wait_ge(s["kT_kept"], KJ * (seq + 1))

                def scores(b):
                    seq = TB * i + b
                    if not context_norm:
                        pe.wait_ge(context[b], loads * (i + 1))
                    for m in range(M):
                        if m >= 3 or b == 1:
                            pe.wait_ge(s["max_taken"], M * seq + m - 2)
                        r, j = m // KJ, m % KJ
                        nc.tensor.matmul(g.ps[0:RG, m % 3, 0:LJ], qa[0:KQ, b, r * RG:(r + 1) * RG],
                                         kT[0:KQ, b, j * (LC // KJ):(j + 1) * (LC // KJ), :]
                                         .rearrange("p c k -> p (c k)"),
                                         start=True, stop=True).then_inc(s["scores"], 1)

                def maxima_row(b):
                    seq = TB * i + b
                    pe.wait_ge(s["diag"], seq + 1)
                    if b:
                        pe.wait_ge(s["row_kept"], seq)
                    nc.tensor.matmul(g.ps[0:DC + 1, 7, 0:R], g.last_row[0:RG, :],
                                     diag[:, b, :, :].rearrange("p r c -> p (r c)"), start=True, stop=True)\
                        .then_inc(s["row"], 1)

                def turned_scores(b, c):
                    n = LC * (TB * i + b) + c
                    if c == 0:
                        pe.wait_ge(s["row_kept"], TB * i + b + 1)
                    if c >= 2:
                        pe.wait_ge(s["probs"], n - 1)
                    nc.tensor.matmul(g.ps[0:LP, 3 + c % 2, 0:R], kT[:, b, c, :], qa[:, b, :], start=True,
                                     stop=True).then_inc(s["turned_scores"], 1)

                def mix(b, c):
                    n = LC * (TB * i + b) + c
                    pe.wait_ge(s["probs"], n + 1)
                    nc.tensor.matmul(g.ps[0:DC + 1, 5 + b, 0:R], tok[:, b, c, :], probs[:, c % RING, :],
                                     start=(c == 0), stop=(c == LC - 1)).then_inc(s["mixed"], 1)

                def spread_inverse(b):
                    pe.wait_ge(s["inverse"], TB * i + b + 1)
                    if b:
                        pe.wait_ge(s["spread_kept"], TB * i + b)
                    nc.tensor.matmul(g.ps[0:DC, 7, 0:R], g.ones[DC:DC + 1, 0:DC], inverse[DC:DC + 1, b, :],
                                     start=True, stop=True).then_inc(s["spread"], 1)

                queries()
                pe.wait_ge(s["q_kept"], (H // HB) * (i + 1))
                for b in range(TB):
                    if context_norm:
                        turn_context(b)
                    scores(b)
                for b in range(TB):
                    maxima_row(b)
                    for c in range(LC + 2):
                        if c < LC:
                            turned_scores(b, c)
                        if c >= 2:
                            mix(b, c - 2)
                        if b and c == 4:
                            spread_inverse(0)
                spread_inverse(1)
                pe.wait_ge(s["normal_o"], TB * i + 2)
                y = g.ps[0:P, 7, 0:D]
                if out_row is not None:
                    nc.tensor.matmul(y, g.ones[0:1, 0:P], out_row, start=True, stop=False)
                for h in range(H):
                    wt = wvo(h)
                    k = wt.shape[0]
                    last = nc.tensor.matmul(y, oT[0:k, h, :, :].rearrange("p b t -> p (b t)"), wt,
                                            start=(h == 0 and out_row is None), stop=(h == H - 1))
                last.then_inc(s["projected"], 1)
                pe.wait_ge(s["added"], i + 1)

        @block.gpsimd
        def _(pool):
            if context_norm:
                nc.gpsimd.memset(half[:], -0.5).then_inc(s["pool_steps"], 1)
                pool.wait_ge(s["pool_steps"], 1)
            nc.gpsimd.memset(oT[DC:DC + 1, :, :, :], 1.0).then_inc(s["set"], 1)
            with pool.Fori(0, T) as i:
                if context_norm:
                    for b in range(TB):
                        seq = TB * i + b
                        pool.wait_ge(s["deviation"], seq + 1)
                        nc.gpsimd.tensor_tensor(cstat[:, b, 3, :], cstat[:, b, 2, :], half[:], ALU.pow)\
                            .then_inc(s["rstd"], 1)
                for b in range(TB):
                    pool.wait_ge(s["negmax"], TB * i + b + 1)
                    for r in range(G):
                        last = nc.gpsimd.tensor_tensor(diag[:, b, r, :], g.ident[0:RG, 0:RG],
                                                       negmax[:, b, r:r + 1].to_broadcast([RG, RG]), ALU.mult)
                    last.then_inc(s["diag"], 1)

        @block.scalar
        def _(act):
            with act.Fori(0, T) as i:
                act.wait_ge(s["q"], (H // HB) * i + 1)
                nc.scalar.copy(qa[0:KQ, :, 0:HB * S].rearrange("p b (h t) -> p h b t", h=HB),
                               g.ps[0:KQ, 5, 0:HB * P].rearrange("p (h b t) -> p h b t", h=HB, b=TB))\
                    .then_inc(s["q_kept"], 1)
                if context_norm:
                    for b in range(TB):
                        act.wait_ge(s["centred"], TB * i + b + 1)
                        nc.scalar.activation(square[:, b, :, :], tok[:, b, :, 0:DC], ACT.Square)\
                            .then_inc(s["squared"], 1)
                    for b in range(TB):
                        for j in (0, 2):
                            act.wait_ge(s["turned"], KJ * (TB * i + b) + j + 1)
                            nc.scalar.copy(kT[:, b, 4 * j:4 * j + 4, :].rearrange("p c k -> p (c k)"),
                                           g.ps[0:DC + 1, j, 0:LJ]).then_inc(s["kT_kept"], 1)
                for b in range(TB):
                    act.wait_ge(s["row"], TB * i + b + 1)
                    if KQ == DC:
                        nc.scalar.copy(qa[DC:DC + 1, b, :], g.ps[DC:DC + 1, 7, 0:R]).then_inc(s["row_kept"], 1)
                    for c in range(LC):
                        n = LC * (TB * i + b) + c
                        act.wait_ge(s["turned_scores"], n + 1)
                        if c >= RING or b:
                            act.wait_ge(s["mixed"], n - RING + 1)
                        nc.scalar.activation(probs[:, c % RING, :], g.ps[0:LP, 3 + c % 2, 0:R], ACT.Exp)\
                            .then_inc(s["probs"], 1)
                        if b and c == 5:
                            act.wait_ge(s["spread"], TB * i + 1)
                            nc.scalar.copy(spread[:, 0, :], g.ps[0:DC, 7, 0:R]).then_inc(s["spread_kept"], 1)
                act.wait_ge(s["spread"], TB * i + 2)
                nc.scalar.copy(spread[:, 1, :], g.ps[0:DC, 7, 0:R]).then_inc(s["spread_kept"], 1)

        @block.vector
        def _(dve):
            with dve.Fori(0, T) as i:
                def normalize_context(b):
                    seq = TB * i + b
                    dve.wait_ge(context[b], loads * (i + 1))
                    nc.vector.tensor_reduce(cstat[:, b, 0, :], raw[:, b, :, 0:DC], AX_X, ALU.add).then_inc(s["sum"], 1)
                    dve.wait_ge(s["sum"], seq + 1)
                    nc.vector.tensor_scalar(cstat[:, b, 1, :], cstat[:, b, 0, :], -1.0 / DC, None, ALU.mult)\
                        .then_inc(s["context_steps"], 1)
                    nc.vector.tensor_copy(tok[:, b, :, DC:DC + 1], raw[:, b, :, DC:DC + 1])\
                        .then_inc(s["context_steps"], 1)
                    dve.wait_ge(s["context_steps"], 2 * seq + 2)
                    nc.vector.tensor_tensor(tok[:, b, :, 0:DC], raw[:, b, :, 0:DC], over(cstat[:, b, 1, :], DC),
                                            ALU.add).then_inc(s["centred"], 1)

                def scale_context(b):
                    seq = TB * i + b
                    dve.wait_ge(s["squared"], seq + 1)
                    nc.vector.tensor_reduce(cstat[:, b, 0, :], square[:, b, :, :], AX_X, ALU.add)\
                        .then_inc(s["variance"], 1)
                    dve.wait_ge(s["variance"], seq + 1)
                    nc.vector.tensor_scalar(cstat[:, b, 2, :], cstat[:, b, 0, :], 1.0 / DC, EPS, ALU.mult, ALU.add)\
                        .then_inc(s["deviation"], 1)
                    dve.wait_ge(s["rstd"], seq + 1)
                    nc.vector.tensor_tensor(tok[:, b, :, 0:DC], tok[:, b, :, 0:DC], over(cstat[:, b, 3, :], DC),
                                            ALU.mult).then_inc(s["normal"], 1)

                if H > GH:
                    dve.wait_ge(s["q"], 2 * i + 2)
                    nc.vector.tensor_copy(qa[0:KQ, :, GH * S:R].rearrange("p b (h t) -> p h b t", h=GH),
                                          g.ps[0:KQ, 6, 0:GH * P].rearrange("p (h b t) -> p h b t", h=GH, b=TB))\
                        .then_inc(s["q_kept"], 1)
                if context_norm:
                    for b in range(TB):
                        normalize_context(b)
                    for b in range(TB):
                        scale_context(b)
                for b in range(TB):
                    seq = TB * i + b
                    if context_norm:
                        dve.wait_ge(s["turned"], KJ * seq + 2)
                        nc.vector.tensor_copy(kT[:, b, 4:8, :].rearrange("p c k -> p (c k)"),
                                              g.ps[0:DC + 1, 1, 0:LJ]).then_inc(s["kT_kept"], 1)
                    for m in range(M):
                        dve.wait_ge(s["scores"], M * seq + m + 1)
                        nc.vector.tensor_reduce(maxima[:, b, m // KJ, m % KJ:m % KJ + 1], g.ps[0:RG, m % 3, 0:LJ],
                                                AX_X, ALU.max).then_inc(s["max_taken"], 1)
                    dve.wait_ge(s["max_taken"], M * (seq + 1))
                    nc.vector.tensor_reduce(negmax[:, b, :], maxima[:, b, :, :], AX_X, ALU.max, negate=True)\
                        .then_inc(s["negmax"], 1)
                if KQ > DC:
                    for b in range(TB):
                        dve.wait_ge(s["row"], TB * i + b + 1)
                        nc.vector.tensor_tensor(qa[DC:DC + 1, b, :], qa[DC:DC + 1, b, :], g.ps[DC:DC + 1, 7, 0:R],
                                                ALU.add).then_inc(s["row_kept"], 1)
                        if b == 0:
                            invert(nc, g, s, dve, i, 0, inverse, R)
                            dve.wait_ge(s["row"], TB * i + 1)
                else:
                    invert(nc, g, s, dve, i, 0, inverse, R)
                for b in range(TB):
                    if b:
                        invert(nc, g, s, dve, i, 1, inverse, R)
                    dve.wait_ge(s["spread_kept"], TB * i + b + 1)
                    nc.vector.tensor_tensor(oT[0:DC, :, b, :],
                                            g.ps[0:DC, 5 + b, 0:R].rearrange("p (h t) -> p h t", h=H),
                                            spread[:, b, :].rearrange("p (h t) -> p h t", h=H), ALU.mult)\
                        .then_inc(s["normal_o"], 1)
                dve.wait_ge(s["projected"], i + 1)
                nc.vector.tensor_tensor(g.x[:, i, :], g.x[:, i, :], g.ps[0:P, 7, 0:D], ALU.add).then_inc(s["added"], 1)


def invert(nc, g, s, dve, i, b, inverse, R):
    dve.wait_ge(s["mixed"], LC * (TB * i + b + 1))
    nc.vector.reciprocal(inverse[DC:DC + 1, b, :], g.ps[DC:DC + 1, 5 + b, 0:R]).then_inc(s["inverse"], 1)


def plain_cross(layer):
    def sublayer(nc, g, w, sb):
        H, DH = 8, 64
        name, src = f"x{layer}", f"L{layer}_xattn"
        wqT, wo = (sb(f"{name}_{n}", [DH, H, D]) for n in ("wqT", "wo"))
        wkT, wvT = (sb(f"{name}_{n}", [DH, H, DC]) for n in ("wkT", "wvT"))
        bo = sb(f"{name}_bo", [1, D])
        normalize(nc, g, f"{name}_norm", g.x, [
            (wqT[:], w[f"{src}_WqT"].rearrange("(h d) c -> d h c", d=DH)),
            (wkT[:], w[f"{src}_WkT"].rearrange("(h d) c -> d h c", d=DH)),
            (wvT[:], w[f"{src}_WvT"].rearrange("(h d) c -> d h c", d=DH)),
            (wo[:], w[f"{src}_Wo"].rearrange("(h d) c -> d h c", d=DH)), (bo[:], row(w[f"{src}_bo"]))])
        wqk, wvo = sb(f"{name}_wqk", [D, H, DC]), sb(f"{name}_wvo", [DC, H, D])
        with stage(nc, f"{name}_weights", "made", "kept") as (block, s):
            @block.tensor
            def _(pe):
                for h in range(H):
                    last = nc.tensor.matmul(g.ps[:, h // GH, (h % GH) * DC:(h % GH + 1) * DC], wqT[:, h, :],
                                            wkT[:, h, :], start=True, stop=True)
                    if h % GH == GH - 1:
                        last.then_inc(s["made"], 1)
                for h in range(H):
                    last = nc.tensor.matmul(g.ps[0:DC, 2 + h // GH, (h % GH) * D:(h % GH + 1) * D], wvT[:, h, :],
                                            wo[:, h, :], start=True, stop=True)
                    if h % GH == GH - 1:
                        last.then_inc(s["made"], 1)

            @block.scalar
            def _(act):
                for n in range(2):
                    act.wait_ge(s["made"], n + 1)
                    nc.scalar.mul(wqk[:, GH * n:GH * n + GH, :],
                                  g.ps[:, n, 0:GH * DC].rearrange("p (h c) -> p h c", h=GH), DH ** -0.5)\
                        .then_inc(s["kept"], 1)

            @block.vector
            def _(dve):
                for n in range(2):
                    dve.wait_ge(s["made"], 2 + n + 1)
                    nc.vector.tensor_copy(wvo[:, GH * n:GH * n + GH, :],
                                          g.ps[0:DC, 2 + n, :].rearrange("p (h c) -> p h c", h=GH))\
                        .then_inc(s["kept"], 1)
        cross_attend(nc, g, w, sb, name, H, lambda h: wqk[:, h, :], lambda h: wvo[:, h, :], bo[:])
    return sublayer


def normed_cross(nc, g, w, sb):
    name = "x0"
    wk, wv = sb("x0_wk", [DC, D]), sb("x0_wv", [DC, D])
    wkT, wvT = sb("x0_wkT", [D, DC + 1]), sb("x0_wvT", [D, DC + 1])
    wqT, wo = sb("x0_wqT", [D, D]), sb("x0_wo", [D, D])
    g1, b1 = sb("x0_g1", [D, 1]), sb("x0_b1", [D, 1])
    g2, b2 = sb("x0_g2", [D, DC]), sb("x0_b2", [DC, 1])
    cols = sb("x0_cols", [D, 3])
    bo = sb("x0_bo", [1, D])
    normalize(nc, g, "x0_norm", g.x, [
        (wk[:], w["L0_xattn_Wk"]), (wv[:], w["L0_xattn_Wv"]), (wkT[:, 0:DC], w["L0_xattn_WkT"]),
        (wvT[:, 0:DC], w["L0_xattn_WvT"]), (wqT[:], w["L0_xattn_WqT"]), (wo[:], w["L0_xattn_Wo"]),
        (g1[:], column(w["L0_xattn_ln1_g"])), (b1[:], column(w["L0_xattn_ln1_b"])),
        (g2[:], rows(w["L0_xattn_ln2_g"], D)), (b2[:], column(w["L0_xattn_ln2_b"])),
        *[(cols[:, n:n + 1], column(w[f"L0_xattn_{b}"])) for n, b in enumerate(("bq", "bk", "bv"))],
        (bo[:], row(w["L0_xattn_bo"]))], turn=False)
    normalize(nc, g, "x0_norm_again", g.xn, [])
    wqk, wvo, wq_row = sb("x0_wqk", [D, DC + 1]), sb("x0_wvo", [DC + 1, D]), sb("x0_wq_row", [1, DC + 1])
    with stage(nc, "x0_weights", "made", "kept", "steps", "mixed", "mixed_kept") as (block, s):
        @block.tensor
        def _(pe):
            nc.tensor.matmul(g.ps[:, 0, 0:1], wk[:], b2[:], start=True, stop=True)
            nc.tensor.matmul(g.ps[:, 0, 1:2], wv[:], b2[:], start=True, stop=True).then_inc(s["made"], 1)
            pe.wait_ge(s["kept"], 1)
            nc.tensor.matmul(g.ps[:, 1, 0:DC + 1], wqT[:], wkT[:], start=True, stop=True).then_inc(s["mixed"], 1)
            nc.tensor.matmul(g.ps[0:DC + 1, 2, 0:D], wvT[:], wo[:], start=True, stop=True).then_inc(s["mixed"], 1)
            pe.wait_ge(s["mixed_kept"], 1)
            nc.tensor.matmul(g.ps[0:1, 3, 0:DC + 1], cols[:, 0:1], wkT[:], start=True, stop=False)
            nc.tensor.matmul(g.ps[0:1, 3, 0:DC + 1], b1[:], wqk[:], start=False, stop=True).then_inc(s["mixed"], 1)

        @block.vector
        def _(dve):
            link = in_order(dve, s["steps"])
            dve.wait_ge(s["made"], 1)
            link(nc.vector.tensor_tensor(wkT[:, DC:DC + 1], g.ps[:, 0, 0:1], cols[:, 1:2], ALU.add))
            link(nc.vector.tensor_tensor(wvT[:, DC:DC + 1], g.ps[:, 0, 1:2], cols[:, 2:3], ALU.add))
            link(nc.vector.tensor_tensor(wkT[:, 0:DC], wkT[:, 0:DC], g2[:], ALU.mult))
            link(nc.vector.tensor_tensor(wvT[:, 0:DC], wvT[:, 0:DC], g2[:], ALU.mult))
            nc.vector.tensor_scalar(wkT[:], wkT[:], D ** -0.5, None, ALU.mult).then_inc(s["kept"], 1)
            dve.wait_ge(s["mixed"], 1)
            nc.vector.tensor_copy(wqk[:], g.ps[:, 1, 0:DC + 1]).then_inc(s["mixed_kept"], 1)
            dve.wait_ge(s["mixed"], 3)
            link(nc.vector.tensor_copy(wq_row[:], g.ps[0:1, 3, 0:DC + 1]))
            link(nc.vector.tensor_scalar(wqk[:], wqk[:], g1[:, 0:1], None, ALU.mult))
            link(nc.vector.tensor_copy(wvo[:], g.ps[0:DC + 1, 2, 0:D]))
    cross_attend(nc, g, w, sb, name, 1, lambda h: wqk[:], lambda h: wvo[:], bo[:], context_norm=True, q_row=wq_row)


def sparse_scores(nc, g, w, sb, name, wqk, mean_T):
    H, KTOP = 4, 32
    R, RG, G, KJ = H * S, P, 2, 3
    LJ = L // KJ
    HG = RG // S
    kT = sb(f"{name}_kT", [DC + 1, TB, LC, LP])
    tok = sb(f"{name}_tok", [LP, TB, LC, DC + 1])
    qa = sb(f"{name}_qa", [DC + 1, TB, R])
    rest, kept = sb(f"{name}_rest", [RG, 2, L]), sb(f"{name}_kept", [RG, 2, L])
    best = sb(f"{name}_best", [RG, 2, KTOP // 8, 8])
    negmax, sums, share = sb(f"{name}_negmax", [RG, 2]), sb(f"{name}_sums", [RG, 2]), sb(f"{name}_share", [RG, 2])
    pick, which = sb(f"{name}_pick", [RG, 2, S]), sb(f"{name}_which", [RG, S])
    weights = sb(f"{name}_weights", [LP, 2, LC, S])
    tick = sb(f"{name}_tick", [1, 8])
    with stage(nc, name, "context_0", "context_1", "set", "q", "q_kept", "scores", "best", "rest", "negmax", "exps",
               "rest_exps", "chosen", "summed", "inverse", "pick", "weights", "weights_kept", "mixed",
               "mixed_kept") as (block, s):
        context = (s["context_0"], s["context_1"])

        @block.sync
        def _(sp):
            def load(i, b):
                n = TB * i + b
                sp.dma_start(kT[0:DC, b, :, :], g.ctxT[n, 0:DC, :, :]).then_inc(context[b], 16)
                sp.dma_start(kT[DC:DC + 1, b, :, :], g.key_bias[n, :, :, :]).then_inc(context[b], 16)
                sp.dma_start(tok[:, b, :, :], g.ctx[n, :, :, :]).then_inc(context[b], 16)

            for b in range(TB):
                load(0, b)
            with sp.Fori(0, T - 1) as i:
                for b in range(TB):
                    sp.wait_ge(s["mixed"], TB * i + b + 1)
                    load(i + 1, b)

        @block.tensor
        def _(pe):
            pe.wait_ge(s["set"], 4)

            def queries(i):
                for h in range(H):
                    last = nc.tensor.matmul(g.ps[0:DC, 6, h * P:(h + 1) * P], wqk(h), g.tile_of(g.xnT, i),
                                            start=True, stop=True)
                last.then_inc(s["q"], 1)

            queries(0)
            with pe.Fori(0, T) as i:
                def scores(u):
                    b, r = u // G, u % G
                    if u == 0:
                        pe.wait_ge(s["q_kept"], i + 1)
                    if r == 0:
                        pe.wait_ge(context[b], 48 * (i + 1))
                    if u >= 2:
                        pe.wait_ge(s["exps"], 4 * i + u - 1)
                    for j in range(KJ):
                        last = nc.tensor.matmul(g.ps[0:RG, 3 * r + j, 0:LJ], qa[:, b, r * RG:(r + 1) * RG],
                                                kT[:, b, j * (LC // KJ):(j + 1) * (LC // KJ), :]
                                                .rearrange("p c k -> p (c k)"), start=True, stop=True)
                    last.then_inc(s["scores"], 1)

                def token_weights(b):
                    for half, chunks in enumerate((range(0, 8), range(8, LC))):
                        if half == 0:
                            pe.wait_ge(s["pick"], 4 * i + 2 * b + 2)
                        for c in chunks:
                            for r in range(G):
                                last = nc.tensor.matmul(g.ps[0:LP, 6 + half, (c % 8) * S:(c % 8) * S + S],
                                                        kept[:, r, c * LP:(c + 1) * LP], pick[:, r, :],
                                                        start=(r == 0), stop=(r == G - 1))
                        last.then_inc(s["weights"], 1)
                    pe.wait_ge(s["weights_kept"], 2 * (TB * i + b) + 2)
                    for c in range(LC):
                        last = nc.tensor.matmul(g.ps[0:DC, 7, 256:256 + S], tok[:, b, c, 0:DC],
                                                weights[:, b, c, :], start=(c == 0), stop=(c == LC - 1))
                    last.then_inc(s["mixed"], 1)

                scores(0)
                scores(1)
                scores(2)
                scores(3)
                token_weights(0)
                pe.wait_ge(s["mixed_kept"], TB * i + 1)
                token_weights(1)
                pe.wait_ge(s["mixed_kept"], TB * i + 2)
                pe.wait_ge(s["exps"], 4 * i + 4)
                for h in range(H):
                    last = nc.tensor.matmul(g.ps[0:DC, 6, h * P:(h + 1) * P], wqk(h), g.next_tile(g.xnT, i),
                                            start=True, stop=True)
                last.then_inc(s["q"], 1)

        @block.gpsimd
        def _(pool):
            nc.gpsimd.memset(qa[DC:DC + 1, :, :], 1.0).then_inc(s["set"], 1)
            pool.wait_ge(s["set"], 1)
            nc.gpsimd.memset(which[:], 0.0).then_inc(s["set"], 1)
            for n in range(HG):
                pool.wait_ge(s["set"], 2 + n)
                nc.gpsimd.affine_select(out=which[:], in_=which[:], compare_op=ALU.not_equal, fill=1.0 / H,
                                        base=-S * n, pattern=[[-1, S]], channel_multiplier=1).then_inc(s["set"], 1)
            with pool.Fori(0, T) as i:
                for u in range(4):
                    n = 4 * i + u
                    pool.wait_ge(s["exps"], n + 1)
                    pool.wait_ge(s["rest_exps"], n + 1)
                    nc.gpsimd.tensor_tensor(kept[:, u % 2, :], kept[:, u % 2, :], rest[:, u % 2, :], ALU.subtract)\
                        .then_inc(s["chosen"], 1)

        @block.scalar
        def _(act):
            with act.Fori(0, T) as i:
                act.wait_ge(s["q"], i + 1)
                nc.scalar.copy(qa[0:DC, :, :].rearrange("p b (h t) -> p h b t", h=H),
                               g.ps[0:DC, 6, 0:H * P].rearrange("p (h b t) -> p h b t", h=H, b=TB))\
                    .then_inc(s["q_kept"], 1)
                for u in range(4):
                    n = 4 * i + u
                    bank = g.ps[0:RG, 3 * (u % 2):3 * (u % 2) + 3, 0:LJ]
                    act.wait_ge(s["negmax"], n + 1)
                    if u >= 2:
                        act.wait_ge(s["weights"], 2 * (TB * i) + 2)
                    act.wait_ge(s["rest"], 4 * n + 4)
                    nc.scalar.activation(kept[:, u % 2, :].rearrange("p (j l) -> p j l", j=KJ), bank, ACT.Exp,
                                         bias=negmax[:, u % 2:u % 2 + 1]).then_inc(s["exps"], 1)
                    nc.scalar.activation(rest[:, u % 2, :], rest[:, u % 2, :], ACT.Exp,
                                         bias=negmax[:, u % 2:u % 2 + 1]).then_inc(s["rest_exps"], 1)

        @block.vector
        def _(dve):
            with dve.Fori(0, T) as i:
                def search(u):
                    n = 4 * i + u
                    dve.wait_ge(s["scores"], n + 1)
                    source = g.ps[0:RG, 3 * (u % 2):3 * (u % 2) + 3, 0:LJ]
                    left = rest[:, u % 2, :].rearrange("p (j l) -> p j l", j=KJ)
                    for k in range(KTOP // 8):
                        m = 4 * n + k
                        if k:
                            dve.wait_ge(s["rest"], m)
                        nc.vector.memset(tick[:, k:k + 1], 0.0)
                        nc.vector.max(best[:, u % 2, k, :], source if k == 0 else left).then_inc(s["best"], 1)
                        dve.wait_ge(s["best"], m + 1)
                        if k == 0:
                            nc.vector.tensor_scalar(negmax[:, u % 2:u % 2 + 1], best[:, u % 2, 0, 0:1], -1.0, None,
                                                    ALU.mult).then_inc(s["negmax"], 1)
                        else:
                            nc.vector.memset(tick[:, 4 + k:5 + k], 0.0)
                        nc.vector.match_replace(left, best[:, u % 2, k, :], source if k == 0 else left, 2 * NEG)\
                            .then_inc(s["rest"], 1)

                def shares(u):
                    n = 4 * i + u
                    dve.wait_ge(s["chosen"], n + 1)
                    nc.vector.tensor_reduce(sums[:, u % 2:u % 2 + 1], kept[:, u % 2, :], AX_X, ALU.add)\
                        .then_inc(s["summed"], 1)
                    dve.wait_ge(s["summed"], n + 1)
                    nc.vector.reciprocal(share[:, u % 2:u % 2 + 1], sums[:, u % 2:u % 2 + 1]).then_inc(s["inverse"], 1)
                    dve.wait_ge(s["inverse"], n + 1)
                    nc.vector.tensor_scalar(pick[:, u % 2, :], which[:], share[:, u % 2:u % 2 + 1], None, ALU.mult)\
                        .then_inc(s["pick"], 1)

                def keep_weights(b):
                    seq = TB * i + b
                    for half, (lo, hi) in enumerate(((0, 8), (8, LC))):
                        dve.wait_ge(s["weights"], 2 * seq + half + 1)
                        nc.vector.tensor_copy(weights[:, b, lo:hi, :],
                                              g.ps[0:LP, 6 + half, 0:(hi - lo) * S].rearrange("p (c t) -> p c t", t=S))\
                            .then_inc(s["weights_kept"], 1)
                    dve.wait_ge(s["mixed"], seq + 1)
                    nc.vector.tensor_copy(g.tile_of(mean_T, i)[0:DC, b * S:(b + 1) * S], g.ps[0:DC, 7, 256:256 + S])\
                        .then_inc(s["mixed_kept"], 1)

                search(0)
                search(1)
                shares(0)
                shares(1)
                search(2)
                search(3)
                keep_weights(0)
                shares(2)
                shares(3)
                keep_weights(1)


def mod_features(nc, g, w, sb):
    H, NS, F = 4, 64, 4 * D
    wqT, wkT = sb("x2_wqT", [32, H, D]), sb("x2_wkT", [32, H, DC])
    wv = sb("x2_wv", [DC, D])
    film = sb("x2_film", [D, 2, 2, D])
    film_b = sb("x2_film_b", [D, 4])
    cols = sb("x2_cols", [D, 6])
    gate = sb("x2_gate", [D, 1])
    w1, w2 = sb("x2_w1", [D, F]), sb("x2_w2", [128, F // 128, D])
    b1, b2 = sb("x2_b1", [128, F // 128]), sb("x2_b2", [1, D])
    ends = sb("x2_ends", [P, 2, D])
    mask_text, mask_keys = sb("x2_mask_text", [D, N], U8), sb("x2_mask_keys", [B, L], U8)
    key_bias = sb("x2_key_bias", [B, L])
    src = "L2_xattn_"
    vectors = ("g_norm_in", "b_norm_in", "g_ffn", "b_ffn", "D_skip", "log_dt")
    normalize(nc, g, "x2_norm", g.x, [
        (mask_keys[:], w["mask_keys"]), (mask_text[:], rows(w["mask_text"], D)),
        (wqT[:], w[src + "WqT"].rearrange("(h d) c -> d h c", h=H)),
        (wkT[:], w[src + "WkT"].rearrange("(h d) c -> d h c", h=H)), (wv[:], w[src + "Wv"]),
        (film[:, 0, :, :], w[src + "W_film_in"].rearrange("d (a e) -> d a e", a=2)),
        (film[:, 1, :, :], w[src + "W_film_out"].rearrange("d (a e) -> d a e", a=2)),
        (film_b[:], w[src + "film_b_cols"]),
        *[(cols[:, n:n + 1], column(w[src + v])) for n, v in enumerate(vectors)],
        (gate[:], rows(w[src + "mod_gate_row"], D)), (w1[:], w[src + "W1"]),
        (w2[:], w[src + "W2"].rearrange("(m p) d -> p m d", p=128)), (b1[:], w[src + "b1_cols"]),
        (b2[:], row(w[src + "b2"])), (ends[:, 0, :], rows(w[src + "g_norm_out"], P)),
        (ends[:, 1, :], rows(w[src + "b_norm_out"], P))])
    meanT = g.keyT
    with ExitStack() as own:
        part = lambda name, shape, dt=F32: own.enter_context(nc.sbuf_tensor(name, shape, dt))
        wqk = part("x2_wqk", [D, H, DC])
        with stage(nc, "x2_weights", "bias", "stored", "made", "kept") as (block, s):
            @block.vector
            def _(dve):
                nc.vector.tensor_scalar(key_bias[:], mask_keys[:], 1.0, -NEG, ALU.subtract, ALU.mult)\
                    .then_inc(s["bias"], 1)

            @block.sync
            def _(sp):
                sp.wait_ge(s["bias"], 1)
                sp.dma_start(g.key_bias.rearrange("b a c k -> b (a c k)"), key_bias[:]).then_inc(s["stored"], 16)
                sp.wait_ge(s["stored"], 16)

            @block.tensor
            def _(pe):
                for h in range(H):
                    last = nc.tensor.matmul(g.ps[:, 0, h * DC:(h + 1) * DC], wqT[:, h, :], wkT[:, h, :], start=True,
                                            stop=True)
                last.then_inc(s["made"], 1)

            @block.scalar
            def _(act):
                act.wait_ge(s["made"], 1)
                nc.scalar.mul(wqk[:], g.ps[:, 0, 0:H * DC].rearrange("p (h c) -> p h c", h=H), 32 ** -0.5)\
                    .then_inc(s["kept"], 1)
        sparse_scores(nc, g, w, part, "x2_top", lambda h: wqk[:, h, :], meanT)

    taps = sb("x2_taps", [D, S])
    with ExitStack() as own:
        part = lambda name, shape, dt=F32: own.enter_context(nc.sbuf_tensor(name, shape, dt))
        state_kernel(nc, g, w, part, cols, taps, NS)

    cT, filmT = sb("x2_cT", [D, N]), sb("x2_filmT", [D, 2, N])
    yT, uT = sb("x2_yT", [D, N]), sb("x2_uT", [D, N])
    with stage(nc, "x2_c", "c", "kept") as (block, s):
        @block.tensor
        def _(pe):
            for b in range(NB):
                nc.tensor.matmul(g.ps[:, b, 0:W], wv[:], meanT[0:DC, b * W:(b + 1) * W], start=True, stop=True)\
                    .then_inc(s["c"], 1)

        @block.vector
        def _(dve):
            for b in range(NB):
                dve.wait_ge(s["c"], b + 1)
                nc.vector.tensor_tensor(cT[:, b * W:(b + 1) * W], g.ps[:, b, 0:W], mask_text[:, b * W:(b + 1) * W],
                                        ALU.mult).then_inc(s["kept"], 1)
    normalize(nc, g, "x2_norm_in", g.xn, [], dst=g.work)
    modulate(nc, g, "x2_in", film[:, 0, :, :], film_b, 0, cT, filmT, gate, g.xnT, uT, cols[:, 0:1], cols[:, 1:2])
    with stage(nc, "x2_conv", "steps") as (block, s):
        @block.vector
        def _(dve):
            link = in_order(dve, s["steps"])
            u3, y3 = (a[:].rearrange("p (b t) -> p b t", t=S) for a in (uT, yT))
            link(nc.vector.tensor_scalar(yT[:], uT[:], taps[:, 0:1], None, ALU.mult))
            for m in range(1, S):
                link(nc.vector.scalar_tensor_tensor(out=y3[:, :, m:S], in0=u3[:, :, 0:S - m],
                                                    scalar=taps[:, m:m + 1], in1=y3[:, :, m:S],
                                                    op0=ALU.mult, op1=ALU.add))
    modulate(nc, g, "x2_out", film[:, 1, :, :], film_b, 2, cT, filmT, gate, yT, uT, None, None)
    add_turned(nc, g, "x2_add", uT, g.xn)
    normalize(nc, g, "x2_norm_ffn", g.xn, [], dst=g.work)
    with stage(nc, "x2_gain", "scaled") as (block, s):
        @block.vector
        def _(dve):
            nc.vector.tensor_scalar(g.xnT[:, 0:N], g.xnT[:, 0:N], cols[:, 2:3], cols[:, 3:4], ALU.mult, ALU.add)\
                .then_inc(s["scaled"], 1)
    jobs = [Expert([(w1[:, m * 128:(m + 1) * 128], b1[:, m:m + 1], None) for m in range(F // 128)],
                   [w2[:, m, :] for m in range(F // 128)], out_bias=b2[:])]
    experts(nc, g, "x2_ffn", sb, jobs, ACT.Gelu, g.xn)
    normalize(nc, g, "x2_norm_out", g.xn, [], turn=False, dst=g.work)
    with stage(nc, "x2_end", "steps") as (block, s):
        @block.vector
        def _(dve):
            link = in_order(dve, s["steps"])
            link(nc.vector.tensor_tensor(g.work[:], g.work[:], under(ends[:, 0, :], T), ALU.mult))
            link(nc.vector.tensor_tensor(g.x[:], g.x[:], under(ends[:, 1, :], T), ALU.add))
            link(nc.vector.tensor_tensor(g.x[:], g.x[:], g.work[:], ALU.add))


def modulate(nc, g, name, weights, film_b, first, cT, filmT, gate, srcT, dstT, gain, shift):
    with stage(nc, name, "film", "film_kept", "steps") as (block, s):
        @block.tensor
        def _(pe):
            for n in range(2 * NB):
                half, b = n // NB, n % NB
                nc.tensor.matmul(g.ps[:, n, 0:W], weights[:, half, :], cT[:, b * W:(b + 1) * W], start=True,
                                 stop=True).then_inc(s["film"], 1)

        @block.scalar
        def _(act):
            for n in range(2 * NB):
                half, b = n // NB, n % NB
                act.wait_ge(s["film"], n + 1)
                nc.scalar.activation(filmT[:, half, b * W:(b + 1) * W], g.ps[:, n, 0:W], ACT.Identity,
                                     bias=film_b[:, first + half:first + half + 1]).then_inc(s["film_kept"], 1)

        @block.vector
        def _(dve):
            link = in_order(dve, s["steps"])
            if gain is not None:
                link(nc.vector.tensor_scalar(dstT[:], srcT[:, 0:N], gain, shift, ALU.mult, ALU.add))
            else:
                link(nc.vector.tensor_copy(dstT[:], srcT[:, 0:N]))
            dve.wait_ge(s["film_kept"], NB)
            link(nc.vector.tensor_scalar(filmT[:, 0, :], filmT[:, 0, :], gate[:, 0:1], 1.0, ALU.mult, ALU.add))
            link(nc.vector.tensor_tensor(dstT[:], dstT[:], filmT[:, 0, :], ALU.mult))
            dve.wait_ge(s["film_kept"], 2 * NB)
            link(nc.vector.scalar_tensor_tensor(out=dstT[:], in0=filmT[:, 1, :], scalar=gate[:, 0:1], in1=dstT[:],
                                                op0=ALU.mult, op1=ALU.add))


def add_turned(nc, g, name, srcT, dst):
    with stage(nc, name, "turned", "added") as (block, s):
        @block.tensor
        def _(pe):
            for b in range(NB):
                for j in range(BT):
                    t = b * BT + j
                    last = nc.tensor.transpose(g.ps[0:P, b, j * D:(j + 1) * D], srcT[:, t * P:(t + 1) * P],
                                               g.ident[:])
                last.then_inc(s["turned"], 1)

        @block.vector
        def _(dve):
            for b in range(NB):
                dve.wait_ge(s["turned"], b + 1)
                part = dst[:, b * BT:(b + 1) * BT, :]
                nc.vector.tensor_tensor(part, part, g.ps[0:P, b, :].rearrange("p (j d) -> p j d", j=BT), ALU.add)\
                    .then_inc(s["added"], 1)


def state_kernel(nc, g, w, sb, cols, taps, NS):
    import math
    A, C = sb("s4_A", [D, 2, NS]), sb("s4_C", [D, 2, NS])
    z, r, t = sb("s4_z", [D, 2, NS]), sb("s4_r", [D, 2, NS]), sb("s4_t", [D, 4, NS])
    wave = sb("s4_wave", [D, 2, NS])
    dC, dt = sb("s4_dC", [D, 2, NS]), sb("s4_dt", [D, 1])
    base = sb("s4_base", [D, 2, NS])
    power = sb("s4_power", [D, 2, S, NS])
    prod = sb("s4_prod", [D, 2, S, NS])
    TWO_PI = 2 * math.pi
    hi = 6.28125
    mid = float(int((TWO_PI - hi) * 2 ** 21)) / 2 ** 21
    lo = TWO_PI - hi - mid
    ROUND = 1.5 * 2.0 ** 23
    with stage(nc, "s4", "loads", "dt", "steps", "angles", "exps", "waves") as (block, s):
        @block.sync
        def _(sp):
            src = "L2_xattn_"
            load_all(sp, s["loads"], [(A[:, 0, :], w[src + "A_re"]), (A[:, 1, :], w[src + "A_im"]),
                                   (C[:, 0, :], w[src + "C_re"]), (C[:, 1, :], w[src + "C_im"])])

        @block.scalar
        def _(act):
            nc.scalar.activation(dt[:], cols[:, 5:6], ACT.Exp).then_inc(s["dt"], 1)
            act.wait_ge(s["angles"], 1)
            nc.scalar.activation(r[:, 0, :], z[:, 0, :], ACT.Exp).then_inc(s["exps"], 1)
            act.wait_ge(s["angles"], 2)
            nc.scalar.activation(wave[:], t[:, 0:2, :], ACT.Sin).then_inc(s["waves"], 1)

        @block.vector
        def _(dve):
            link = in_order(dve, s["steps"])
            dve.wait_ge(s["loads"], 64)
            dve.wait_ge(s["dt"], 1)
            nc.vector.tensor_scalar(z[:], A[:], dt[:, 0:1], None, ALU.mult).then_inc(s["angles"], 1)
            dve.wait_ge(s["angles"], 1)
            link(nc.vector.tensor_copy(t[:, 0, :], z[:, 1, :]))
            link(nc.vector.tensor_scalar(t[:, 2, :], t[:, 0, :], 1.0 / TWO_PI, ROUND, ALU.mult, ALU.add))
            link(nc.vector.tensor_scalar(t[:, 2, :], t[:, 2, :], ROUND, None, ALU.subtract))
            for part in (hi, mid, lo):
                link(nc.vector.scalar_tensor_tensor(out=t[:, 0, :], in0=t[:, 2, :], scalar=-part, in1=t[:, 0, :],
                                                    op0=ALU.mult, op1=ALU.add))
            link(nc.vector.tensor_scalar(t[:, 1, :], t[:, 0, :], math.pi / 2, None, ALU.add))
            link(nc.vector.tensor_scalar(t[:, 3, :], t[:, 1, :], math.pi, -TWO_PI, ALU.is_gt, ALU.mult))
            link(nc.vector.tensor_tensor(t[:, 1, :], t[:, 1, :], t[:, 3, :], ALU.add))
            link(nc.vector.tensor_scalar(t[:, 0:2, :], t[:, 0:2, :], 3.14159250259, -3.14159250259, ALU.min, ALU.max))
            nc.vector.tensor_scalar(z[:, 1, :], z[:, 1, :], 1.0, None, ALU.mult).then_inc(s["angles"], 1)
            dve.wait_ge(s["exps"], 1)
            dve.wait_ge(s["waves"], 1)
            link(nc.vector.tensor_tensor(base[:, 0, :], r[:, 0, :], wave[:, 1, :], ALU.mult))
            link(nc.vector.tensor_tensor(base[:, 1, :], r[:, 0, :], wave[:, 0, :], ALU.mult))

            def times(out, a, b, tmp):
                link(nc.vector.tensor_tensor(out[0], a[0], b[0], ALU.mult))
                link(nc.vector.tensor_tensor(tmp, a[1], b[1], ALU.mult))
                link(nc.vector.tensor_tensor(out[0], out[0], tmp, ALU.subtract))
                link(nc.vector.tensor_tensor(out[1], a[0], b[1], ALU.mult))
                link(nc.vector.tensor_tensor(tmp, a[1], b[0], ALU.mult))
                link(nc.vector.tensor_tensor(out[1], out[1], tmp, ALU.add))

            pair = lambda a: (a[:, 0, :], a[:, 1, :])
            link(nc.vector.tensor_copy(t[:, 0:2, :], base[:]))
            link(nc.vector.tensor_scalar(t[:, 0, :], t[:, 0, :], -1.0, None, ALU.add))
            times(pair(z), pair(C), (t[:, 0, :], t[:, 1, :]), r[:, 1, :])
            link(nc.vector.tensor_tensor(t[:, 0, :], A[:, 0, :], A[:, 0, :], ALU.mult))
            link(nc.vector.tensor_tensor(t[:, 1, :], A[:, 1, :], A[:, 1, :], ALU.mult))
            link(nc.vector.tensor_tensor(t[:, 0, :], t[:, 0, :], t[:, 1, :], ALU.add))
            link(nc.vector.reciprocal(t[:, 0, :], t[:, 0, :]))
            link(nc.vector.tensor_scalar(t[:, 0, :], t[:, 0, :], 2.0, None, ALU.mult))
            link(nc.vector.tensor_tensor(t[:, 2, :], A[:, 0, :], t[:, 0, :], ALU.mult))
            link(nc.vector.tensor_tensor(t[:, 3, :], A[:, 1, :], t[:, 0, :], ALU.mult))
            link(nc.vector.tensor_scalar(t[:, 3, :], t[:, 3, :], -1.0, None, ALU.mult))
            times(pair(dC), pair(z), (t[:, 2, :], t[:, 3, :]), r[:, 1, :])
            link(nc.vector.memset(power[:, 0, 0, :], 1.0))
            link(nc.vector.memset(power[:, 1, 0, :], 0.0))
            n = 1
            while n < S:
                m = min(n, S - n)
                wide = lambda a, k: a[:, k, :].unsqueeze(1).to_broadcast([D, m, NS])
                times((power[:, 0, n:n + m, :], power[:, 1, n:n + m, :]),
                      (power[:, 0, 0:m, :], power[:, 1, 0:m, :]), (wide(base, 0), wide(base, 1)),
                      prod[:, 0, 0:m, :])
                if n + m < S:
                    times(pair(z), pair(base), pair(base), r[:, 1, :])
                    link(nc.vector.tensor_copy(base[:], z[:]))
                n += m
            for k in range(2):
                link(nc.vector.tensor_tensor(prod[:, k, :, :], power[:, k, :, :],
                                             dC[:, k, :].unsqueeze(1).to_broadcast([D, S, NS]), ALU.mult))
            link(nc.vector.tensor_tensor(prod[:, 0, :, :], prod[:, 0, :, :], prod[:, 1, :, :], ALU.subtract))
            link(nc.vector.tensor_reduce(taps[:], prod[:, 0, :, :], AX_X, ALU.add))
            link(nc.vector.tensor_tensor(taps[:, 0:1], taps[:, 0:1], cols[:, 4:5], ALU.add))


SUBLAYERS = [wide_attention, normed_cross, shared_and_routed, biased_attention, plain_cross(1), capped_experts,
             scaled_attention, mod_features, small_experts, rotary_attention, plain_cross(3), adapted_experts]



def build(nc, w, out):
    with ExitStack() as ctx:
        def sb(name, shape, dt=F32):
            return ctx.enter_context(nc.sbuf_tensor(name, shape, dt))

        g = Chip()
        g.x = sb("x", [P, T, D])
        g.xn = sb("xn", [P, T, D])
        g.work, g.square = sb("work", [P, T, D]), sb("square", [P, T, D])
        g.xnT, g.workT, g.keyT = (sb(n, [D, N + P]) for n in ("xnT", "workT", "keyT"))
        g.stat = sb("stat", [P, 4, T])
        g.minus_half = sb("minus_half", [P, T])
        g.ident, g.ones = sb("ident", [128, 128]), sb("ones", [128, 128])
        g.last_row = sb("last_row", [128, DC + 1])
        g.mask_any, g.mask_q, g.mask_k = (sb(n, [P, BT, P]) for n in ("mask_any", "mask_q", "mask_k"))
        g.ps = ctx.enter_context(nc.psum_tensor("ps", [128, 8, 512], F32))
        g.next_tile = lambda a, i: a[:, 0:N + P].rearrange("p (t c) -> p t c", c=P)[:, i + 1, :]
        g.ctx, g.ctxT, g.key_bias = w["ctx"], w["ctxT"], w["key_bias"]
        g.tile_of = lambda a, i: a[:, 0:N].rearrange("p (t c) -> p t c", c=P)[:, i, :]
        g.block_of = lambda a, i: a[:, 0:N].rearrange("p (b c) -> p b c", c=W)[:, i, :]
        g.tiles_of = lambda a, i: a[:].rearrange("p (b j) d -> p b j d", j=BT)[:, i, :, :]
        g.block_gate = lambda a, i: a.rearrange("p (b j) -> p b j", j=BT)[:, i, :]
        build_constants(nc, g)
        with stage(nc, "start", "x_in", "set") as (block, s):
            @block.sync
            def _(sp):
                load_all(sp, s["x_in"], [(g.x[:], w["x"].rearrange("(t a) s d -> (a s) t d", a=TB))])

            @block.gpsimd
            def _(pool):
                nc.gpsimd.memset(g.minus_half[:], -0.5).then_inc(s["set"], 1)
                for padded in (g.xnT, g.workT, g.keyT):
                    nc.gpsimd.memset(padded[:, N:N + P], 0.0).then_inc(s["set"], 1)
        for sub in SUBLAYERS[FIRST_SUBLAYER:LAST_SUBLAYER]:
            with ExitStack() as own:
                sub(nc, g, w, lambda name, shape, dt=F32: own.enter_context(nc.sbuf_tensor(name, shape, dt)))
        with stage(nc, "end", "x_out") as (block, s):
            @block.sync
            def _(sp):
                sp.dma_start(out.rearrange("(t a) s d -> (a s) t d", a=TB), g.x[:]).then_inc(s["x_out"], 16)
                sp.wait_ge(s["x_out"], 16)


def laid_out(inputs):
    import numpy as np
    w = dict(inputs)
    wqkv = w.pop("L1_attn_Wqkv")
    w["L1_attn_WqT"] = wqkv[:, 0:D].T
    w["L1_attn_Wkv"] = wqkv[:, D:3 * D]
    dirs = w.pop("L1_attn_head_dirs")
    padded = np.zeros((8, 16), dirs.dtype)
    padded[:, 0:3] = dirs
    w["L1_attn_head_dirs_row"] = padded.reshape(-1)
    w["L1_attn_head_scales_row"] = np.repeat(w.pop("L1_attn_head_scales"), 16)
    w["L2_attn_bo4"] = np.tile(w.pop("L2_attn_bo"), 4)
    w["L3_attn_bo4"] = np.tile(w.pop("L3_attn_bo"), 4)
    for name in ("wqr", "wkr", "bqr", "bkr"):
        w[f"L3_attn_{name}_swapped"] = np.roll(w[f"L3_attn_{name}"], D // 2, axis=-1)
    inv = np.float32(1.0) / np.float32(10000.0) ** (np.arange(0, D, 2, dtype=np.float32) / np.float32(D))
    angle = (np.arange(S, dtype=np.float32)[:, None] * inv[None, :]).astype(np.float32)
    angle = np.tile(np.concatenate([angle, angle], axis=1).T, (1, TB))
    sign = np.where(np.arange(D) < D // 2, -1.0, 1.0)[:, None]
    w["rotary"] = np.stack([np.cos(angle), np.sin(angle) * sign]).astype(np.float32)
    w["L0_ffn_centroidsT"] = w.pop("L0_ffn_centroids").T
    w["L0_ffn_WfcT"] = np.concatenate([w.pop("L0_ffn_Wfc_sh"), w.pop("L0_ffn_Wfc_r")]).transpose(0, 2, 1)
    w["L0_ffn_WprojT"] = np.concatenate([w.pop("L0_ffn_Wproj_sh"), w.pop("L0_ffn_Wproj_r")]).transpose(0, 2, 1)
    w["L1_ffn_rb1_cols"] = w.pop("L1_ffn_rb1").reshape(4, 128).T
    w["L1_ffn_eb1_cols"] = w.pop("L1_ffn_eb1").reshape(8, 4, 128).transpose(2, 0, 1)
    w["L2_ffn_b1_cols"] = w.pop("L2_ffn_b1").reshape(4, 128).T
    for name in ("Wg", "Wi", "Wo"):
        w[f"L3_ffn_{name}T"] = w.pop(f"L3_ffn_{name}").T
    w["L3_ffn_AT"] = w.pop("L3_ffn_A").reshape(16, D).T
    w["L3_ffn_BT"] = w.pop("L3_ffn_B").transpose(2, 0, 1).reshape(4, 4 * 512)
    ctx = w.pop("ctx_768").reshape(B, LP, LC, DC)
    w["ctx"] = np.concatenate([ctx, np.ones((B, LP, LC, 1), ctx.dtype)], axis=3)
    w["ctxT"] = w["ctx"].transpose(0, 3, 2, 1)
    w["mask_keys"] = w.pop("mask_BxS2_bf1").reshape(B, LP, LC).transpose(0, 2, 1).reshape(B, L).view(np.uint8)
    w["mask_text"] = w.pop("mask_BxS_bf1").reshape(-1).view(np.uint8)
    for name in ("Wq", "Wk"):
        w[f"L2_xattn_{name}T"] = w.pop(f"L2_xattn_{name}").T
    w["L2_xattn_film_b_cols"] = np.concatenate(
        [w.pop("L2_xattn_b_film_in").reshape(2, D), w.pop("L2_xattn_b_film_out").reshape(2, D)]).T
    w["L2_xattn_b1_cols"] = w.pop("L2_xattn_b1").reshape(4, 128).T
    w["L2_xattn_mod_gate_row"] = w.pop("L2_xattn_mod_gate").reshape(1)
    for layer in (1, 3):
        for name in ("Wq", "Wk", "Wv"):
            w[f"L{layer}_xattn_{name}T"] = w.pop(f"L{layer}_xattn_{name}").T
    w["L0_xattn_WqT"] = w.pop("L0_xattn_Wq").T
    for name in ("Wk", "Wv"):
        w[f"L0_xattn_{name}T"] = w[f"L0_xattn_{name}"].T
    for unused in ("L3_attn_wq", "L3_attn_bq", "L3_attn_wqc", "L3_attn_bqc", "L3_attn_wkc", "L3_attn_bkc"
):
        w.pop(unused)
    return {k: np.ascontiguousarray(v) for k, v in w.items()}


def kernel(**inputs):
    import numpy as np
    import concourse.bacc as bacc
    from concourse.bass_utils import run_bass_kernel_spmd as run

    nc = bacc.Bacc("TRN2", target_bir_lowering=False, num_devices=1)
    arrays, w = {}, {}
    for name, a in laid_out(inputs).items():
        arrays[f"in_{name}"] = a
        w[name] = nc.dram_tensor(f"in_{name}", a.shape, mybir.dt.from_np(a.dtype), kind="ExternalInput").ap()
    w["key_bias"] = nc.dram_tensor("key_bias", (B, 1, LC, LP), F32, kind="Internal").ap()
    out = nc.dram_tensor("out_x", (B, S, D), F32, kind="ExternalOutput").ap()
    build(nc, w, out)
    result = run(nc, [arrays], core_ids=[0])
    return result.results[0]["out_x"]
```

```python
from contextlib import ExitStack, contextmanager

import concourse.bass as bass
from concourse import mybir

FIRST_SUBLAYER, LAST_SUBLAYER = 0, 12

F32 = mybir.dt.float32
BF16 = mybir.dt.bfloat16
F32R = mybir.dt.float32r
U8 = mybir.dt.uint8
ALU = mybir.AluOpType
ACT = mybir.ActivationFunctionType
AX_X = mybir.AxisListType.X

B, S, D = 32, 56, 128
TB = 2
P = TB * S
T = B // TB
N = T * P
BT = 4
NB = T // BT
W = BT * P
L, DC = 1500, 96
LC, LP = 12, 125
EPS = 1e-5
NEG = -1e30


class Chip:
    pass


class Routing:

    def __init__(self, sb, name, E):
        self.logits, self.kept_logits = sb(f"{name}_logits", [P, T, E]), sb(f"{name}_kept_logits", [P, T, E])
        self.first, self.second = sb(f"{name}_first", [P, T, E]), sb(f"{name}_second", [P, T, E])
        self.rank, self.combine = sb(f"{name}_rank", [P, T, E]), sb(f"{name}_combine", [P, T, E])
        self.score, self.bias = sb(f"{name}_score", [P, T, E]), sb(f"{name}_bias", [P, E])
        self.top, self.lead = sb(f"{name}_top", [P, 2, T]), sb(f"{name}_lead", [P, T])
        self.a, self.b = sb(f"{name}_a", [P, T]), sb(f"{name}_b", [P, T])


class Expert:

    def __init__(self, up, down, out_bias=None, gate=None):
        self.up, self.down, self.out_bias, self.gate = up, down, out_bias, gate


@contextmanager
def stage(nc, name, *signals):
    sems = {s: nc.alloc_semaphore(f"{name}_{s}") for s in signals}
    with nc.Block(no_gpsimd_drain=True) as block:
        yield block, sems
    nc.clear_and_free_semaphores(list(sems.values()))
    nc.all_engine_barrier()


def in_order(eng, sem):
    count = [0]

    def link(ins):
        count[0] += 1
        ins.then_inc(sem, 1)
        eng.wait_ge(sem, count[0])

    return link


def over(ap, n):
    return ap.unsqueeze(2).to_broadcast([ap.shape[0], ap.shape[1], n])


def under(ap, n):
    return ap.unsqueeze(1).to_broadcast([ap.shape[0], n, ap.shape[1]])


def column(ap):
    return ap.rearrange("(p a) -> p a", a=1)


def row(ap):
    return ap.rearrange("(a n) -> a n", a=1)


def rows(ap, p):
    return row(ap).to_broadcast([p, ap.shape[0]])


def build_constants(nc, g):
    with stage(nc, "const", "filled", "cut", "kept") as (block, s):
        @block.gpsimd
        def _(pool):
            link = in_order(pool, s["cut"])
            nc.gpsimd.memset(g.ones[:], 1.0).then_inc(s["filled"], 1)
            link(nc.gpsimd.memset(g.ident[:], 0.0))
            link(nc.gpsimd.affine_select(out=g.ident[:], in_=g.ident[:], compare_op=ALU.not_equal, fill=1.0,
                                         base=0, pattern=[[-1, 128]], channel_multiplier=1))
            link(nc.gpsimd.tensor_copy(g.ident_b[:], g.ident[:]))
            for mask in (g.mask_any, g.mask_q):
                link(nc.gpsimd.memset(mask[:], 0.0))
                link(nc.gpsimd.affine_select(out=mask[:, :, 0:S], in_=mask[:, :, 0:S], compare_op=ALU.is_ge,
                                             fill=NEG, base=S - 1, pattern=[[0, BT], [0, S]],
                                             channel_multiplier=-1))
                link(nc.gpsimd.affine_select(out=mask[:, :, S:P], in_=mask[:, :, S:P], compare_op=ALU.is_ge,
                                             fill=NEG, base=-S, pattern=[[0, BT], [0, S]],
                                             channel_multiplier=1))
            link(nc.gpsimd.affine_select(out=g.mask_q[:], in_=g.mask_q[:], compare_op=ALU.is_ge, fill=NEG,
                                         base=0, pattern=[[0, BT], [-1, P]], channel_multiplier=1))


def load_all(eng, arrived, loads):
    for dst, src in loads:
        eng.dma_start(dst, src).then_inc(arrived, 16)
    if loads:
        eng.wait_ge(arrived, 16 * len(loads))


def normalize(nc, g, name, src, loads=(), turn=True, dst=None):
    dst = g.xn if dst is None else dst
    half = len(loads) // 2
    halves = [slice(0, T // 2), slice(T // 2, T)]
    with stage(nc, name, "load_a", "load_b", "sum", "mean", "centred", "squared", "spread", "variance", "rstd",
               "normal", "turned", "kept") as (block, s):
        @block.sync
        def _(sp):
            load_all(sp, s["load_a"], loads[half:])

        @block.vector
        def _(dve):
            for n, h in enumerate(halves):
                nc.vector.tensor_reduce(g.stat[:, 0, h], src[:, h, :], AX_X, ALU.add).then_inc(s["sum"], 1)
                dve.wait_ge(s["sum"], n + 1)
                nc.vector.tensor_scalar(g.stat[:, 1, h], g.stat[:, 0, h], -1.0 / D, None, ALU.mult)\
                    .then_inc(s["mean"], 1)
                dve.wait_ge(s["mean"], n + 1)
                nc.vector.tensor_tensor(dst[:, h, :], src[:, h, :], over(g.stat[:, 1, h], D), ALU.add)\
                    .then_inc(s["centred"], 1)
            for n, h in enumerate(halves):
                dve.wait_ge(s["squared"], n + 1)
                nc.vector.tensor_reduce(g.stat[:, 2, h], g.square[:, h, :], AX_X, ALU.add).then_inc(s["spread"], 1)
            for n, h in enumerate(halves):
                dve.wait_ge(s["rstd"], n + 1)
                nc.vector.tensor_tensor(dst[:, h, :], dst[:, h, :], over(g.stat[:, 3, h], D), ALU.mult)\
                    .then_inc(s["normal"], 1)
            if turn:
                for b in range(1, NB, 2):
                    dve.wait_ge(s["turned"], b + 1)
                    nc.vector.tensor_copy(g.xnT[:, b * W:(b + 1) * W], g.ps[:, b, 0:W]).then_inc(s["kept"], 1)

        @block.gpsimd
        def _(pool):
            for n, h in enumerate(halves):
                pool.wait_ge(s["spread"], n + 1)
                nc.gpsimd.tensor_scalar(g.stat[:, 2, h], g.stat[:, 2, h], 1.0 / D, EPS, ALU.mult, ALU.add)\
                    .then_inc(s["variance"], 1)
                pool.wait_ge(s["variance"], n + 1)
                nc.gpsimd.tensor_tensor(g.stat[:, 3, h], g.stat[:, 2, h], g.minus_half[:, h], ALU.pow)\
                    .then_inc(s["rstd"], 1)

        @block.scalar
        def _(act):
            for dst_, src_ in loads[:half]:
                act.dma_start(dst_, src_).then_inc(s["load_b"], 16)
            for n, h in enumerate(halves):
                act.wait_ge(s["centred"], n + 1)
                nc.scalar.activation(g.square[:, h, :], dst[:, h, :], ACT.Square).then_inc(s["squared"], 1)
            if turn:
                for b in range(0, NB, 2):
                    act.wait_ge(s["turned"], b + 1)
                    nc.scalar.copy(g.xnT[:, b * W:(b + 1) * W], g.ps[:, b, 0:W]).then_inc(s["kept"], 1)
            if half:
                act.wait_ge(s["load_b"], 16 * half)

        @block.tensor
        def _(pe):
            if turn:
                pe.wait_ge(s["normal"], 1)
                turn_tiles(nc, g, dst, s["turned"], 0, NB // 2)
                pe.wait_ge(s["normal"], 2)
                turn_tiles(nc, g, dst, s["turned"], NB // 2, NB)


def turn_tiles(nc, g, src, turned, first=0, last_block=None):
    for b in range(first, NB if last_block is None else last_block):
        for j in range(BT):
            last = nc.tensor.transpose(g.ps[:, b, j * P:(j + 1) * P], src[:, b * BT + j, :], g.ident[0:P, 0:P])
        last.then_inc(turned, 1)


def turn_and_project(nc, g, name, src, wo, bo4, add_to):
    with stage(nc, name, "turned", "kept", "projected", "added") as (block, s):
        @block.tensor
        def _(pe):
            turn_tiles(nc, g, src, s["turned"])
            for b in range(NB):
                pe.wait_ge(s["kept"], b + 1)
                bank = g.ps[0:P, NB + b, :]
                if bo4 is not None:
                    nc.tensor.matmul(bank, g.ones[0:1, 0:P], bo4[0:1, :], start=True, stop=False,
                                     skip_group_check=True)
                for j in range(BT):
                    t = b * BT + j
                    last = nc.tensor.matmul(bank[:, j * D:(j + 1) * D], g.workT[:, t * P:(t + 1) * P], wo[:],
                                            start=bo4 is None, stop=True, skip_group_check=True)
                last.then_inc(s["projected"], 1)

        @block.scalar
        def _(act):
            for b in range(NB):
                act.wait_ge(s["turned"], b + 1)
                nc.scalar.copy(g.workT[:, b * W:(b + 1) * W], g.ps[:, b, 0:W]).then_inc(s["kept"], 1)

        @block.vector
        def _(dve):
            for b in range(NB):
                dve.wait_ge(s["projected"], b + 1)
                part = add_to[:, b * BT:(b + 1) * BT, :]
                nc.vector.tensor_tensor(part, part, g.ps[0:P, NB + b, :].rearrange("p (j d) -> p j d", j=BT),
                                        ALU.add).then_inc(s["added"], 1)


GH = 4


ATTEND = ("scores", "max_taken", "shifted", "exps", "turned_probs", "probs", "mixed", "inverse", "mixed_kept")
LAG = 3


def over_pairs(eng, tile):
    def pair(j):
        for u in range(2):
            tile(2 * j + u, u)

    pair(0)
    with eng.Fori(1, T // 2 - 1) as j:
        pair(j)
    pair(T // 2 - 1)


def wait_from(eng, sem, value):
    if not (isinstance(value, int) and value < 1):
        eng.wait_ge(sem, value)


class Attention:

    def __init__(self, nc, g, s, sb, name, H, dv, mask, head, query, key, value, out):
        self.nc, self.g, self.s = nc, g, s
        self.groups, self.dv, self.mask = H // GH, dv, mask
        self.head, self.query, self.key, self.value, self.out = head, query, key, value, out
        self.expo, self.probs = sb(f"{name}_expo", [P, 2, GH, P]), sb(f"{name}_probs", [P, 2, GH, P])
        self.negmax, self.over_sum = sb(f"{name}_negmax", [P, 2, GH]), sb(f"{name}_over_sum", [P, 2, GH])

    def before(self, t, u, k, lag):
        d, kk = divmod(k - lag, self.groups)
        if isinstance(t, int) and not 0 <= t + d < T:
            return None
        return t + d, (u + d) % 2, kk, self.groups * (t + d) + kk

    def tensor(self, pe, t, u, k, before_mix=None):
        nc, g, s = self.nc, self.g, self.s
        at = self.before(t, u, k, 0)
        if at:
            _, _, _, n = at
            wait_from(pe, s["shifted"], n - 1)
            bank = g.ps[0:P, k % 2, 0:W]
            nc.tensor.matmul(bank, g.ident_b[0:P, 0:P], self.mask[:].rearrange("p a b -> p (a b)"),
                             start=True, stop=False, skip_group_check=True)
            for h in range(GH):
                last = nc.tensor.matmul(bank[:, h * P:(h + 1) * P], self.query(u, self.head(k, h)),
                                        self.key(t, u, self.head(k, h)), start=False, stop=(h == GH - 1),
                                        skip_group_check=True)
            last.then_inc(s["scores"], 1)
        at = self.before(t, u, k, LAG - 1)
        if at:
            _, _, kk, n = at
            pe.wait_ge(s["exps"], n + 1)
            wait_from(pe, s["probs"], n - 1)
            for h in range(GH):
                last = nc.tensor.transpose(g.ps[0:P, 2 + kk % 2, h * P:(h + 1) * P], self.expo[:, kk % 2, h, :],
                                           g.ident[0:P, 0:P])
            last.then_inc(s["turned_probs"], 1)
        if before_mix is not None:
            before_mix()
        at = self.before(t, u, k, LAG)
        if at:
            tt, uu, kk, n = at
            pe.wait_ge(s["probs"], n + 1)
            wait_from(pe, s["mixed_kept"], n - 1)
            bank = g.ps[0:P, 4 + kk % 2, :]
            for h in range(GH):
                last = nc.tensor.matmul(bank[:, h * self.dv:(h + 1) * self.dv], self.probs[:, kk % 2, h, :],
                                        self.value(tt, uu, self.head(kk, h)), start=True, stop=True,
                                        skip_group_check=True)
            last.then_inc(s["mixed"], 1)

    def scalar(self, act, t, u, k):
        nc, g, s = self.nc, self.g, self.s
        at = self.before(t, u, k, 0)
        if at:
            _, _, _, n = at
            act.wait_ge(s["shifted"], n + 1)
            part = self.expo[:, k % 2, :, :]
            nc.scalar.activation(part, part, ACT.Exp).then_inc(s["exps"], 1)
        at = self.before(t, u, k, LAG - 1)
        if at:
            _, _, kk, n = at
            act.wait_ge(s["turned_probs"], n + 1)
            wait_from(act, s["mixed"], n - 1)
            nc.scalar.copy(self.probs[:, kk % 2, :, :].rearrange("p h q -> p (h q)"), g.ps[0:P, 2 + kk % 2, 0:W])\
                .then_inc(s["probs"], 1)

    def vector(self, dve, t, u, k):
        nc, g, s = self.nc, self.g, self.s
        at = self.before(t, u, k, 0)
        if at:
            _, _, _, n = at
            dve.wait_ge(s["scores"], n + 1)
            bank = g.ps[0:P, k % 2, 0:W].rearrange("p (h q) -> p h q", h=GH)
            nc.vector.tensor_reduce(self.negmax[:, k % 2, :], bank, AX_X, ALU.max, negate=True)\
                .then_inc(s["max_taken"], 1)
            dve.wait_ge(s["max_taken"], n + 1)
            wait_from(dve, s["turned_probs"], n - 1)
            nc.vector.tensor_tensor(self.expo[:, k % 2, :, :], bank, over(self.negmax[:, k % 2, :], P), ALU.add)\
                .then_inc(s["shifted"], 1)
        at = self.before(t, u, k, LAG)
        if at:
            tt, uu, kk, n = at
            dve.wait_ge(s["mixed"], n + 1)
            bank = g.ps[0:P, 4 + kk % 2, 0:GH * self.dv].rearrange("p (h d) -> p h d", h=GH)
            nc.vector.reciprocal(self.over_sum[:, kk % 2, :], bank[:, :, self.dv - 1]).then_inc(s["inverse"], 1)
            dve.wait_ge(s["inverse"], n + 1)
            nc.vector.tensor_tensor(self.out(tt, kk), bank[:, :, 0:self.dv - 1],
                                    over(self.over_sum[:, kk % 2, :], self.dv - 1), ALU.mult)\
                .then_inc(s["mixed_kept"], 1)

    def drain(self, slot, eng):
        for e in range(LAG):
            slot(eng, T + e // self.groups, (e // self.groups) % 2, e % self.groups)


def wide_attention(nc, g, w, sb):
    H, DH = 16, 64
    INNER = H * DH
    C = INNER // 128
    groups = H // GH
    wq, wk, wv = (sb(f"a0_{n}", [D, INNER]) for n in ("wq", "wk", "wv"))
    wo = sb("a0_wo", [128, C, D])
    bo = sb("a0_bo", [1, D])
    normalize(nc, g, "a0_norm", g.x, [
        (wq[:], w["L0_attn_Wq"]), (wk[:], w["L0_attn_Wk"]), (wv[:], w["L0_attn_Wv"]),
        (wo[:], w["L0_attn_Wo"].rearrange("(c p) d -> p c d", p=128)), (bo[:], row(w["L0_attn_bo"]))])
    xt = sb("a0_xt", [D, P])
    qT, kT = (sb(f"a0_{n}", [128, 2, C, P]) for n in ("qT", "kT"))
    v = sb("a0_v", [P, 2, H, DH + 1])
    on = sb("a0_on", [P, INNER])
    onT = sb("a0_onT", [128, C, P])
    rows_of = lambda h: slice(DH * (h % 2), DH * (h % 2) + DH)
    with stage(nc, "a0", "ones_set", "xt", "q", "k", "v", "q_kept", "k_kept", "v_kept", "on_turned", "onT_kept",
               "projected", "added", *ATTEND) as (block, s):
        a = Attention(
            nc, g, s, sb, "a0", H, DH + 1, g.mask_q,
            head=lambda k, h: 8 * (k // 2) + 2 * h + k % 2,
            query=lambda u, h: qT[rows_of(h), u, h // 2, :],
            key=lambda t, u, h: kT[rows_of(h), u, h // 2, :],
            value=lambda t, u, h: v[:, u, h, :],
            out=lambda t, k: on[:, (k // 2) * 2 * GH * DH:(k // 2 + 1) * 2 * GH * DH].rearrange(
                "p (h two d) -> p two h d", two=2, d=DH)[:, k % 2, :, :])
        more = lambda t: not (isinstance(t, int) and t >= T)

        @block.tensor
        def _(pe):
            def features(wx, made):
                for c in range(C):
                    last = nc.tensor.matmul(g.ps[:, 6 + c // 4, (c % 4) * P:(c % 4) * P + P],
                                            wx[:, c * 128:(c + 1) * 128], xt[:], start=True, stop=True)
                    if c % 4 == 3:
                        last.then_inc(s[made], 1)

            def values(t):
                pe.wait_ge(s["k_kept"], 2 * t + 2)
                for c in range(2):
                    nc.tensor.matmul(g.ps[0:P, 6 + c, :], xt[:], wv[:, c * 512:(c + 1) * 512],
                                     start=True, stop=True).then_inc(s["v"], 1)

            def turn_out(t):
                pe.wait_ge(s["mixed_kept"], groups * t + groups)
                for c in range(C):
                    last = nc.tensor.transpose(g.ps[:, 6 + c // 4, (c % 4) * P:(c % 4) * P + P],
                                               on[:, c * 128:(c + 1) * 128], g.ident[0:P, 0:P])
                    if c % 4 == 3:
                        last.then_inc(s["on_turned"], 1)

            def project(t):
                pe.wait_ge(s["onT_kept"], 2 * t + 2)
                nc.tensor.matmul(g.ps[0:P, 6, 0:D], g.ones[0:1, 0:P], bo[:], start=True, stop=False)
                for c in range(C):
                    last = nc.tensor.matmul(g.ps[0:P, 6, 0:D], onT[:, c, :], wo[:, c, :], start=False,
                                            stop=(c == C - 1))
                last.then_inc(s["projected"], 1)

            def tile(t, u):
                def finish_before():
                    if not (isinstance(t, int) and t < 2):
                        project(t - 2)

                def turn_before():
                    if more(t + 1):
                        pe.wait_ge(s["v_kept"], 2 * t + 4)
                    if not (isinstance(t, int) and t < 1):
                        turn_out(t - 1)

                a.tensor(pe, t, u, 0, finish_before)
                if more(t + 1):
                    wait_from(pe, s["added"], t - 1)
                    pe.wait_ge(s["xt"], t + 2)
                    features(wq, "q")
                a.tensor(pe, t, u, 1)
                if more(t + 1):
                    pe.wait_ge(s["q_kept"], 2 * t + 4)
                    features(wk, "k")
                a.tensor(pe, t, u, 2)
                if more(t + 1):
                    values(t + 1)
                a.tensor(pe, t, u, 3, turn_before)

            pe.wait_ge(s["ones_set"], 1)
            pe.wait_ge(s["xt"], 1)
            features(wq, "q")
            pe.wait_ge(s["q_kept"], 2)
            features(wk, "k")
            values(0)
            pe.wait_ge(s["v_kept"], 2)
            over_pairs(pe, tile)
            project(T - 2)
            a.drain(a.tensor, pe)
            pe.wait_ge(s["added"], T - 1)
            turn_out(T - 1)
            project(T - 1)

        @block.gpsimd
        def _(pool):
            nc.gpsimd.memset(v[:, :, :, DH:DH + 1], 1.0).then_inc(s["ones_set"], 1)

        @block.scalar
        def _(act):
            def keep_queries(t, u):
                for c in range(2):
                    act.wait_ge(s["q"], 2 * t + c + 1)
                    nc.scalar.mul(qT[:, u, 4 * c:4 * c + 4, :],
                                  g.ps[:, 6 + c, 0:W].rearrange("p (c t) -> p c t", c=4), DH ** -0.5)\
                        .then_inc(s["q_kept"], 1)

            def keep_values(t, u):
                act.wait_ge(s["v"], 2 * t + 1)
                nc.scalar.copy(v[:, u, 0:H // 2, 0:DH], g.ps[0:P, 6, :].rearrange("p (h d) -> p h d", d=DH))\
                    .then_inc(s["v_kept"], 1)
                act.wait_ge(s["v"], 2 * t + 2)

            def keep_turned(t):
                for c in range(2):
                    act.wait_ge(s["on_turned"], 2 * t + c + 1)
                    nc.scalar.copy(onT[:, 4 * c:4 * c + 4, :],
                                   g.ps[:, 6 + c, 0:W].rearrange("p (c t) -> p c t", c=4)).then_inc(s["onT_kept"], 1)

            def tile(t, u):
                a.scalar(act, t, u, 0)
                if more(t + 1):
                    keep_queries(t + 1, 1 - u)
                a.scalar(act, t, u, 1)
                a.scalar(act, t, u, 2)
                if more(t + 1):
                    keep_values(t + 1, 1 - u)
                    nc.scalar.copy(xt[:], g.next_tile(g.xnT, t + 1)).then_inc(s["xt"], 1)
                a.scalar(act, t, u, 3)
                if not (isinstance(t, int) and t < 1):
                    keep_turned(t - 1)

            nc.scalar.copy(xt[:], g.xnT[:, 0:P]).then_inc(s["xt"], 1)
            keep_queries(0, 0)
            act.wait_ge(s["ones_set"], 1)
            keep_values(0, 0)
            nc.scalar.copy(xt[:], g.xnT[:, P:2 * P]).then_inc(s["xt"], 1)
            over_pairs(act, tile)
            a.drain(a.scalar, act)
            keep_turned(T - 1)

        @block.vector
        def _(dve):
            def keep_keys(t, u):
                for c in range(2):
                    dve.wait_ge(s["k"], 2 * t + c + 1)
                    nc.vector.tensor_copy(kT[:, u, 4 * c:4 * c + 4, :],
                                          g.ps[:, 6 + c, 0:W].rearrange("p (c t) -> p c t", c=4))\
                        .then_inc(s["k_kept"], 1)

            def keep_values(t, u):
                dve.wait_ge(s["v"], 2 * t + 2)
                nc.vector.tensor_copy(v[:, u, H // 2:H, 0:DH], g.ps[0:P, 7, :].rearrange("p (h d) -> p h d", d=DH))\
                    .then_inc(s["v_kept"], 1)

            def add(t):
                dve.wait_ge(s["projected"], t + 1)
                nc.vector.tensor_tensor(g.x[:, t, :], g.x[:, t, :], g.ps[0:P, 6, 0:D], ALU.add)\
                    .then_inc(s["added"], 1)

            def tile(t, u):
                if not (isinstance(t, int) and t < 2):
                    add(t - 2)
                a.vector(dve, t, u, 0)
                a.vector(dve, t, u, 1)
                if more(t + 1):
                    keep_keys(t + 1, 1 - u)
                a.vector(dve, t, u, 2)
                if more(t + 1):
                    keep_values(t + 1, 1 - u)
                a.vector(dve, t, u, 3)

            dve.wait_ge(s["ones_set"], 1)
            keep_keys(0, 0)
            keep_values(0, 0)
            over_pairs(dve, tile)
            add(T - 2)
            a.drain(a.vector, dve)
            add(T - 1)


def narrow_attention(nc, g, sb, name, v, qT, kT, head_scale, H, DH, mask, out):
    groups = H // GH
    qm = sb(f"{name}_qm", [128, 2, H, P])
    with stage(nc, name, "qm", *ATTEND) as (block, s):
        a = Attention(nc, g, s, sb, name, H, DH + 1, mask, head=lambda k, h: GH * k + h,
                      query=lambda u, h: qm[:, u, h, :], key=lambda t, u, h: g.tile_of(kT, t),
                      value=lambda t, u, h: v[:, t, h, :], out=out)

        @block.tensor
        def _(pe):
            def tile(t, u):
                pe.wait_ge(s["qm"], t + 1)
                for k in range(groups):
                    a.tensor(pe, t, u, k)

            over_pairs(pe, tile)
            a.drain(a.tensor, pe)

        @block.gpsimd
        def _(pool):
            def tile(t, u):
                wait_from(pool, s["scores"], groups * (t - 1))
                nc.gpsimd.tensor_tensor(qm[:, u, :, :], under(g.tile_of(qT, t), H), over(head_scale, P),
                                        ALU.mult).then_inc(s["qm"], 1)

            over_pairs(pool, tile)

        @block.scalar
        def _(act):
            def tile(t, u):
                for k in range(groups):
                    a.scalar(act, t, u, k)

            over_pairs(act, tile)
            a.drain(a.scalar, act)

        @block.vector
        def _(dve):
            def tile(t, u):
                for k in range(groups):
                    a.vector(dve, t, u, k)

            over_pairs(dve, tile)
            a.drain(a.vector, dve)


def project_values(nc, g, name, lhs, wv, bias, v, H, DH):
    with stage(nc, name, "v", "ones", "kept") as (block, s):
        @block.tensor
        def _(pe):
            for b in range(NB):
                for j in range(BT):
                    t = b * BT + j
                    bank = g.ps[0:P, b, j * D:(j + 1) * D]
                    if bias is not None:
                        nc.tensor.matmul(bank, g.ones[0:1, 0:P], bias[:], start=True, stop=False)
                    last = nc.tensor.matmul(bank, lhs[:, t * P:(t + 1) * P], wv, start=bias is None, stop=True)
                last.then_inc(s["v"], 1)

        @block.gpsimd
        def _(pool):
            nc.gpsimd.memset(v[:, :, :, DH:DH + 1], 1.0).then_inc(s["ones"], 1)

        @block.vector
        def _(dve):
            for b in range(NB):
                dve.wait_ge(s["v"], b + 1)
                for j in range(BT):
                    last = nc.vector.tensor_copy(
                        v[:, b * BT + j, :, 0:DH],
                        g.ps[0:P, b, j * D:(j + 1) * D].rearrange("p (h d) -> p h d", h=H))
                last.then_inc(s["kept"], 1)


def head_features(nc, link, mask, H, DH):
    link(nc.gpsimd.memset(mask[:], 1.0))
    link(nc.gpsimd.affine_select(out=mask[:], in_=mask[:], compare_op=ALU.is_ge, fill=0.0, base=0,
                                 pattern=[[-DH, H]], channel_multiplier=1))
    link(nc.gpsimd.affine_select(out=mask[:], in_=mask[:], compare_op=ALU.is_ge, fill=0.0, base=DH - 1,
                                 pattern=[[DH, H]], channel_multiplier=-1))


def biased_attention(nc, g, w, sb):
    H, DH = 8, 16
    wqT, wkv, wo = sb("a1_wqT", [D, D]), sb("a1_wkv", [D, 2, D]), sb("a1_wo", [D, D])
    scale_col, dir_row = sb("a1_scale_col", [D, 1]), sb("a1_dir_row", [1, D])
    normalize(nc, g, "a1_norm", g.x, [
        (wqT[:], w["L1_attn_WqT"]), (wkv[:], w["L1_attn_Wkv"].rearrange("d (a e) -> d a e", a=2)),
        (wo[:], w["L1_attn_Wout"]), (scale_col[:], column(w["L1_attn_head_scales_row"])),
        (dir_row[:], row(w["L1_attn_head_dirs_row"]))])
    same, mix, wq = sb("a1_same", [D, D]), sb("a1_mix", [D, D]), sb("a1_wq", [D, D])
    heads, v = sb("a1_heads", [D, H]), sb("a1_v", [P, T, H, DH + 1])
    qT, kT = g.workT, g.keyT
    with stage(nc, "a1_weights", "cut", "outer", "steps", "mixed", "wq", "wq_kept", "qk", "kept") as (block, s):
        @block.gpsimd
        def _(pool):
            link = in_order(pool, s["cut"])
            head_features(nc, link, heads, H, DH)
            link(nc.gpsimd.tensor_copy(same[:].rearrange("p (h d) -> p h d", h=H), over(heads[:], DH)))

        @block.tensor
        def _(pe):
            nc.tensor.matmul(g.ps[:, 0, 0:D], dir_row[:], dir_row[:], start=True, stop=True).then_inc(s["outer"], 1)
            pe.wait_ge(s["mixed"], 1)
            nc.tensor.matmul(g.ps[:, 1, 0:D], wqT[:], mix[:], start=True, stop=True).then_inc(s["wq"], 1)
            pe.wait_ge(s["wq_kept"], 1)
            for b in range(NB):
                nc.tensor.matmul(g.ps[:, b, 0:W], wq[:], g.xnT[:, b * W:(b + 1) * W], start=True, stop=True)
                nc.tensor.matmul(g.ps[:, NB + b, 0:W], wkv[:, 0, :], g.xnT[:, b * W:(b + 1) * W], start=True,
                                 stop=True).then_inc(s["qk"], 1)

        @block.vector
        def _(dve):
            link = in_order(dve, s["steps"])
            dve.wait_ge(s["cut"], 4)
            dve.wait_ge(s["outer"], 1)
            link(nc.vector.scalar_tensor_tensor(out=mix[:], in0=g.ps[:, 0, 0:D], scalar=scale_col[:, 0:1],
                                                in1=same[:], op0=ALU.mult, op1=ALU.mult))
            nc.vector.scalar_tensor_tensor(out=mix[:], in0=g.ident[:], scalar=DH ** -0.5, in1=mix[:],
                                           op0=ALU.mult, op1=ALU.add).then_inc(s["mixed"], 1)
            dve.wait_ge(s["wq"], 1)
            nc.vector.tensor_copy(wq[:], g.ps[:, 1, 0:D]).then_inc(s["wq_kept"], 1)
            for b in range(NB):
                dve.wait_ge(s["qk"], b + 1)
                nc.vector.tensor_copy(kT[:, b * W:(b + 1) * W], g.ps[:, NB + b, 0:W]).then_inc(s["kept"], 1)

        @block.scalar
        def _(act):
            for b in range(NB):
                act.wait_ge(s["qk"], b + 1)
                nc.scalar.copy(qT[:, b * W:(b + 1) * W], g.ps[:, b, 0:W]).then_inc(s["kept"], 1)
    project_values(nc, g, "a1_values", g.xnT, wkv[:, 1, :], None, v, H, DH)
    narrow_attention(nc, g, sb, "a1", v, qT, kT, heads[:], H, DH, g.mask_q,
                     lambda i, k: g.work[:, i, k * GH * DH:(k + 1) * GH * DH].rearrange("p (h d) -> p h d", h=GH))
    turn_and_project(nc, g, "a1_out", g.work, wo, None, g.x)


def scaled_attention(nc, g, w, sb):
    H, DH = 16, 8
    wq, wk, wv, wo = (sb(f"a2_{n}", [D, D]) for n in ("wq", "wk", "wv", "wo"))
    cols = sb("a2_cols", [D, 6])
    bv, bo4 = sb("a2_bv", [1, D]), sb("a2_bo4", [1, 4 * D])
    gains = sb("a2_gains", [P, 2, D])
    names = ("bq", "bk", "lq1", "lk1", "lq2", "lk2")
    flat = lambda ap: ap if len(ap.shape) == 1 else ap.rearrange("h d -> (h d)")
    normalize(nc, g, "a2_norm", g.x, [
        (wq[:], w["L2_attn_Wq"]), (wk[:], w["L2_attn_Wk"]), (wv[:], w["L2_attn_Wv"]), (wo[:], w["L2_attn_Wo"]),
        *[(cols[:, n:n + 1], column(flat(w[f"L2_attn_{name}"]))) for n, name in enumerate(names)],
        (bv[:], row(w["L2_attn_bv"])), (bo4[:], row(w["L2_attn_bo4"])),
        (gains[:, 0, :], rows(flat(w["L2_attn_gn_w"]), P)), (gains[:, 1, :], rows(flat(w["L2_attn_gn_b"]), P))])
    heads, same, v = sb("a2_heads", [D, H]), sb("a2_same", [D, D]), sb("a2_v", [P, T, H, DH + 1])
    dots, lams, scale = sb("a2_dots", [D, 2]), sb("a2_lams", [D, 3]), sb("a2_scale", [D, H])
    qT, kT = g.workT, g.keyT
    with stage(nc, "a2_weights", "cut", "steps", "dots", "sums", "exps", "qk", "kept") as (block, s):
        @block.gpsimd
        def _(pool):
            link = in_order(pool, s["cut"])
            head_features(nc, link, heads, H, DH)
            link(nc.gpsimd.tensor_copy(same[:].rearrange("p (h d) -> p h d", h=H), over(heads[:], DH)))

        @block.tensor
        def _(pe):
            for b in range(NB):
                if b == 2:
                    pe.wait_ge(s["dots"], 2)
                    pe.wait_ge(s["cut"], 4)
                    nc.tensor.matmul(g.ps[:, 7, 0:2], same[:], dots[:], start=True, stop=True).then_inc(s["sums"], 1)
                    pe.wait_ge(s["exps"], 1)
                nc.tensor.matmul(g.ps[:, b, 0:W], wq[:], g.xnT[:, b * W:(b + 1) * W], start=True, stop=True)
                nc.tensor.matmul(g.ps[:, NB + b, 0:W], wk[:], g.xnT[:, b * W:(b + 1) * W], start=True,
                                 stop=True).then_inc(s["qk"], 1)

        @block.vector
        def _(dve):
            link = in_order(dve, s["steps"])
            nc.vector.tensor_tensor(dots[:, 0:1], cols[:, 2:3], cols[:, 3:4], ALU.mult).then_inc(s["dots"], 1)
            nc.vector.tensor_tensor(dots[:, 1:2], cols[:, 4:5], cols[:, 5:6], ALU.mult).then_inc(s["dots"], 1)
            dve.wait_ge(s["exps"], 1)
            link(nc.vector.tensor_tensor(lams[:, 2:3], lams[:, 0:1], lams[:, 1:2], ALU.subtract))
            link(nc.vector.tensor_scalar(lams[:, 2:3], lams[:, 2:3], 0.8, DH ** -0.5, ALU.add, ALU.mult))
            dve.wait_ge(s["cut"], 4)
            link(nc.vector.tensor_scalar(scale[:], heads[:], lams[:, 2:3], None, ALU.mult))
            for b in range(NB):
                dve.wait_ge(s["qk"], b + 1)
                nc.vector.tensor_scalar(kT[:, b * W:(b + 1) * W], g.ps[:, NB + b, 0:W], cols[:, 1:2], None,
                                        ALU.add).then_inc(s["kept"], 1)

        @block.scalar
        def _(act):
            act.wait_ge(s["sums"], 1)
            nc.scalar.activation(lams[:, 0:2], g.ps[:, 7, 0:2], ACT.Exp).then_inc(s["exps"], 1)
            for b in range(NB):
                act.wait_ge(s["qk"], b + 1)
                nc.scalar.activation(qT[:, b * W:(b + 1) * W], g.ps[:, b, 0:W], ACT.Identity,
                                     bias=cols[:, 0:1]).then_inc(s["kept"], 1)
    project_values(nc, g, "a2_values", g.xnT, wv[:], bv, v, H, DH)
    narrow_attention(nc, g, sb, "a2", v, qT, kT, scale[:], H, DH, g.mask_any,
                     lambda i, k: g.work[:, i, k * GH * DH:(k + 1) * GH * DH].rearrange("p (h d) -> p h d", h=GH))
    both = sb("a2_both", [P, P])
    sums, mean, rstd = (sb(f"a2_{n}", [P, T * H]) for n in ("sums", "mean", "rstd"))
    wide = g.work[:].rearrange("p t (h d) -> p (t h) d", d=DH)
    square = g.xn[:].rearrange("p t (h d) -> p (t h) d", d=DH)
    share = 1.0 / (S * DH)
    with stage(nc, "a2_gn", "cut", "sums", "steps", "total", "centred", "squared", "spread", "deviation") as (block, s):
        @block.gpsimd
        def _(pool):
            link = in_order(pool, s["cut"])
            link(nc.gpsimd.tensor_scalar(both[:], g.mask_any[:, 0, :], 0.0, None, ALU.is_ge))

        @block.tensor
        def _(pe):
            pe.wait_ge(s["cut"], 1)
            for n in range(2):
                pe.wait_ge(s["sums"], n + 1)
                nc.tensor.matmul(g.ps[0:P, n, 0:T * H], both[:], sums[:], start=True, stop=True).then_inc(s["total"], 1)

        @block.scalar
        def _(act):
            act.wait_ge(s["centred"], 1)
            nc.scalar.activation(square, wide, ACT.Square).then_inc(s["squared"], 1)
            act.wait_ge(s["spread"], 1)
            nc.scalar.sqrt(rstd[:], sums[:]).then_inc(s["deviation"], 1)

        @block.vector
        def _(dve):
            link = in_order(dve, s["steps"])
            nc.vector.tensor_reduce(sums[:], wide, AX_X, ALU.add).then_inc(s["sums"], 1)
            dve.wait_ge(s["total"], 1)
            link(nc.vector.tensor_scalar(mean[:], g.ps[0:P, 0, 0:T * H], -share, None, ALU.mult))
            nc.vector.tensor_tensor(wide, wide, over(mean[:], DH), ALU.add).then_inc(s["centred"], 1)
            dve.wait_ge(s["squared"], 1)
            nc.vector.tensor_reduce(sums[:], square, AX_X, ALU.add).then_inc(s["sums"], 1)
            dve.wait_ge(s["total"], 2)
            nc.vector.tensor_scalar(sums[:], g.ps[0:P, 1, 0:T * H], share, EPS, ALU.mult, ALU.add)\
                .then_inc(s["spread"], 1)
            dve.wait_ge(s["deviation"], 1)
            link(nc.vector.reciprocal(rstd[:], rstd[:]))
            link(nc.vector.tensor_tensor(wide, wide, over(rstd[:], DH), ALU.mult))
            link(nc.vector.tensor_tensor(g.work[:], g.work[:], under(gains[:, 0, :], T), ALU.mult))
            link(nc.vector.tensor_tensor(g.work[:], g.work[:], under(gains[:, 1, :], T), ALU.add))
    turn_and_project(nc, g, "a2_out", g.work, wo, bo4, g.x)


def rotary_attention(nc, g, w, sb):
    H, DH, DV = 16, 8, 32
    wqk = sb("a3_wqk", [D, 4, D])
    bqk = sb("a3_bqk", [D, 4])
    cs = sb("a3_cs", [D, 2, P])
    wkv, bkv = sb("a3_wkv", [D, DV]), sb("a3_bkv", [DV, 1])
    wv, bv, wo, bo4 = sb("a3_wv", [DV, D]), sb("a3_bv", [1, D]), sb("a3_wo", [D, D]), sb("a3_bo4", [1, 4 * D])
    names = ("wqr", "wqr_swapped", "wkr", "wkr_swapped")
    normalize(nc, g, "a3_norm", g.x, [
        *[(wqk[:, n, :], w[f"L3_attn_{name}"]) for n, name in enumerate(names)],
        *[(bqk[:, n:n + 1], column(w[f"L3_attn_{name.replace('w', 'b', 1)}"])) for n, name in enumerate(names)],
        (cs[:], w["rotary"].rearrange("a d t -> d a t")), (wkv[:], w["L3_attn_wkv"]),
        (bkv[:], column(w["L3_attn_bkv"])), (wv[:], w["L3_attn_wv"]), (bv[:], row(w["L3_attn_bv"])),
        (wo[:], w["L3_attn_wo"]), (bo4[:], row(w["L3_attn_bo4"]))])
    heads, v, cT = sb("a3_heads", [D, H]), sb("a3_v", [P, T, H, DH + 1]), sb("a3_cT", [DV, N])
    ra, rb = sb("a3_ra", [D, 2, W]), sb("a3_rb", [D, 2, W])
    outs = (g.workT, g.keyT)
    with stage(nc, "a3_qk", "cut", "c", "c_kept", "pair", "turned", "summed", "kept") as (block, s):
        @block.gpsimd
        def _(pool):
            link = in_order(pool, s["cut"])
            head_features(nc, link, heads, H, DH)
            link(nc.gpsimd.tensor_scalar(heads[:], heads[:], DH ** -0.5, None, ALU.mult))

        @block.tensor
        def _(pe):
            for b in range(NB):
                nc.tensor.matmul(g.ps[0:DV, b, 0:W], wkv[:], g.xnT[:, b * W:(b + 1) * W], start=True,
                                 stop=True).then_inc(s["c"], 1)
            pe.wait_ge(s["c_kept"], NB)
            for n in range(2 * NB):
                which, b = n // NB, n % NB
                if n >= 2:
                    pe.wait_ge(s["turned"], 2 * (n - 1))
                for m in range(2):
                    last = nc.tensor.matmul(g.ps[:, 2 * (n % 2) + m, 0:W], wqk[:, 2 * which + m, :],
                                            g.xnT[:, b * W:(b + 1) * W], start=True, stop=True)
                last.then_inc(s["pair"], 1)

        @block.vector
        def _(dve):
            for n in range(2 * NB):
                which = n // NB
                dve.wait_ge(s["pair"], n + 1)
                if n >= 2:
                    dve.wait_ge(s["kept"], n - 1)
                for m, r in enumerate((ra, rb)):
                    nc.vector.scalar_tensor_tensor(
                        out=r[:, n % 2, :].rearrange("p (j t) -> p j t", j=BT),
                        in0=g.ps[:, 2 * (n % 2) + m, 0:W].rearrange("p (j t) -> p j t", j=BT),
                        scalar=bqk[:, 2 * which + m:2 * which + m + 1], in1=under(cs[:, m, :], BT),
                        op0=ALU.add, op1=ALU.mult).then_inc(s["turned"], 1)
                dve.wait_ge(s["turned"], 2 * n + 2)
                nc.vector.tensor_tensor(ra[:, n % 2, :], ra[:, n % 2, :], rb[:, n % 2, :], ALU.add)\
                    .then_inc(s["summed"], 1)

        @block.scalar
        def _(act):
            for b in range(NB):
                act.wait_ge(s["c"], b + 1)
                nc.scalar.activation(cT[:, b * W:(b + 1) * W], g.ps[0:DV, b, 0:W], ACT.Gelu, bias=bkv[:, 0:1])\
                    .then_inc(s["c_kept"], 1)
            for n in range(2 * NB):
                which, b = n // NB, n % NB
                act.wait_ge(s["summed"], n + 1)
                nc.scalar.activation(outs[which][:, b * W:(b + 1) * W], ra[:, n % 2, :], ACT.Gelu)\
                    .then_inc(s["kept"], 1)
    project_values(nc, g, "a3_values", cT, wv[:], bv, v, H, DH)
    narrow_attention(nc, g, sb, "a3", v, outs[0], outs[1], heads[:], H, DH, g.mask_q,
                     lambda i, k: g.work[:, i, k * GH * DH:(k + 1) * GH * DH].rearrange("p (h d) -> p h d", h=GH))
    turn_and_project(nc, g, "a3_out", g.work, wo, bo4, g.x)


def best_two(nc, g, link, logits, E, r):
    for n, pick in enumerate((r.first, r.second)):
        link(nc.vector.tensor_reduce(r.top[:, n, :], logits[:], AX_X, ALU.max))
        link(nc.vector.tensor_tensor(pick[:], logits[:], over(r.top[:, n, :], E), ALU.is_equal))
        link(nc.vector.tensor_tensor(pick[:], pick[:], r.rank[:], ALU.mult))
        link(nc.vector.tensor_reduce(r.lead[:], pick[:], AX_X, ALU.max))
        link(nc.vector.tensor_tensor(pick[:], r.rank[:], over(r.lead[:], E), ALU.is_equal))
        if n == 0:
            link(nc.vector.scalar_tensor_tensor(out=logits[:], in0=pick[:], scalar=NEG, in1=logits[:],
                                                op0=ALU.mult, op1=ALU.add))


def rank_experts(nc, link, rank, E):
    for e in range(E):
        link(nc.gpsimd.memset(rank[:, :, e:e + 1], float(E - e)))


def token_logits(nc, g, wg, E, done):
    for t in range(T):
        last = nc.tensor.matmul(g.ps[0:P, 0, t * E:(t + 1) * E], g.xnT[:, t * P:(t + 1) * P], wg, start=True,
                                stop=True)
    last.then_inc(done, 1)


GATED_BIAS = ("gates_turned", "gates_kept", "bias", "bias_added")


class GatedBias:

    def __init__(self, nc, g, s, sb, name, combine, bias, E):
        self.nc, self.g, self.s, self.combine, self.bias, self.E = nc, g, s, combine, bias, E
        self.gatesT = sb(f"{name}_gatesT", [E, N])

    def tensor(self, pe):
        nc, g, s, E = self.nc, self.g, self.s, self.E
        for b in range(NB):
            for j in range(BT):
                last = nc.tensor.transpose(g.ps[0:E, b, j * P:(j + 1) * P], self.combine[:, b * BT + j, :],
                                           g.ident[0:P, 0:P])
            last.then_inc(s["gates_turned"], 1)
        for b in range(NB):
            pe.wait_ge(s["gates_kept"], b + 1)
            for j in range(BT):
                t = b * BT + j
                last = nc.tensor.matmul(g.ps[0:P, NB + b, j * D:(j + 1) * D], self.gatesT[:, t * P:(t + 1) * P],
                                        self.bias, start=True, stop=True)
            last.then_inc(s["bias"], 1)
        pe.wait_ge(s["bias_added"], NB)

    def scalar(self, act):
        for b in range(NB):
            act.wait_ge(self.s["gates_turned"], b + 1)
            self.nc.scalar.copy(self.gatesT[:, b * W:(b + 1) * W], self.g.ps[0:self.E, b, 0:W])\
                .then_inc(self.s["gates_kept"], 1)

    def vector(self, dve):
        for b in range(NB):
            dve.wait_ge(self.s["bias"], b + 1)
            part = self.g.x[:, b * BT:(b + 1) * BT, :]
            self.nc.vector.tensor_tensor(part, part, self.g.ps[0:P, NB + b, :].rearrange("p (j d) -> p j d", j=BT),
                                         ALU.add).then_inc(self.s["bias_added"], 1)
        dve.wait_ge(self.s["bias_added"], NB)


def experts(nc, g, name, sb, jobs, act_func, out, add_xn=False, biases=None):
    hT = sb(f"{name}_hT", [128, 2, 4, W])
    part = sb(f"{name}_part", [P, 2, BT, D])
    J = len(jobs)
    ups = sum(len(j.up) for j in jobs)
    assert all(len(j.up) <= 4 for j in jobs)
    first_up = [sum(len(j.up) for j in jobs[:n]) for n in range(J)]
    with stage(nc, name, "up", "hidden", "down", "gated", "added", *GATED_BIAS) as (block, s):
        gated = biases and GatedBias(nc, g, s, sb, name, *biases)

        @block.tensor
        def _(pe):
            if gated:
                gated.tensor(pe)
            with pe.Fori(0, NB) as i:
                def up(n):
                    for m, (wt, _, extra) in enumerate(jobs[n].up):
                        u = first_up[n] + m
                        if u >= 2:
                            pe.wait_ge(s["hidden"], ups * i + u - 1)
                        bank = g.ps[:, u % 2, 0:W]
                        rows_ = wt.shape[1]
                        last = nc.tensor.matmul(bank[0:rows_], wt, g.block_of(g.xnT, i), start=True,
                                                stop=extra is None)
                        if extra is not None:
                            last = nc.tensor.matmul(bank[0:rows_], extra[0], extra[1](i), start=False, stop=True)
                        last.then_inc(s["up"], 1)

                def down(n):
                    job = jobs[n]
                    pe.wait_ge(s["hidden"], ups * i + first_up[n] + len(job.up))
                    if n >= 2:
                        pe.wait_ge(s["gated"], J * i + n - 1)
                    for j in range(BT):
                        bank = g.ps[0:P, 4 + n % 2, j * D:(j + 1) * D]
                        if job.out_bias is not None:
                            nc.tensor.matmul(bank, g.ones[0:1, 0:P], job.out_bias, start=True, stop=False,
                                             skip_group_check=True)
                        for m, wt in enumerate(job.down):
                            last = nc.tensor.matmul(bank, hT[:, n % 2, m, j * P:(j + 1) * P], wt,
                                                    start=(m == 0 and job.out_bias is None),
                                                    stop=(m == len(job.down) - 1), skip_group_check=True)
                    last.then_inc(s["down"], 1)

                up(0)
                for n in range(J):
                    if n + 1 < J:
                        up(n + 1)
                    down(n)
                pe.wait_ge(s["gated"], J * i + J)

        @block.scalar
        def _(act):
            if gated:
                gated.scalar(act)
            with act.Fori(0, NB) as i:
                for n, job in enumerate(jobs):
                    if n >= 2:
                        act.wait_ge(s["down"], J * i + n - 1)
                    for m, (wt, bias, _) in enumerate(job.up):
                        u = first_up[n] + m
                        act.wait_ge(s["up"], ups * i + u + 1)
                        nc.scalar.activation(hT[0:wt.shape[1], n % 2, m, :], g.ps[0:wt.shape[1], u % 2, 0:W],
                                             act_func, bias=0.0 if bias is None else bias).then_inc(s["hidden"], 1)

        @block.vector
        def _(dve):
            if gated:
                gated.vector(dve)
            with dve.Fori(0, NB) as i:
                target = g.tiles_of(out, i)
                if add_xn:
                    nc.vector.tensor_tensor(target, target, g.tiles_of(g.xn, i), ALU.add).then_inc(s["added"], 1)
                for n, job in enumerate(jobs):
                    dve.wait_ge(s["down"], J * i + n + 1)
                    bank = g.ps[0:P, 4 + n % 2, :].rearrange("p (j d) -> p j d", j=BT)
                    if job.gate is None:
                        nc.vector.tensor_copy(part[:, n % 2, :, :], bank).then_inc(s["gated"], 1)
                    else:
                        nc.vector.tensor_tensor(part[:, n % 2, :, :], bank, over(g.block_gate(job.gate, i), D),
                                                ALU.mult).then_inc(s["gated"], 1)
                    dve.wait_ge(s["gated"], J * i + n + 1)
                    if add_xn or n:
                        dve.wait_ge(s["added"], (J + int(add_xn)) * i + n + int(add_xn))
                    nc.vector.tensor_tensor(target, target, part[:, n % 2, :, :], ALU.add).then_inc(s["added"], 1)
                dve.wait_ge(s["added"], (J + int(add_xn)) * i + J + int(add_xn))


def shared_and_routed(nc, g, w, sb):
    E, F = 8, 4 * D
    FB = F // 128
    A = E + 2
    w1, w2 = sb("f0_w1", [D, A, F]), sb("f0_w2", [128, A, FB, D])
    wg, r = sb("f0_wg", [D, E]), Routing(sb, "f0", E)
    normalize(nc, g, "f0_norm", g.x, [
        (wg[:], w["L0_ffn_centroidsT"]), (r.bias[:], rows(w["L0_ffn_routing_bias"], P)),
        *[(w1[:, e, :], w["L0_ffn_WfcT"][e]) for e in range(A)],
        *[(w2[:, e, :, :], w["L0_ffn_WprojT"][e].rearrange("(c p) d -> p c d", p=128)) for e in range(A)]])
    with stage(nc, "f0_route", "ranked", "logits", "steps", "raw", "score", "gap", "exp") as (block, s):
        @block.gpsimd
        def _(pool):
            rank_experts(nc, in_order(pool, s["ranked"]), r.rank, E)

        @block.tensor
        def _(pe):
            token_logits(nc, g, wg[:], E, s["logits"])

        @block.scalar
        def _(act):
            act.wait_ge(s["logits"], 1)
            nc.scalar.activation(r.score[:], g.ps[0:P, 0, 0:T * E].rearrange("p (t e) -> p t e", t=T), ACT.Sigmoid)\
                .then_inc(s["score"], 1)
            act.wait_ge(s["gap"], 1)
            nc.scalar.activation(g.stat[:, 0, :], g.stat[:, 0, :], ACT.Exp).then_inc(s["exp"], 1)

        @block.vector
        def _(dve):
            link = in_order(dve, s["steps"])
            dve.wait_ge(s["logits"], 1)
            dve.wait_ge(s["ranked"], E)
            dve.wait_ge(s["score"], 1)
            link(nc.vector.tensor_tensor(r.logits[:], g.ps[0:P, 0, 0:T * E].rearrange("p (t e) -> p t e", t=T),
                                         under(r.bias[:], T), ALU.add))
            best_two(nc, g, link, r.logits, E, r)
            dve.wait_ge(s["score"], 1)
            for n, pick in enumerate((r.first, r.second)):
                link(nc.vector.tensor_tensor(r.combine[:], pick[:], r.score[:], ALU.mult))
                link(nc.vector.tensor_reduce(r.top[:, n, :], r.combine[:], AX_X, ALU.add))
            link(nc.vector.tensor_tensor(r.a[:], r.top[:, 0, :], r.top[:, 1, :], ALU.max))
            link(nc.vector.tensor_tensor(r.b[:], r.top[:, 0, :], r.top[:, 1, :], ALU.min))
            nc.vector.tensor_tensor(g.stat[:, 0, :], r.b[:], r.a[:], ALU.subtract).then_inc(s["gap"], 1)
            dve.wait_ge(s["exp"], 1)
            link(nc.vector.tensor_scalar(r.a[:], g.stat[:, 0, :], 1.0, None, ALU.add))
            link(nc.vector.reciprocal(r.a[:], r.a[:]))
            link(nc.vector.tensor_tensor(r.b[:], g.stat[:, 0, :], r.a[:], ALU.mult))
            link(nc.vector.tensor_tensor(r.lead[:], r.top[:, 0, :], r.top[:, 1, :], ALU.is_ge))
            link(nc.vector.tensor_tensor(g.stat[:, 1, :], r.a[:], r.b[:], ALU.subtract))
            link(nc.vector.tensor_tensor(g.stat[:, 1, :], g.stat[:, 1, :], r.lead[:], ALU.mult))
            link(nc.vector.tensor_tensor(g.stat[:, 2, :], g.stat[:, 1, :], r.b[:], ALU.add))
            link(nc.vector.tensor_tensor(g.stat[:, 3, :], r.a[:], g.stat[:, 1, :], ALU.subtract))
            link(nc.vector.tensor_tensor(r.first[:], r.first[:], over(g.stat[:, 2, :], E), ALU.mult))
            link(nc.vector.tensor_tensor(r.second[:], r.second[:], over(g.stat[:, 3, :], E), ALU.mult))
            link(nc.vector.tensor_tensor(r.combine[:], r.first[:], r.second[:], ALU.add))
    jobs = [Expert([(w1[:, e, m * 128:(m + 1) * 128], None, None) for m in range(FB)],
                   [w2[:, e, m, :] for m in range(FB)], gate=None if e < 2 else r.combine[:, :, e - 2])
            for e in range(A)]
    experts(nc, g, "f0", sb, jobs, ACT.Gelu, g.x, add_xn=True)


def capped_experts(nc, g, w, sb):
    E, F, CAP = 8, 512, 512
    FB = F // 128
    w1, w2 = sb("f1_w1", [D, E, F]), sb("f1_w2", [128, E, FB, D])
    b1, b2 = sb("f1_b1", [128, E, FB]), sb("f1_b2", [E, D])
    rw1, rb1, rw2 = sb("f1_rw1", [D, F]), sb("f1_rb1", [128, FB]), sb("f1_rw2", [128, FB, E])
    r = Routing(sb, "f1", E)
    normalize(nc, g, "f1_norm", g.x, [
        (rw1[:], w["L1_ffn_rw1"]), (rb1[:], w["L1_ffn_rb1_cols"]),
        (rw2[:], w["L1_ffn_rw2"].rearrange("(m p) e -> p m e", p=128)), (r.bias[:], rows(w["L1_ffn_rb2"], P)),
        (b1[:], w["L1_ffn_eb1_cols"]),
        (b2[:], w["L1_ffn_eb2"]),
        *[(w1[:, e, :], w["L1_ffn_ew1"][e]) for e in range(E)],
        *[(w2[:, e, :, :], w["L1_ffn_ew2"][e].rearrange("(c p) d -> p c d", p=128)) for e in range(E)]])
    hT = sb("f1_router_hT", [128, FB, W])
    earlier = sb("f1_earlier", [P, P])
    chosen, before, total = (sb(f"f1_{n}", [P, T, E]) for n in ("chosen", "before", "total"))
    with stage(nc, "f1_route", "ranked", "up", "hidden", "logits", "logits_kept", "steps", "gap", "exp", "chosen",
               "counts") as (block, s):
        @block.gpsimd
        def _(pool):
            link = in_order(pool, s["ranked"])
            rank_experts(nc, link, r.rank, E)
            link(nc.gpsimd.memset(earlier[:], 1.0))
            link(nc.gpsimd.affine_select(out=earlier[:], in_=earlier[:], compare_op=ALU.is_ge, fill=0.0,
                                         base=-1, pattern=[[1, P]], channel_multiplier=-1))

        @block.tensor
        def _(pe):
            for b in range(NB):
                for m in range(FB):
                    if b:
                        pe.wait_ge(s["hidden"], FB * (b - 1) + m + 1)
                    nc.tensor.matmul(g.ps[:, m, 0:W], rw1[:, m * 128:(m + 1) * 128], g.xnT[:, b * W:(b + 1) * W],
                                     start=True, stop=True).then_inc(s["up"], 1)
                pe.wait_ge(s["hidden"], FB * (b + 1))
                for j in range(BT):
                    for m in range(FB):
                        last = nc.tensor.matmul(g.ps[0:P, 4 + b % 2, j * E:(j + 1) * E], hT[:, m, j * P:(j + 1) * P],
                                                rw2[:, m, :], start=(m == 0), stop=(m == FB - 1))
                last.then_inc(s["logits"], 1)
                if b % 2:
                    pe.wait_ge(s["logits_kept"], b + 1)
            pe.wait_ge(s["chosen"], 1)
            nc.tensor.matmul(g.ps[0:P, 6, 0:T * E], earlier[:], chosen[:].rearrange("p t e -> p (t e)"),
                             start=True, stop=True)
            nc.tensor.matmul(g.ps[0:P, 7, 0:T * E], g.ones[0:P, 0:P], chosen[:].rearrange("p t e -> p (t e)"),
                             start=True, stop=True).then_inc(s["counts"], 1)

        @block.scalar
        def _(act):
            for b in range(NB):
                if b:
                    act.wait_ge(s["logits"], b)
                for m in range(FB):
                    act.wait_ge(s["up"], FB * b + m + 1)
                    nc.scalar.activation(hT[:, m, :], g.ps[:, m, 0:W], ACT.Relu, bias=rb1[:, m:m + 1])\
                        .then_inc(s["hidden"], 1)
            act.wait_ge(s["gap"], 1)
            nc.scalar.activation(r.a[:], g.stat[:, 0, :], ACT.Exp).then_inc(s["exp"], 1)

        @block.vector
        def _(dve):
            link = in_order(dve, s["steps"])
            for b in range(NB):
                dve.wait_ge(s["logits"], b + 1)
                nc.vector.tensor_tensor(r.logits[:, b * BT:(b + 1) * BT, :],
                                        g.ps[0:P, 4 + b % 2, 0:BT * E].rearrange("p (t e) -> p t e", t=BT),
                                        under(r.bias[:], BT), ALU.add).then_inc(s["logits_kept"], 1)
            dve.wait_ge(s["logits_kept"], NB)
            dve.wait_ge(s["ranked"], E + 2)
            best_two(nc, g, link, r.logits, E, r)
            nc.vector.tensor_tensor(chosen[:], r.first[:], r.second[:], ALU.add).then_inc(s["chosen"], 1)
            nc.vector.tensor_tensor(g.stat[:, 0, :], r.top[:, 1, :], r.top[:, 0, :], ALU.subtract)\
                .then_inc(s["gap"], 1)
            dve.wait_ge(s["exp"], 1)
            weigh_two(nc, link, r, E)
            dve.wait_ge(s["counts"], 1)
            link(nc.vector.tensor_copy(total[:], g.ps[0:P, 7, 0:T * E].rearrange("p (t e) -> p t e", t=T)))
            link(nc.vector.memset(before[:, 0:1, :], 0.0))
            for t in range(1, T):
                link(nc.vector.tensor_tensor(before[:, t, :], before[:, t - 1, :], total[:, t - 1, :], ALU.add))
            link(nc.vector.tensor_tensor(before[:], before[:],
                                         g.ps[0:P, 6, 0:T * E].rearrange("p (t e) -> p t e", t=T), ALU.add))
            link(nc.vector.scalar_tensor_tensor(out=r.combine[:], in0=before[:], scalar=float(CAP),
                                                in1=r.combine[:], op0=ALU.is_lt, op1=ALU.mult))
    jobs = [Expert([(w1[:, e, m * 128:(m + 1) * 128], b1[:, e, m:m + 1], None) for m in range(FB)],
                   [w2[:, e, m, :] for m in range(FB)], gate=r.combine[:, :, e]) for e in range(E)]
    experts(nc, g, "f1", sb, jobs, ACT.Relu, g.x, biases=(r.combine, b2[:], E))


def weigh_two(nc, link, r, E):
    link(nc.vector.tensor_scalar(r.b[:], r.a[:], 1.0, None, ALU.add))
    link(nc.vector.reciprocal(r.b[:], r.b[:]))
    link(nc.vector.tensor_tensor(r.a[:], r.a[:], r.b[:], ALU.mult))
    link(nc.vector.tensor_tensor(r.first[:], r.first[:], over(r.b[:], E), ALU.mult))
    link(nc.vector.tensor_tensor(r.second[:], r.second[:], over(r.a[:], E), ALU.mult))
    link(nc.vector.tensor_tensor(r.combine[:], r.first[:], r.second[:], ALU.add))


def small_experts(nc, g, w, sb):
    E, F = 8, 64
    w1, w2 = sb("f2_w1", [D, E * F]), sb("f2_w2", [128, E // 2, D])
    b1, b2 = sb("f2_b1", [128, E // 2]), sb("f2_b2", [E, D])
    wg, r = sb("f2_wg", [D, E]), Routing(sb, "f2", E)
    normalize(nc, g, "f2_norm", g.x, [
        (wg[:], w["L2_ffn_gate_w"]), (r.bias[:], rows(w["L2_ffn_gate_b"], P)),
        (w1[:].rearrange("d (e f) -> d e f", e=E), w["L2_ffn_w1"].rearrange("e d f -> d e f")),
        (w2[:], w["L2_ffn_w2"].rearrange("(c a) f d -> (a f) c d", a=2)),
        (b1[:], w["L2_ffn_b1_cols"]),
        (b2[:], w["L2_ffn_b2"])])
    with stage(nc, "f2_route", "ranked", "logits", "steps", "gap", "exp") as (block, s):
        @block.gpsimd
        def _(pool):
            rank_experts(nc, in_order(pool, s["ranked"]), r.rank, E)

        @block.tensor
        def _(pe):
            token_logits(nc, g, wg[:], E, s["logits"])

        @block.scalar
        def _(act):
            act.wait_ge(s["gap"], 1)
            nc.scalar.activation(r.a[:], g.stat[:, 0, :], ACT.Exp).then_inc(s["exp"], 1)

        @block.vector
        def _(dve):
            link = in_order(dve, s["steps"])
            dve.wait_ge(s["logits"], 1)
            dve.wait_ge(s["ranked"], E)
            link(nc.vector.tensor_tensor(r.logits[:], g.ps[0:P, 0, 0:T * E].rearrange("p (t e) -> p t e", t=T),
                                         under(r.bias[:], T), ALU.add))
            best_two(nc, g, link, r.logits, E, r)
            nc.vector.tensor_tensor(g.stat[:, 0, :], r.top[:, 1, :], r.top[:, 0, :], ALU.subtract)\
                .then_inc(s["gap"], 1)
            dve.wait_ge(s["exp"], 1)
            weigh_two(nc, link, r, E)
    jobs = [Expert([(w1[:, c * 128:(c + 1) * 128], b1[:, c:c + 1], None)], []) for c in range(E // 2)]
    paired_experts(nc, g, "f2", sb, jobs, w2, b2, r, E, F)


def paired_experts(nc, g, name, sb, jobs, w2, b2, r, E, F):
    hT = sb(f"{name}_hT", [128, 2, W])
    part = sb(f"{name}_part", [P, 2, BT, D])
    C = E // 2
    with stage(nc, name, "up", "hidden", "down", "gated", "added", *GATED_BIAS) as (block, s):
        biases = GatedBias(nc, g, s, sb, name, r.combine, b2[:], E)

        @block.tensor
        def _(pe):
            biases.tensor(pe)
            with pe.Fori(0, NB) as i:
                def up(c):
                    if c >= 2:
                        pe.wait_ge(s["hidden"], C * i + c - 1)
                    nc.tensor.matmul(g.ps[:, c % 2, 0:W], jobs[c].up[0][0], g.block_of(g.xnT, i), start=True,
                                     stop=True).then_inc(s["up"], 1)

                up(0)
                for c in range(C):
                    if c + 1 < C:
                        up(c + 1)
                    pe.wait_ge(s["hidden"], C * i + c + 1)
                    for half in range(2):
                        e = 2 * c + half
                        if e >= 4:
                            pe.wait_ge(s["gated"], E * i + e - 3)
                        for j in range(BT):
                            bank = g.ps[0:P, 4 + 2 * half + c % 2, j * D:(j + 1) * D]
                            last = nc.tensor.matmul(bank, hT[F * half:F * half + F, c % 2, j * P:(j + 1) * P],
                                                    w2[F * half:F * half + F, c, :], start=True, stop=True,
                                                    skip_group_check=True)
                        last.then_inc(s["down"], 1)
                pe.wait_ge(s["gated"], E * i + E)

        @block.scalar
        def _(act):
            biases.scalar(act)
            with act.Fori(0, NB) as i:
                for c in range(C):
                    if c >= 2:
                        act.wait_ge(s["down"], E * i + 2 * c - 2)
                    act.wait_ge(s["up"], C * i + c + 1)
                    nc.scalar.activation(hT[:, c % 2, :], g.ps[:, c % 2, 0:W], ACT.Gelu, bias=jobs[c].up[0][1])\
                        .then_inc(s["hidden"], 1)

        @block.vector
        def _(dve):
            biases.vector(dve)
            with dve.Fori(0, NB) as i:
                target = g.tiles_of(g.x, i)
                for e in range(E):
                    dve.wait_ge(s["down"], E * i + e + 1)
                    bank = g.ps[0:P, 4 + 2 * (e % 2) + e // 2 % 2, :].rearrange("p (j d) -> p j d", j=BT)
                    nc.vector.tensor_tensor(part[:, e % 2, :, :], bank, over(g.block_gate(r.combine[:, :, e], i), D),
                                            ALU.mult).then_inc(s["gated"], 1)
                    dve.wait_ge(s["gated"], E * i + e + 1)
                    if e:
                        dve.wait_ge(s["added"], E * i + e)
                    nc.vector.tensor_tensor(target, target, part[:, e % 2, :, :], ALU.add).then_inc(s["added"], 1)
                dve.wait_ge(s["added"], E * i + E)


def adapted_experts(nc, g, w, sb):
    E, F, R = 4, 512, 4
    FB = F // 128
    wi, wo = sb("f3_wi", [D, F]), sb("f3_wo", [128, FB, D])
    low, high = sb("f3_low", [D, E, R]), sb("f3_high", [R, E, F])
    wg, r = sb("f3_wg", [D, E]), Routing(sb, "f3", E)
    normalize(nc, g, "f3_norm", g.x, [
        (wg[:], w["L3_ffn_WgT"]), (r.bias[:], rows(w["L3_ffn_bg"], P)), (wi[:], w["L3_ffn_WiT"]),
        (wo[:], w["L3_ffn_WoT"].rearrange("(c p) d -> p c d", p=128)),
        (low[:], w["L3_ffn_AT"].rearrange("d (e r) -> d e r", e=E)),
        (high[:], w["L3_ffn_BT"].rearrange("r (e f) -> r e f", e=E))])
    lowT = sb("f3_lowT", [R, E, N])
    with stage(nc, "f3_route", "ranked", "logits", "low", "low_kept", "steps", "gap", "exp") as (block, s):
        @block.gpsimd
        def _(pool):
            rank_experts(nc, in_order(pool, s["ranked"]), r.rank, E)

        @block.tensor
        def _(pe):
            token_logits(nc, g, wg[:], E, s["logits"])
            for e in range(E):
                for b in range(NB):
                    n = e * NB + b
                    if n >= 2:
                        pe.wait_ge(s["low_kept"], n - 1)
                    nc.tensor.matmul(g.ps[0:R, 1 + n % 2, 0:W], low[:, e, :], g.xnT[:, b * W:(b + 1) * W],
                                     start=True, stop=True).then_inc(s["low"], 1)

        @block.scalar
        def _(act):
            for e in range(E):
                for b in range(NB):
                    n = e * NB + b
                    act.wait_ge(s["low"], n + 1)
                    nc.scalar.copy(lowT[:, e, b * W:(b + 1) * W], g.ps[0:R, 1 + n % 2, 0:W]).then_inc(s["low_kept"], 1)
            act.wait_ge(s["gap"], 1)
            nc.scalar.activation(r.score[:], r.score[:], ACT.Exp).then_inc(s["exp"], 1)

        @block.vector
        def _(dve):
            link = in_order(dve, s["steps"])
            dve.wait_ge(s["logits"], 1)
            dve.wait_ge(s["ranked"], E)
            link(nc.vector.tensor_tensor(r.logits[:], g.ps[0:P, 0, 0:T * E].rearrange("p (t e) -> p t e", t=T),
                                         under(r.bias[:], T), ALU.add))
            link(nc.vector.tensor_copy(r.kept_logits[:], r.logits[:]))
            best_two(nc, g, link, r.logits, E, r)
            nc.vector.tensor_tensor(r.score[:], r.kept_logits[:], over(r.top[:, 0, :], E), ALU.subtract)\
                .then_inc(s["gap"], 1)
            dve.wait_ge(s["exp"], 1)
            link(nc.vector.tensor_reduce(r.a[:], r.score[:], AX_X, ALU.add))
            link(nc.vector.reciprocal(r.a[:], r.a[:]))
            link(nc.vector.tensor_tensor(r.score[:], r.score[:], over(r.a[:], E), ALU.mult))
            link(nc.vector.tensor_tensor(r.first[:], r.first[:], r.second[:], ALU.add))
            link(nc.vector.tensor_tensor(r.combine[:], r.first[:], r.score[:], ALU.mult))
    jobs = [Expert([(wi[:, m * 128:(m + 1) * 128], None,
                     (high[:, e, m * 128:(m + 1) * 128], lambda i, e=e: g.block_of(lowT[:, e, :], i)))
                    for m in range(FB)],
                   [wo[:, m, :] for m in range(FB)], gate=r.combine[:, :, e]) for e in range(E)]
    experts(nc, g, "f3", sb, jobs, ACT.Relu, g.x)


SLOTS = 4
STEPS = B // SLOTS


def over_steps(eng, step):
    step(0)
    with eng.Fori(1, STEPS - 1) as i:
        step(i)
    step(STEPS - 1)


def cross_attend(nc, g, w, sb, name, H, wqk, wvo, out_row, context_norm=False, q_row=None):
    R = H * S
    RG = min(R, P)
    G, KJ = R // RG, 3
    CJ = LC // KJ
    LJ = CJ * LP
    KQ = wqk(0).shape[1]
    CB = 1 if R > 256 else CJ
    NS, RING = LC // CB, 3
    PARTS = 3 if R > 256 else 1
    CP, NP = LC // PARTS, NS // PARTS
    EXPS = 6 if R > 256 else 1
    CE = LC // EXPS
    EARLY = 3 if R > 256 else 1
    split = not context_norm
    KS = 2 if split else SLOTS
    kT = sb(f"{name}_kT", [KQ, KS, LC, LP])
    tok = sb(f"{name}_tok", [LP, SLOTS, LC, DC + 1])
    qT = sb(f"{name}_qT", [KQ, 2, R], F32R if split else F32)
    if split:
        q_low = sb(f"{name}_q_low", [KQ, 2, R], F32R)
        k_high, k_low = (sb(f"{name}_{n}", [KQ, 2, LC, LP], F32R) for n in ("k_high", "k_low"))
    sc = sb(f"{name}_sc", [LP, 2, LC, R])
    top = sb(f"{name}_top", [LP, PARTS, max(R, P)])
    negmax, diag = sb(f"{name}_negmax", [RG, 2, G]), sb(f"{name}_diag", [RG, 2, G, RG])
    inverse, spread = sb(f"{name}_inverse", [DC + 1, 2, R]), sb(f"{name}_spread", [DC, 2, R])
    oT = sb(f"{name}_oT", [DC + 1, H, TB, S])
    LEAD = 3 if context_norm else 2
    extra = ("keys_0", "keys_1", "k_high", "k_low", "q_low")
    if context_norm:
        raw = sb(f"{name}_raw", [LP, SLOTS, LC, DC + 1])
        cstat = sb(f"{name}_cstat", [LP, 2, 4, LC])
        square = sb(f"{name}_square", [LP, 2, LC, DC])
        half = sb(f"{name}_half", [LP, LC])
        extra = ("sum", "mean", "centred", "squared", "variance", "deviation", "rstd", "normal", "turned", "kT_kept")
    QUERIES_AT, TURN_AT, SHIFT_AT = 0, 3, 6
    SPREAD_AT, PROJECT_AT = (1, 3) if context_norm else (2, 8)
    with stage(nc, name, *[f"context_{u}" for u in range(SLOTS)], "set", "q", "q_kept", "scores", "copied",
               "part_max", "joined", "top_turned", "negmax", "diag", "minus_max", "shifted", "probs", "mixed",
               "inverse", "spread", "spread_kept", "normal_o", "projected", "added", *extra) as (block, s):
        context = [s[f"context_{u}"] for u in range(SLOTS)]

        def units(unit):
            def step(i):
                for u in range(SLOTS):
                    def exists(d):
                        return not (isinstance(i, int) and not 0 <= SLOTS * i + u + d < B)
                    unit(i, u, exists)
            return step

        @block.sync
        def _(sp):
            def load(i, u):
                sp.dma_start((raw if context_norm else tok)[:, u, :, :], g.ctx[SLOTS * i + u, :, :, :])\
                    .then_inc(context[u], 16)

            def load_keys(i, u):
                sp.dma_start(kT[:, u % 2, :, :], g.ctxT[SLOTS * i + u, 0:DC, :, :]).then_inc(s[f"keys_{u % 2}"], 16)

            if split:
                load_keys(0, 0)
                load_keys(0, 1)
            for u in range(SLOTS):
                load(0, u)
            if split:
                for u in range(2, SLOTS):
                    sp.wait_ge(s["k_low"], u - 1)
                    load_keys(0, u)
            with sp.Fori(0, STEPS - 1) as i:
                for u in range(SLOTS):
                    if split:
                        sp.wait_ge(s["k_low"], SLOTS * i + u + 3)
                        load_keys(i + 1, u)
                    sp.wait_ge(s["centred"] if context_norm else s["mixed"], SLOTS * i + u + 1)
                    load(i + 1, u)

        @block.tensor
        def _(pe):
            def queries(n):
                for h in range(H):
                    last = nc.tensor.matmul(g.ps[0:KQ, 6, h * S:(h + 1) * S], wqk(h), g.sequence_of(g.xnT, n),
                                            start=True, stop=q_row is None)
                    if q_row is not None:
                        last = nc.tensor.matmul(g.ps[0:KQ, 6, 0:S], q_row[:], g.ones[0:1, 0:S], start=False,
                                                stop=True)
                last.then_inc(s["q"], 1)

            def turn_context(n, u):
                pe.wait_ge(s["normal"], n + 1)
                pe.wait_ge(s["q_kept"], n + 1)
                for j in range(KJ):
                    if j == 2:
                        pe.wait_ge(s["kT_kept"], KJ * n + 1)
                    for c in range(CJ):
                        last = nc.tensor.transpose(g.ps[0:DC + 1, 7 - j % 2, c * LP:(c + 1) * LP],
                                                   tok[:, u, j * CJ + c, :], g.ident[0:LP, 0:LP])
                    last.then_inc(s["turned"], 1)
                pe.wait_ge(s["kT_kept"], KJ * n + KJ)

            def scores(n, i, u, b):
                k = NS * n + b
                if b == 0:
                    pe.wait_ge(s["q_kept"], n + 1)
                    if context_norm:
                        pe.wait_ge(s["kT_kept"], KJ * n + KJ)
                    else:
                        pe.wait_ge(s["q_low"], n + 1)
                        pe.wait_ge(s["k_low"], n + 1)
                if not (isinstance(k, int) and k < RING):
                    pe.wait_ge(s["copied"], k - RING + 1)
                if split:
                    out = g.ps[0:LP, b % RING, 0:R]
                    nc.tensor.matmul(out, k_high[:, u % 2, b, :], qT[:, u % 2, :], start=True, stop=False)
                    nc.tensor.matmul(out, k_high[:, u % 2, b, :], q_low[:, u % 2, :], start=False, stop=False)
                    nc.tensor.matmul(out, k_low[:, u % 2, b, :], qT[:, u % 2, :], start=False, stop=True)\
                        .then_inc(s["scores"], 1)
                    return
                for c in range(CB):
                    last = nc.tensor.matmul(g.ps[0:LP, b % RING, c * R:(c + 1) * R], kT[:, u, b * CB + c, :],
                                            qT[:, u % 2, :], start=True, stop=True)
                last.then_inc(s["scores"], 1)

            def turn_top(n):
                pe.wait_ge(s["joined"], (PARTS - 1) * (n + 1) if PARTS > 1 else n + 1)
                for r in range(G):
                    last = nc.tensor.transpose(g.ps[0:P, 4, r * LP:(r + 1) * LP], top[:, 0, r * P:(r + 1) * P],
                                               g.ident[0:LP, 0:LP])
                last.then_inc(s["top_turned"], 1)

            def minus_max(n, u):
                pe.wait_ge(s["diag"], n + 1)
                nc.tensor.matmul(g.ps[0:LP, 4, 0:R], g.ones[0:RG, 0:LP],
                                 diag[:, u % 2, :, :].rearrange("p r c -> p (r c)"), start=True, stop=True)\
                    .then_inc(s["minus_max"], 1)

            def mix(n, i, u, c):
                if c == 0 and split:
                    pe.wait_ge(context[u], 16 * i + 16)
                if c == 0 and not (isinstance(n, int) and n < 2):
                    pe.wait_ge(s["normal_o"], n - 1)
                if c % CE == 0:
                    pe.wait_ge(s["probs"], EXPS * n + c // CE + 1)
                last = nc.tensor.matmul(g.ps[0:DC + 1, 3 + 2 * (u % 2), 0:R], tok[:, u, c, :], sc[:, u % 2, c, :],
                                        start=(c == 0), stop=(c == LC - 1))
                if c == LC - 1:
                    last.then_inc(s["mixed"], 1)

            def spread_inverse(n, u):
                pe.wait_ge(s["inverse"], n + 1)
                nc.tensor.matmul(g.ps[0:DC, 7, 0:R], g.ones[DC:DC + 1, 0:DC], inverse[DC:DC + 1, u % 2, :],
                                 start=True, stop=True).then_inc(s["spread"], 1)

            def project(n):
                pe.wait_ge(s["normal_o"], n + 1)
                y = g.ps[0:P, 7, 0:D]
                nc.tensor.matmul(y, g.ones[0:1, 0:P], out_row, start=True, stop=False)
                for h in range(H):
                    wt = wvo(h)
                    last = nc.tensor.matmul(y, oT[0:wt.shape[0], h, :, :].rearrange("p b t -> p (b t)"), wt,
                                            start=False, stop=(h == H - 1))
                last.then_inc(s["projected"], 1)

            def unit(i, u, exists):
                n = SLOTS * i + u
                v = (u + 1) % SLOTS
                for b in range(NS):
                    if exists(1):
                        scores(n + 1, i + (u + 1) // SLOTS, v, b)
                for c in range(LC):
                    if c == QUERIES_AT and u % TB == 1 and not (isinstance(i, int) and i == 0 and u == 1):
                        pe.wait_ge(s["added"], (SLOTS // TB) * i + u // TB)
                    mix(n, i, u, c)
                    if c == QUERIES_AT and exists(2):
                        if split:
                            pe.wait_ge(s["q_low"], n + 2)
                        queries(n + 2)
                        if context_norm:
                            turn_context(n + 2, (u + 2) % SLOTS)
                    if c == SPREAD_AT and exists(-1):
                        spread_inverse(n - 1, (u - 1) % SLOTS)
                    if c == PROJECT_AT and u % TB == 0 and exists(-1):
                        project(n - 1)
                    if c == TURN_AT and exists(1):
                        turn_top(n + 1)
                    if c == SHIFT_AT and exists(1):
                        minus_max(n + 1, v)

            pe.wait_ge(s["set"], 4 if context_norm else 1)
            for n in range(2):
                if n:
                    pe.wait_ge(s["q_low"] if split else s["q_kept"], n)
                queries(n)
                if context_norm:
                    turn_context(n, n)
            for b in range(NS):
                scores(0, 0, 0, b)
            turn_top(0)
            minus_max(0, 0)
            over_steps(pe, units(unit))
            pe.wait_ge(s["normal_o"], B - 1)
            spread_inverse(B - 1, SLOTS - 1)
            project(B - 1)

        @block.gpsimd
        def _(pool):
            def centre(n, u):
                pool.wait_ge(s["mean"], n + 1)
                nc.gpsimd.tensor_tensor(tok[:, u, :, 0:DC], raw[:, u, :, 0:DC], over(cstat[:, u % 2, 1, :], DC),
                                        ALU.add).then_inc(s["centred"], 1)

            def scale(n, u):
                pool.wait_ge(s["deviation"], n + 1)
                nc.gpsimd.tensor_tensor(cstat[:, u % 2, 3, :], cstat[:, u % 2, 2, :], half[:], ALU.pow)\
                    .then_inc(s["rstd"], 1)
                pool.wait_ge(s["rstd"], n + 1)
                nc.gpsimd.tensor_tensor(tok[:, u, :, 0:DC], tok[:, u, :, 0:DC], over(cstat[:, u % 2, 3, :], DC),
                                        ALU.mult).then_inc(s["normal"], 1)

            def low_keys(n, u):
                pool.wait_ge(s["k_high"], n + 1)
                nc.gpsimd.tensor_tensor(k_low[:, u % 2, :, :], kT[:, u % 2, :, :], k_high[:, u % 2, :, :],
                                        ALU.subtract).then_inc(s["k_low"], 1)

            def diagonal(n, u):
                pool.wait_ge(s["negmax"], n + 1)
                nc.gpsimd.tensor_tensor(diag[:, u % 2, :, :], under(g.ident[0:RG, 0:RG], G),
                                        over(negmax[:, u % 2, :], RG), ALU.mult).then_inc(s["diag"], 1)

            def unit(i, u, exists):
                n = SLOTS * i + u
                if context_norm and exists(LEAD):
                    centre(n + LEAD, (u + LEAD) % SLOTS)
                if split and exists(2):
                    low_keys(n + 2, u + 2)
                if exists(1):
                    diagonal(n + 1, (u + 1) % SLOTS)
                if context_norm and exists(LEAD):
                    scale(n + LEAD, (u + LEAD) % SLOTS)

            link = in_order(pool, s["set"])
            link(nc.gpsimd.memset(oT[DC:DC + 1, :, :, :], 1.0))
            if context_norm:
                link(nc.gpsimd.memset(tok[:, :, :, DC:DC + 1], 1.0))
                link(nc.gpsimd.memset(half[:], -0.5))
                link(nc.gpsimd.memset(top[:, :, R:P], 0.0))
                for n in range(LEAD):
                    centre(n, n)
                    scale(n, n)
            if split:
                low_keys(0, 0)
                low_keys(1, 1)
            diagonal(0, 0)
            over_steps(pool, units(unit))

        @block.scalar
        def _(act):
            def keep_queries(n, u):
                act.wait_ge(s["q"], n + 1)
                nc.scalar.copy(qT[:, u % 2, :], g.ps[0:KQ, 6, 0:R]).then_inc(s["q_kept"], 1)

            def high_keys(i, u):
                act.wait_ge(s[f"keys_{u % 2}"], 16 * (SLOTS // 2 * i + u // 2) + 16)
                nc.scalar.copy(k_high[:, u % 2, :, :], kT[:, u % 2, :, :]).then_inc(s["k_high"], 1)

            def squares(n, u):
                act.wait_ge(s["centred"], n + 1)
                nc.scalar.activation(square[:, u % 2, :, :], tok[:, u, :, 0:DC], ACT.Square)\
                    .then_inc(s["squared"], 1)

            def keep_keys(n, u):
                for j in (0, 2):
                    act.wait_ge(s["turned"], KJ * n + j + 1)
                    if j:
                        act.wait_ge(s["kT_kept"], KJ * n + 2)
                    nc.scalar.copy(kT[:, u, CJ * j:CJ * j + CJ, :].rearrange("p c k -> p (c k)"),
                                   g.ps[0:DC + 1, 7, 0:LJ]).then_inc(s["kT_kept"], 1)

            def keep_scores(n, u, b):
                act.wait_ge(s["scores"], NS * n + b + 1)
                nc.scalar.copy(sc[:, u % 2, b * CB:(b + 1) * CB, :].rearrange("p c r -> p (c r)"),
                               g.ps[0:LP, b % RING, 0:CB * R]).then_inc(s["copied"], 1)

            def exponentials(n, u, j):
                act.wait_ge(s["shifted"], EXPS * n + j + 1)
                part = sc[:, u % 2, j * CE:(j + 1) * CE, :]
                nc.scalar.activation(part, part, ACT.Exp).then_inc(s["probs"], 1)

            def keep_spread(n, u):
                act.wait_ge(s["spread"], n + 1)
                nc.scalar.copy(spread[:, u % 2, :], g.ps[0:DC, 7, 0:R]).then_inc(s["spread_kept"], 1)

            def unit(i, u, exists):
                n = SLOTS * i + u
                v = (u + 1) % SLOTS
                for b in range(NS):
                    if exists(1):
                        keep_scores(n + 1, v, b)
                    if EXPS > EARLY and b % (NS // (EXPS - EARLY)) == 1:
                        exponentials(n, u, EARLY + b // (NS // (EXPS - EARLY)))
                if split and exists(2):
                    high_keys(i, u + 2)
                if exists(2):
                    keep_queries(n + 2, (u + 2) % SLOTS)
                    if context_norm:
                        keep_keys(n + 2, (u + 2) % SLOTS)
                if exists(-1):
                    keep_spread(n - 1, (u - 1) % SLOTS)
                if context_norm and exists(LEAD):
                    squares(n + LEAD, (u + LEAD) % SLOTS)
                if exists(1):
                    for j in range(EARLY):
                        exponentials(n + 1, v, j)

            if context_norm:
                for n in range(LEAD):
                    squares(n, n)
            for n in range(2):
                keep_queries(n, n)
                if context_norm:
                    keep_keys(n, n)
                else:
                    high_keys(0, n)
            for b in range(NS):
                keep_scores(0, 0, b)
            for j in range(EARLY):
                exponentials(0, 0, j)
            over_steps(act, units(unit))
            keep_spread(B - 1, SLOTS - 1)

        @block.vector
        def _(dve):
            def low_queries(n, u):
                dve.wait_ge(s["q_kept"], n + 1)
                nc.vector.tensor_tensor(q_low[:, u % 2, :], g.ps[0:KQ, 6, 0:R], qT[:, u % 2, :], ALU.subtract)\
                    .then_inc(s["q_low"], 1)

            def mean(n, u, i):
                dve.wait_ge(context[u], 16 * i + 16)
                nc.vector.tensor_reduce(cstat[:, u % 2, 0, :], raw[:, u, :, 0:DC], AX_X, ALU.add)\
                    .then_inc(s["sum"], 1)
                dve.wait_ge(s["sum"], n + 1)
                nc.vector.tensor_scalar(cstat[:, u % 2, 1, :], cstat[:, u % 2, 0, :], -1.0 / DC, None, ALU.mult)\
                    .then_inc(s["mean"], 1)

            def deviation(n, u):
                dve.wait_ge(s["squared"], n + 1)
                nc.vector.tensor_reduce(cstat[:, u % 2, 0, :], square[:, u % 2, :, :], AX_X, ALU.add)\
                    .then_inc(s["variance"], 1)
                dve.wait_ge(s["variance"], n + 1)
                nc.vector.tensor_scalar(cstat[:, u % 2, 2, :], cstat[:, u % 2, 0, :], 1.0 / DC, EPS, ALU.mult,
                                        ALU.add).then_inc(s["deviation"], 1)

            def keep_keys(n, u):
                dve.wait_ge(s["turned"], KJ * n + 2)
                dve.wait_ge(s["kT_kept"], KJ * n + 1)
                nc.vector.tensor_copy(kT[:, u, CJ:2 * CJ, :].rearrange("p c k -> p (c k)"),
                                      g.ps[0:DC + 1, 6, 0:LJ]).then_inc(s["kT_kept"], 1)

            def part_max(n, u, j):
                dve.wait_ge(s["copied"], NS * n + NP * (j + 1))
                last = nc.vector.tensor_reduce(top[:, j, 0:R],
                                               sc[:, u % 2, j * CP:(j + 1) * CP, :].rearrange("p c r -> p r c"),
                                               AX_X, ALU.max)
                if PARTS == 1:
                    last.then_inc(s["joined"], 1)
                else:
                    last.then_inc(s["part_max"], 1)

            def join_max(n, j):
                dve.wait_ge(s["part_max"], PARTS * n + j + 1)
                if j > 1:
                    dve.wait_ge(s["joined"], (PARTS - 1) * n + j - 1)
                nc.vector.tensor_tensor(top[:, 0, 0:R], top[:, 0, 0:R], top[:, j, 0:R], ALU.max).then_inc(s["joined"], 1)

            def query_max(n, u):
                dve.wait_ge(s["top_turned"], n + 1)
                nc.vector.tensor_reduce(negmax[:, u % 2, :],
                                        g.ps[0:RG, 4, 0:G * LP].rearrange("p (r k) -> p r k", r=G), AX_X, ALU.max,
                                        negate=True).then_inc(s["negmax"], 1)

            def shift(n, u, j):
                if j == 0:
                    dve.wait_ge(s["minus_max"], n + 1)
                part = sc[:, u % 2, j * CE:(j + 1) * CE, :]
                nc.vector.tensor_tensor(part, part, under(g.ps[0:LP, 4, 0:R], CE), ALU.add).then_inc(s["shifted"], 1)

            def invert(n, u):
                dve.wait_ge(s["mixed"], n + 1)
                nc.vector.reciprocal(inverse[DC:DC + 1, u % 2, :], g.ps[DC:DC + 1, 3 + 2 * (u % 2), 0:R])\
                    .then_inc(s["inverse"], 1)

            def normalize_mixed(n, u):
                dve.wait_ge(s["spread_kept"], n + 1)
                nc.vector.tensor_tensor(oT[0:DC, :, u % TB, :],
                                        g.ps[0:DC, 3 + 2 * (u % 2), 0:R].rearrange("p (h t) -> p h t", h=H),
                                        spread[:, u % 2, :].rearrange("p (h t) -> p h t", h=H), ALU.mult)\
                    .then_inc(s["normal_o"], 1)

            def add(t):
                dve.wait_ge(s["projected"], t + 1)
                nc.vector.tensor_tensor(g.x[:, t, :], g.x[:, t, :], g.ps[0:P, 7, 0:D], ALU.add)\
                    .then_inc(s["added"], 1)

            def unit(i, u, exists):
                n = SLOTS * i + u
                v, z = (u + 1) % SLOTS, (u - 1) % SLOTS
                if exists(-1):
                    invert(n - 1, z)
                if context_norm and exists(LEAD):
                    mean(n + LEAD, (u + LEAD) % SLOTS, i + (u + LEAD) // SLOTS)
                if exists(1):
                    part_max(n + 1, v, 0)
                    for j in range(1, PARTS):
                        part_max(n + 1, v, j)
                        join_max(n + 1, j)
                if context_norm and exists(2):
                    keep_keys(n + 2, (u + 2) % SLOTS)
                if split and exists(2):
                    low_queries(n + 2, (u + 2) % SLOTS)
                if exists(-1):
                    normalize_mixed(n - 1, z)
                if context_norm and exists(LEAD):
                    deviation(n + LEAD, (u + LEAD) % SLOTS)
                if exists(1):
                    query_max(n + 1, v)
                    for j in range(EXPS):
                        shift(n + 1, v, j)
                if exists(-1) and u % TB == 0:
                    add((SLOTS // TB) * i + u // TB - 1)

            if context_norm:
                for n in range(LEAD):
                    mean(n, n, 0)
                    deviation(n, n)
                for n in range(2):
                    keep_keys(n, n)
            else:
                low_queries(0, 0)
                low_queries(1, 1)
            for j in range(PARTS):
                part_max(0, 0, j)
                if j:
                    join_max(0, j)
            query_max(0, 0)
            for j in range(EXPS):
                shift(0, 0, j)
            over_steps(dve, units(unit))
            invert(B - 1, SLOTS - 1)
            normalize_mixed(B - 1, SLOTS - 1)
            add(T - 1)


def plain_cross(layer):
    def sublayer(nc, g, w, sb):
        H, DH = 8, 64
        name, src = f"x{layer}", f"L{layer}_xattn"
        wqT, wo = (sb(f"{name}_{n}", [DH, H, D]) for n in ("wqT", "wo"))
        wkT, wvT = (sb(f"{name}_{n}", [DH, H, DC]) for n in ("wkT", "wvT"))
        bo = sb(f"{name}_bo", [1, D])
        normalize(nc, g, f"{name}_norm", g.x, [
            (wqT[:], w[f"{src}_WqT"].rearrange("(h d) c -> d h c", d=DH)),
            (wkT[:], w[f"{src}_WkT"].rearrange("(h d) c -> d h c", d=DH)),
            (wvT[:], w[f"{src}_WvT"].rearrange("(h d) c -> d h c", d=DH)),
            (wo[:], w[f"{src}_Wo"].rearrange("(h d) c -> d h c", d=DH)), (bo[:], row(w[f"{src}_bo"]))])
        wqk, wvo = sb(f"{name}_wqk", [D, H, DC]), sb(f"{name}_wvo", [DC, H, D])
        with stage(nc, f"{name}_weights", "made", "kept") as (block, s):
            @block.tensor
            def _(pe):
                for h in range(H):
                    last = nc.tensor.matmul(g.ps[:, h // GH, (h % GH) * DC:(h % GH + 1) * DC], wqT[:, h, :],
                                            wkT[:, h, :], start=True, stop=True)
                    if h % GH == GH - 1:
                        last.then_inc(s["made"], 1)
                for h in range(H):
                    last = nc.tensor.matmul(g.ps[0:DC, 2 + h // GH, (h % GH) * D:(h % GH + 1) * D], wvT[:, h, :],
                                            wo[:, h, :], start=True, stop=True)
                    if h % GH == GH - 1:
                        last.then_inc(s["made"], 1)

            @block.scalar
            def _(act):
                for n in range(2):
                    act.wait_ge(s["made"], n + 1)
                    nc.scalar.mul(wqk[:, GH * n:GH * n + GH, :],
                                  g.ps[:, n, 0:GH * DC].rearrange("p (h c) -> p h c", h=GH), DH ** -0.5)\
                        .then_inc(s["kept"], 1)

            @block.vector
            def _(dve):
                for n in range(2):
                    dve.wait_ge(s["made"], 2 + n + 1)
                    nc.vector.tensor_copy(wvo[:, GH * n:GH * n + GH, :],
                                          g.ps[0:DC, 2 + n, :].rearrange("p (h c) -> p h c", h=GH))\
                        .then_inc(s["kept"], 1)
        cross_attend(nc, g, w, sb, name, H, lambda h: wqk[:, h, :], lambda h: wvo[:, h, :], bo[:])
    return sublayer


def normed_cross(nc, g, w, sb):
    name = "x0"
    wk, wv = sb("x0_wk", [DC, D]), sb("x0_wv", [DC, D])
    wkT, wvT = sb("x0_wkT", [D, DC + 1]), sb("x0_wvT", [D, DC + 1])
    wqT, wo = sb("x0_wqT", [D, D]), sb("x0_wo", [D, D])
    g1, b1 = sb("x0_g1", [D, 1]), sb("x0_b1", [D, 1])
    g2, b2 = sb("x0_g2", [D, DC]), sb("x0_b2", [DC, 1])
    cols = sb("x0_cols", [D, 3])
    bo = sb("x0_bo", [1, D])
    normalize(nc, g, "x0_norm", g.x, [
        (wk[:], w["L0_xattn_Wk"]), (wv[:], w["L0_xattn_Wv"]), (wkT[:, 0:DC], w["L0_xattn_WkT"]),
        (wvT[:, 0:DC], w["L0_xattn_WvT"]), (wqT[:], w["L0_xattn_WqT"]), (wo[:], w["L0_xattn_Wo"]),
        (g1[:], column(w["L0_xattn_ln1_g"])), (b1[:], column(w["L0_xattn_ln1_b"])),
        (g2[:], rows(w["L0_xattn_ln2_g"], D)), (b2[:], column(w["L0_xattn_ln2_b"])),
        *[(cols[:, n:n + 1], column(w[f"L0_xattn_{b}"])) for n, b in enumerate(("bq", "bk", "bv"))],
        (bo[:], row(w["L0_xattn_bo"]))], turn=False)
    normalize(nc, g, "x0_norm_again", g.xn, [])
    wqk, wvo, wq_row = sb("x0_wqk", [D, DC + 1]), sb("x0_wvo", [DC + 1, D]), sb("x0_wq_row", [1, DC + 1])
    with stage(nc, "x0_weights", "made", "kept", "steps", "mixed", "mixed_kept") as (block, s):
        @block.tensor
        def _(pe):
            nc.tensor.matmul(g.ps[:, 0, 0:1], wk[:], b2[:], start=True, stop=True)
            nc.tensor.matmul(g.ps[:, 0, 1:2], wv[:], b2[:], start=True, stop=True).then_inc(s["made"], 1)
            pe.wait_ge(s["kept"], 1)
            nc.tensor.matmul(g.ps[:, 1, 0:DC + 1], wqT[:], wkT[:], start=True, stop=True).then_inc(s["mixed"], 1)
            nc.tensor.matmul(g.ps[0:DC + 1, 2, 0:D], wvT[:], wo[:], start=True, stop=True).then_inc(s["mixed"], 1)
            pe.wait_ge(s["mixed_kept"], 1)
            nc.tensor.matmul(g.ps[0:1, 3, 0:DC + 1], cols[:, 0:1], wkT[:], start=True, stop=False)
            nc.tensor.matmul(g.ps[0:1, 3, 0:DC + 1], b1[:], wqk[:], start=False, stop=True).then_inc(s["mixed"], 1)

        @block.vector
        def _(dve):
            link = in_order(dve, s["steps"])
            dve.wait_ge(s["made"], 1)
            link(nc.vector.tensor_tensor(wkT[:, DC:DC + 1], g.ps[:, 0, 0:1], cols[:, 1:2], ALU.add))
            link(nc.vector.tensor_tensor(wvT[:, DC:DC + 1], g.ps[:, 0, 1:2], cols[:, 2:3], ALU.add))
            link(nc.vector.tensor_tensor(wkT[:, 0:DC], wkT[:, 0:DC], g2[:], ALU.mult))
            link(nc.vector.tensor_tensor(wvT[:, 0:DC], wvT[:, 0:DC], g2[:], ALU.mult))
            nc.vector.tensor_scalar(wkT[:], wkT[:], D ** -0.5, None, ALU.mult).then_inc(s["kept"], 1)
            dve.wait_ge(s["mixed"], 1)
            nc.vector.tensor_copy(wqk[:], g.ps[:, 1, 0:DC + 1]).then_inc(s["mixed_kept"], 1)
            dve.wait_ge(s["mixed"], 3)
            link(nc.vector.tensor_copy(wq_row[:], g.ps[0:1, 3, 0:DC + 1]))
            link(nc.vector.tensor_scalar(wqk[:], wqk[:], g1[:, 0:1], None, ALU.mult))
            link(nc.vector.tensor_copy(wvo[:], g.ps[0:DC + 1, 2, 0:D]))
    cross_attend(nc, g, w, sb, name, 1, lambda h: wqk[:], lambda h: wvo[:], bo[:], context_norm=True, q_row=wq_row)


def sparse_scores(nc, g, w, sb, name, wqk, mean_T):
    H, KTOP = 4, 32
    R, RG, G, KJ = H * S, P, 2, 3
    HG = RG // S
    CJ = LC // KJ
    LJ = CJ * LP
    ROUNDS = KTOP // 8
    kT = sb(f"{name}_kT", [DC + 1, TB, LC, LP])
    tok = sb(f"{name}_tok", [LP, TB, LC, DC + 1])
    qa = sb(f"{name}_qa", [DC + 1, TB, R])
    rest, kept = sb(f"{name}_rest", [RG, TB, G, L]), sb(f"{name}_kept", [RG, TB, G, L])
    best = sb(f"{name}_best", [RG, TB, G, ROUNDS, 8])
    best_exp = sb(f"{name}_best_exp", [RG, G, KTOP])
    negmax, sums = sb(f"{name}_negmax", [RG, TB, G]), sb(f"{name}_sums", [RG, TB, G])
    share = sb(f"{name}_share", [RG, G])
    pick, which = sb(f"{name}_pick", [RG, G, S]), sb(f"{name}_which", [RG, S])
    weights = sb(f"{name}_weights", [LP, TB, LC, S])
    tick = sb(f"{name}_tick", [1, 16])
    HALVES = ((0, 8), (8, LC))
    with stage(nc, name, "keys_0", "keys_1", "tokens_0", "tokens_1", "set", "q", "q_kept", "scores", "best", "rest_0", "rest_1",
               "negmax", "exps", "best_summed", "rest_exps", "chosen", "inverse", "pick", "weights", "weights_kept", "mixed",
               "mixed_kept") as (block, s):
        keys, tokens = (s["keys_0"], s["keys_1"]), (s["tokens_0"], s["tokens_1"])
        rest_made = (s["rest_0"], s["rest_1"])

        def units(unit):
            def step(i):
                for b in range(TB):
                    unit(i, b, lambda d, b=b: not (isinstance(i, int) and not 0 <= TB * i + b + d < B))
            return step

        def over_tiles(eng, step):
            step(0)
            with eng.Fori(1, T - 1) as i:
                step(i)
            step(T - 1)

        @block.sync
        def _(sp):
            def load_keys(n, b):
                sp.dma_start(kT[0:DC, b, :, :], g.ctxT[n, 0:DC, :, :]).then_inc(keys[b], 16)
                sp.dma_start(kT[DC:DC + 1, b, :, :], g.key_bias[n, :, :, :]).then_inc(keys[b], 16)

            def load_tokens(n, b):
                sp.dma_start(tok[:, b, :, :], g.ctx[n, :, :, :]).then_inc(tokens[b], 16)

            def ahead(n, b):
                sp.wait_ge(s["mixed"], n)
                load_tokens(n + 1, 1 - b)
                sp.wait_ge(s["scores"], G * n + 2 * G)
                load_keys(n + 3, 1 - b)

            for n in range(TB):
                load_keys(n, n)
                load_tokens(n, n)
            for n in range(TB):
                sp.wait_ge(s["scores"], G * n + G)
                load_keys(n + 2, n)
            with sp.Fori(0, T - 2) as i:
                ahead(TB * i + 1, 1)
                ahead(TB * i + 2, 0)
            for n in (B - 3, B - 2):
                sp.wait_ge(s["mixed"], n)
                load_tokens(n + 1, (n + 1) % 2)

        @block.tensor
        def _(pe):
            def queries(tile):
                for h in range(H):
                    last = nc.tensor.matmul(g.ps[0:DC, 6, h * P:(h + 1) * P], wqk(h), tile, start=True, stop=True)
                last.then_inc(s["q"], 1)

            def scores(i, b, r):
                n = TB * i + b
                if b == 0 and r == 0:
                    pe.wait_ge(s["q_kept"], i + 1)
                if r == 0:
                    pe.wait_ge(keys[b], 32 * i + 32)
                if not (isinstance(i, int) and n == 0):
                    pe.wait_ge(s["exps"], G * n - G + r + 1)
                for j in range(KJ):
                    last = nc.tensor.matmul(g.ps[0:RG, KJ * r + j, 0:LJ], qa[:, b, r * RG:(r + 1) * RG],
                                            kT[:, b, j * CJ:(j + 1) * CJ, :].rearrange("p c k -> p (c k)"),
                                            start=True, stop=True)
                last.then_inc(s["scores"], 1)

            def mix(i, b, first=False):
                n = TB * i + b
                pe.wait_ge(s["pick"], G * n + G)
                pe.wait_ge(s["chosen"], G * n + G)
                if not first:
                    pe.wait_ge(s["mixed_kept"], n)
                for half, (lo, hi) in enumerate(HALVES):
                    for c in range(lo, hi):
                        for r in range(G):
                            last = nc.tensor.matmul(g.ps[0:LP, 6 + half, (c - lo) * S:(c - lo) * S + S],
                                                    kept[:, b, r, c * LP:(c + 1) * LP], pick[:, r, :],
                                                    start=(r == 0), stop=(r == G - 1))
                    last.then_inc(s["weights"], 1)
                pe.wait_ge(tokens[b], 16 * i + 16)
                pe.wait_ge(s["weights_kept"], 2 * n + 2)
                for c in range(LC):
                    last = nc.tensor.matmul(g.ps[0:DC, 7, 256:256 + S], tok[:, b, c, 0:DC],
                                            weights[:, b, c, :], start=(c == 0), stop=(c == LC - 1))
                last.then_inc(s["mixed"], 1)

            def unit(i, b, exists):
                if b == 1 and exists(1):
                    queries(g.next_tile(g.xnT, i))
                if exists(1):
                    scores(i + b, 1 - b, 0)
                    scores(i + b, 1 - b, 1)
                if exists(-1):
                    mix(i - 1 + b, 1 - b, first=isinstance(i, int) and i == 0)

            pe.wait_ge(s["set"], 4)
            queries(g.tile_of(g.xnT, 0))
            scores(0, 0, 0)
            scores(0, 0, 1)
            over_tiles(pe, units(unit))
            mix(T - 1, 1)

        @block.gpsimd
        def _(pool):
            def choose(i, b, exists):
                for r in range(G):
                    pool.wait_ge(s["exps"], G * (TB * i + b) + r + 1)
                    pool.wait_ge(s["rest_exps"], G * (TB * i + b) + r + 1)
                    nc.gpsimd.tensor_tensor(kept[:, b, r, :], kept[:, b, r, :], rest[:, b, r, :], ALU.subtract)\
                        .then_inc(s["chosen"], 1)

            nc.gpsimd.memset(qa[DC:DC + 1, :, :], 1.0).then_inc(s["set"], 1)
            pool.wait_ge(s["set"], 1)
            nc.gpsimd.memset(which[:], 0.0).then_inc(s["set"], 1)
            for n in range(HG):
                pool.wait_ge(s["set"], 2 + n)
                nc.gpsimd.affine_select(out=which[:], in_=which[:], compare_op=ALU.not_equal, fill=1.0 / H,
                                        base=-S * n, pattern=[[-1, S]], channel_multiplier=1).then_inc(s["set"], 1)
            over_tiles(pool, units(choose))

        @block.scalar
        def _(act):
            def keep_queries(i):
                act.wait_ge(s["q"], i + 1)
                nc.scalar.copy(qa[0:DC, :, :].rearrange("p b (h t) -> p h b t", h=H),
                               g.ps[0:DC, 6, 0:H * P].rearrange("p (h b t) -> p h b t", h=H, b=TB))\
                    .then_inc(s["q_kept"], 1)

            def exponentials(i, b, r):
                n = G * (TB * i + b) + r
                act.wait_ge(s["negmax"], n + 1)
                act.wait_ge(rest_made[r], ROUNDS * (TB * i + b) + 1)
                nc.scalar.activation(kept[:, b, r, :].rearrange("p (j l) -> p j l", j=KJ),
                                     g.ps[0:RG, KJ * r:KJ * r + KJ, 0:LJ], ACT.Exp,
                                     bias=negmax[:, b, r:r + 1]).then_inc(s["exps"], 1)

            def rest_exponentials(i, b, r):
                n = G * (TB * i + b) + r
                act.wait_ge(rest_made[r], ROUNDS * (TB * i + b) + ROUNDS)
                nc.scalar.activation(best_exp[:, r, :], best[:, b, r, :, :].rearrange("p k e -> p (k e)"), ACT.Exp,
                                     bias=negmax[:, b, r:r + 1], accum_out=sums[:, b, r:r + 1]).then_inc(s["best_summed"], 1)
                nc.scalar.activation(rest[:, b, r, :], rest[:, b, r, :], ACT.Exp,
                                     bias=negmax[:, b, r:r + 1]).then_inc(s["rest_exps"], 1)

            def keep_weights(i, b):
                for half, (lo, hi) in enumerate(HALVES):
                    act.wait_ge(s["weights"], 2 * (TB * i + b) + half + 1)
                    nc.scalar.copy(weights[:, b, lo:hi, :].rearrange("p c t -> p (c t)"),
                                   g.ps[0:LP, 6 + half, 0:(hi - lo) * S]).then_inc(s["weights_kept"], 1)

            def unit(i, b, exists):
                if b == 1 and exists(1):
                    keep_queries(i + 1)
                exponentials(i, b, 0)
                exponentials(i, b, 1)
                if exists(-1):
                    keep_weights(i - 1 + b, 1 - b)
                rest_exponentials(i, b, 0)
                rest_exponentials(i, b, 1)

            keep_queries(0)
            over_tiles(act, units(unit))
            keep_weights(T - 1, 1)

        @block.vector
        def _(dve):
            def search(i, b, after_round):
                first = G * (TB * i + b)
                left = [rest[:, b, r, :].rearrange("p (j l) -> p j l", j=KJ) for r in range(G)]
                for k in range(ROUNDS):
                    source = [g.ps[0:RG, KJ * r:KJ * r + KJ, 0:LJ] for r in range(G)] if k == 0 else left
                    for r in range(G):
                        if k == 0:
                            dve.wait_ge(s["scores"], first + r + 1)
                            if not (isinstance(i, int) and i == 0):
                                dve.wait_ge(s["chosen"], first + r - TB * G + 1)
                        else:
                            dve.wait_ge(rest_made[r], ROUNDS * (TB * i + b) + k)
                        nc.vector.memset(tick[:, 2 * k + r:2 * k + r + 1], 0.0)
                        nc.vector.max(best[:, b, r, k, :], source[r]).then_inc(s["best"], 1)
                    for r in range(G):
                        dve.wait_ge(s["best"], ROUNDS * first + G * k + r + 1)
                        if k == 0:
                            nc.vector.tensor_scalar(negmax[:, b, r:r + 1], best[:, b, r, 0, 0:1], -1.0, None,
                                                    ALU.mult).then_inc(s["negmax"], 1)
                        else:
                            nc.vector.memset(tick[:, 8 + 2 * k + r:9 + 2 * k + r], 0.0)
                        nc.vector.match_replace(left[r], best[:, b, r, k, :], source[r], 2 * NEG)\
                            .then_inc(rest_made[r], 1)
                    if k in after_round:
                        after_round[k]()

            def shares(i, b):
                n = TB * i + b
                dve.wait_ge(s["best_summed"], G * n + G)
                nc.vector.reciprocal(share[:], sums[:, b, :]).then_inc(s["inverse"], 1)
                dve.wait_ge(s["inverse"], n + 1)
                if not (isinstance(i, int) and n == 0):
                    dve.wait_ge(s["weights"], 2 * n)
                for r in range(G):
                    nc.vector.tensor_scalar(pick[:, r, :], which[:], share[:, r:r + 1], None, ALU.mult)\
                        .then_inc(s["pick"], 1)

            def keep_mixed(i, b):
                n = TB * i + b
                dve.wait_ge(s["mixed"], n + 1)
                nc.vector.tensor_copy(g.sequence_of(mean_T, n)[0:DC, :], g.ps[0:DC, 7, 256:256 + S])\
                    .then_inc(s["mixed_kept"], 1)

            def unit(i, b, exists):
                search(i, b, {0: lambda: shares(i - 1 + b, 1 - b), ROUNDS - 1: lambda: keep_mixed(i - 1 + b, 1 - b)}
                       if exists(-1) else {})

            over_tiles(dve, units(unit))
            shares(T - 1, 1)
            keep_mixed(T - 1, 1)


def mod_features(nc, g, w, sb):
    H, NS, F = 4, 64, 4 * D
    wqT, wkT = sb("x2_wqT", [32, H, D]), sb("x2_wkT", [32, H, DC])
    wv = sb("x2_wv", [DC, D])
    film = sb("x2_film", [D, 2, 2, D])
    film_b = sb("x2_film_b", [D, 4])
    cols = sb("x2_cols", [D, 6])
    gate = sb("x2_gate", [D, 1])
    w1, w2 = sb("x2_w1", [D, F]), sb("x2_w2", [128, F // 128, D])
    b1, b2 = sb("x2_b1", [128, F // 128]), sb("x2_b2", [1, D])
    ends = sb("x2_ends", [P, 2, D])
    mask_text, mask_keys = sb("x2_mask_text", [D, N], U8), sb("x2_mask_keys", [B, L], U8)
    key_bias = sb("x2_key_bias", [B, L])
    src = "L2_xattn_"
    vectors = ("g_norm_in", "b_norm_in", "g_ffn", "b_ffn", "D_skip", "log_dt")
    normalize(nc, g, "x2_norm", g.x, [
        (mask_keys[:], w["mask_keys"]), (mask_text[:], rows(w["mask_text"], D)),
        (wqT[:], w[src + "WqT"].rearrange("(h d) c -> d h c", h=H)),
        (wkT[:], w[src + "WkT"].rearrange("(h d) c -> d h c", h=H)), (wv[:], w[src + "Wv"]),
        (film[:, 0, :, :], w[src + "W_film_in"].rearrange("d (a e) -> d a e", a=2)),
        (film[:, 1, :, :], w[src + "W_film_out"].rearrange("d (a e) -> d a e", a=2)),
        (film_b[:], w[src + "film_b_cols"]),
        *[(cols[:, n:n + 1], column(w[src + v])) for n, v in enumerate(vectors)],
        (gate[:], rows(w[src + "mod_gate_row"], D)), (w1[:], w[src + "W1"]),
        (w2[:], w[src + "W2"].rearrange("(m p) d -> p m d", p=128)), (b1[:], w[src + "b1_cols"]),
        (b2[:], row(w[src + "b2"])), (ends[:, 0, :], rows(w[src + "g_norm_out"], P)),
        (ends[:, 1, :], rows(w[src + "b_norm_out"], P))])
    meanT = g.keyT
    with ExitStack() as own:
        part = lambda name, shape, dt=F32: own.enter_context(nc.sbuf_tensor(name, shape, dt))
        wqk = part("x2_wqk", [D, H, DC])
        with stage(nc, "x2_weights", "bias", "stored", "made", "kept") as (block, s):
            @block.vector
            def _(dve):
                nc.vector.tensor_scalar(key_bias[:], mask_keys[:], 1.0, -NEG, ALU.subtract, ALU.mult)\
                    .then_inc(s["bias"], 1)

            @block.sync
            def _(sp):
                sp.wait_ge(s["bias"], 1)
                sp.dma_start(g.key_bias.rearrange("b a c k -> b (a c k)"), key_bias[:]).then_inc(s["stored"], 16)
                sp.wait_ge(s["stored"], 16)

            @block.tensor
            def _(pe):
                for h in range(H):
                    last = nc.tensor.matmul(g.ps[:, 0, h * DC:(h + 1) * DC], wqT[:, h, :], wkT[:, h, :], start=True,
                                            stop=True)
                last.then_inc(s["made"], 1)

            @block.scalar
            def _(act):
                act.wait_ge(s["made"], 1)
                nc.scalar.mul(wqk[:], g.ps[:, 0, 0:H * DC].rearrange("p (h c) -> p h c", h=H), 32 ** -0.5)\
                    .then_inc(s["kept"], 1)
        sparse_scores(nc, g, w, part, "x2_top", lambda h: wqk[:, h, :], meanT)

    taps = sb("x2_taps", [D, S])
    with ExitStack() as own:
        part = lambda name, shape, dt=F32: own.enter_context(nc.sbuf_tensor(name, shape, dt))
        state_kernel(nc, g, w, part, cols, taps, NS)

    cT, filmT = sb("x2_cT", [D, N]), sb("x2_filmT", [D, 2, N])
    yT, uT = sb("x2_yT", [D, N]), sb("x2_uT", [D, N])
    with stage(nc, "x2_c", "c", "kept") as (block, s):
        @block.tensor
        def _(pe):
            for b in range(NB):
                nc.tensor.matmul(g.ps[:, b, 0:W], wv[:], meanT[0:DC, b * W:(b + 1) * W], start=True, stop=True)\
                    .then_inc(s["c"], 1)

        @block.vector
        def _(dve):
            for b in range(NB):
                dve.wait_ge(s["c"], b + 1)
                nc.vector.tensor_tensor(cT[:, b * W:(b + 1) * W], g.ps[:, b, 0:W], mask_text[:, b * W:(b + 1) * W],
                                        ALU.mult).then_inc(s["kept"], 1)
    normalize(nc, g, "x2_norm_in", g.xn, [], dst=g.work)
    modulate(nc, g, "x2_in", film[:, 0, :, :], film_b, 0, cT, filmT, gate, g.xnT, uT, cols[:, 0:1], cols[:, 1:2])
    with stage(nc, "x2_conv", "steps") as (block, s):
        @block.vector
        def _(dve):
            link = in_order(dve, s["steps"])
            u3, y3 = (a[:].rearrange("p (b t) -> p b t", t=S) for a in (uT, yT))
            link(nc.vector.tensor_scalar(yT[:], uT[:], taps[:, 0:1], None, ALU.mult))
            for m in range(1, S):
                link(nc.vector.scalar_tensor_tensor(out=y3[:, :, m:S], in0=u3[:, :, 0:S - m],
                                                    scalar=taps[:, m:m + 1], in1=y3[:, :, m:S],
                                                    op0=ALU.mult, op1=ALU.add))
    modulate(nc, g, "x2_out", film[:, 1, :, :], film_b, 2, cT, filmT, gate, yT, uT, None, None)
    add_turned(nc, g, "x2_add", uT, g.xn)
    normalize(nc, g, "x2_norm_ffn", g.xn, [], dst=g.work)
    with stage(nc, "x2_gain", "scaled") as (block, s):
        @block.vector
        def _(dve):
            nc.vector.tensor_scalar(g.xnT[:, 0:N], g.xnT[:, 0:N], cols[:, 2:3], cols[:, 3:4], ALU.mult, ALU.add)\
                .then_inc(s["scaled"], 1)
    jobs = [Expert([(w1[:, m * 128:(m + 1) * 128], b1[:, m:m + 1], None) for m in range(F // 128)],
                   [w2[:, m, :] for m in range(F // 128)], out_bias=b2[:])]
    experts(nc, g, "x2_ffn", sb, jobs, ACT.Gelu, g.xn)
    normalize(nc, g, "x2_norm_out", g.xn, [], turn=False, dst=g.work)
    with stage(nc, "x2_end", "steps") as (block, s):
        @block.vector
        def _(dve):
            link = in_order(dve, s["steps"])
            link(nc.vector.tensor_tensor(g.work[:], g.work[:], under(ends[:, 0, :], T), ALU.mult))
            link(nc.vector.tensor_tensor(g.x[:], g.x[:], under(ends[:, 1, :], T), ALU.add))
            link(nc.vector.tensor_tensor(g.x[:], g.x[:], g.work[:], ALU.add))


def modulate(nc, g, name, weights, film_b, first, cT, filmT, gate, srcT, dstT, gain, shift):
    with stage(nc, name, "film", "film_kept", "steps") as (block, s):
        @block.tensor
        def _(pe):
            for n in range(2 * NB):
                half, b = n // NB, n % NB
                nc.tensor.matmul(g.ps[:, n, 0:W], weights[:, half, :], cT[:, b * W:(b + 1) * W], start=True,
                                 stop=True).then_inc(s["film"], 1)

        @block.scalar
        def _(act):
            for n in range(2 * NB):
                half, b = n // NB, n % NB
                act.wait_ge(s["film"], n + 1)
                nc.scalar.activation(filmT[:, half, b * W:(b + 1) * W], g.ps[:, n, 0:W], ACT.Identity,
                                     bias=film_b[:, first + half:first + half + 1]).then_inc(s["film_kept"], 1)

        @block.vector
        def _(dve):
            link = in_order(dve, s["steps"])
            if gain is not None:
                link(nc.vector.tensor_scalar(dstT[:], srcT[:, 0:N], gain, shift, ALU.mult, ALU.add))
            else:
                link(nc.vector.tensor_copy(dstT[:], srcT[:, 0:N]))
            dve.wait_ge(s["film_kept"], NB)
            link(nc.vector.tensor_scalar(filmT[:, 0, :], filmT[:, 0, :], gate[:, 0:1], 1.0, ALU.mult, ALU.add))
            link(nc.vector.tensor_tensor(dstT[:], dstT[:], filmT[:, 0, :], ALU.mult))
            dve.wait_ge(s["film_kept"], 2 * NB)
            link(nc.vector.scalar_tensor_tensor(out=dstT[:], in0=filmT[:, 1, :], scalar=gate[:, 0:1], in1=dstT[:],
                                                op0=ALU.mult, op1=ALU.add))


def add_turned(nc, g, name, srcT, dst):
    with stage(nc, name, "turned", "added") as (block, s):
        @block.tensor
        def _(pe):
            for b in range(NB):
                for j in range(BT):
                    t = b * BT + j
                    last = nc.tensor.transpose(g.ps[0:P, b, j * D:(j + 1) * D], srcT[:, t * P:(t + 1) * P],
                                               g.ident[:])
                last.then_inc(s["turned"], 1)

        @block.vector
        def _(dve):
            for b in range(NB):
                dve.wait_ge(s["turned"], b + 1)
                part = dst[:, b * BT:(b + 1) * BT, :]
                nc.vector.tensor_tensor(part, part, g.ps[0:P, b, :].rearrange("p (j d) -> p j d", j=BT), ALU.add)\
                    .then_inc(s["added"], 1)


def state_kernel(nc, g, w, sb, cols, taps, NS):
    import math
    A, C = sb("s4_A", [D, 2, NS]), sb("s4_C", [D, 2, NS])
    z, r, t = sb("s4_z", [D, 2, NS]), sb("s4_r", [D, 2, NS]), sb("s4_t", [D, 4, NS])
    wave = sb("s4_wave", [D, 2, NS])
    dC, dt = sb("s4_dC", [D, 2, NS]), sb("s4_dt", [D, 1])
    base = sb("s4_base", [D, 2, NS])
    power = sb("s4_power", [D, 2, S, NS])
    prod = sb("s4_prod", [D, S, NS])
    TWO_PI = 2 * math.pi
    hi = 6.28125
    mid = float(int((TWO_PI - hi) * 2 ** 21)) / 2 ** 21
    lo = TWO_PI - hi - mid
    ROUND = 1.5 * 2.0 ** 23
    with stage(nc, "s4", "loads", "dt", "steps", "angles", "exps", "waves") as (block, s):
        @block.sync
        def _(sp):
            src = "L2_xattn_"
            load_all(sp, s["loads"], [(A[:, 0, :], w[src + "A_re"]), (A[:, 1, :], w[src + "A_im"]),
                                   (C[:, 0, :], w[src + "C_re"]), (C[:, 1, :], w[src + "C_im"])])

        @block.scalar
        def _(act):
            nc.scalar.activation(dt[:], cols[:, 5:6], ACT.Exp).then_inc(s["dt"], 1)
            act.wait_ge(s["angles"], 1)
            nc.scalar.activation(r[:, 0, :], z[:, 0, :], ACT.Exp).then_inc(s["exps"], 1)
            act.wait_ge(s["angles"], 2)
            nc.scalar.activation(wave[:], t[:, 0:2, :], ACT.Sin).then_inc(s["waves"], 1)

        @block.vector
        def _(dve):
            link = in_order(dve, s["steps"])
            dve.wait_ge(s["loads"], 64)
            dve.wait_ge(s["dt"], 1)
            nc.vector.tensor_scalar(z[:], A[:], dt[:, 0:1], None, ALU.mult).then_inc(s["angles"], 1)
            dve.wait_ge(s["angles"], 1)
            link(nc.vector.tensor_copy(t[:, 0, :], z[:, 1, :]))
            link(nc.vector.tensor_scalar(t[:, 2, :], t[:, 0, :], 1.0 / TWO_PI, ROUND, ALU.mult, ALU.add))
            link(nc.vector.tensor_scalar(t[:, 2, :], t[:, 2, :], ROUND, None, ALU.subtract))
            for part in (hi, mid, lo):
                link(nc.vector.scalar_tensor_tensor(out=t[:, 0, :], in0=t[:, 2, :], scalar=-part, in1=t[:, 0, :],
                                                    op0=ALU.mult, op1=ALU.add))
            link(nc.vector.tensor_scalar(t[:, 1, :], t[:, 0, :], math.pi / 2, None, ALU.add))
            link(nc.vector.tensor_scalar(t[:, 3, :], t[:, 1, :], math.pi, -TWO_PI, ALU.is_gt, ALU.mult))
            link(nc.vector.tensor_tensor(t[:, 1, :], t[:, 1, :], t[:, 3, :], ALU.add))
            link(nc.vector.tensor_scalar(t[:, 0:2, :], t[:, 0:2, :], 3.14159250259, -3.14159250259, ALU.min, ALU.max))
            nc.vector.tensor_scalar(z[:, 1, :], z[:, 1, :], 1.0, None, ALU.mult).then_inc(s["angles"], 1)
            dve.wait_ge(s["exps"], 1)
            dve.wait_ge(s["waves"], 1)
            link(nc.vector.tensor_tensor(base[:, 0, :], r[:, 0, :], wave[:, 1, :], ALU.mult))
            link(nc.vector.tensor_tensor(base[:, 1, :], r[:, 0, :], wave[:, 0, :], ALU.mult))

            def times(out, a, b, tmp, real_alone=False):
                link(nc.vector.tensor_tensor(out[0], a[0], b[0], ALU.mult))
                link(nc.vector.tensor_tensor(tmp, a[1], b[1], ALU.mult))
                link(nc.vector.tensor_tensor(out[0], out[0], tmp, ALU.subtract))
                if real_alone:
                    return
                link(nc.vector.tensor_tensor(out[1], a[0], b[1], ALU.mult))
                link(nc.vector.tensor_tensor(tmp, a[1], b[0], ALU.mult))
                link(nc.vector.tensor_tensor(out[1], out[1], tmp, ALU.add))

            pair = lambda a: (a[:, 0, :], a[:, 1, :])
            link(nc.vector.tensor_copy(t[:, 0:2, :], base[:]))
            link(nc.vector.tensor_scalar(t[:, 0, :], t[:, 0, :], -1.0, None, ALU.add))
            times(pair(z), pair(C), (t[:, 0, :], t[:, 1, :]), r[:, 1, :])
            link(nc.vector.tensor_tensor(t[:, 0, :], A[:, 0, :], A[:, 0, :], ALU.mult))
            link(nc.vector.tensor_tensor(t[:, 1, :], A[:, 1, :], A[:, 1, :], ALU.mult))
            link(nc.vector.tensor_tensor(t[:, 0, :], t[:, 0, :], t[:, 1, :], ALU.add))
            link(nc.vector.reciprocal(t[:, 0, :], t[:, 0, :]))
            link(nc.vector.tensor_scalar(t[:, 0, :], t[:, 0, :], 2.0, None, ALU.mult))
            link(nc.vector.tensor_tensor(t[:, 2, :], A[:, 0, :], t[:, 0, :], ALU.mult))
            link(nc.vector.tensor_tensor(t[:, 3, :], A[:, 1, :], t[:, 0, :], ALU.mult))
            link(nc.vector.tensor_scalar(t[:, 3, :], t[:, 3, :], -1.0, None, ALU.mult))
            times(pair(dC), pair(z), (t[:, 2, :], t[:, 3, :]), r[:, 1, :])
            link(nc.vector.tensor_copy(power[:, :, 0, :], dC[:]))
            n = 1
            while n < S:
                m = min(n, S - n)
                wide = lambda a, k: a[:, k, :].unsqueeze(1).to_broadcast([D, m, NS])
                times((power[:, 0, n:n + m, :], power[:, 1, n:n + m, :]),
                      (power[:, 0, 0:m, :], power[:, 1, 0:m, :]), (wide(base, 0), wide(base, 1)),
                      prod[:, 0:m, :], real_alone=n + m == S)
                if n + m < S:
                    times(pair(z), pair(base), pair(base), r[:, 1, :])
                    link(nc.vector.tensor_copy(base[:], z[:]))
                n += m
            link(nc.vector.tensor_reduce(taps[:], power[:, 0, :, :], AX_X, ALU.add))
            link(nc.vector.tensor_tensor(taps[:, 0:1], taps[:, 0:1], cols[:, 4:5], ALU.add))


SUBLAYERS = [wide_attention, normed_cross, shared_and_routed, biased_attention, plain_cross(1), capped_experts,
             scaled_attention, mod_features, small_experts, rotary_attention, plain_cross(3), adapted_experts]



def build(nc, w, out):
    with ExitStack() as ctx:
        def sb(name, shape, dt=F32):
            return ctx.enter_context(nc.sbuf_tensor(name, shape, dt))

        g = Chip()
        g.x = sb("x", [P, T, D])
        g.xn = sb("xn", [P, T, D])
        g.work, g.square = sb("work", [P, T, D]), sb("square", [P, T, D])
        g.xnT, g.workT, g.keyT = (sb(n, [D, N + P]) for n in ("xnT", "workT", "keyT"))
        g.stat = sb("stat", [P, 4, T])
        g.minus_half = sb("minus_half", [P, T])
        g.ident, g.ones = sb("ident", [128, 128]), sb("ones", [128, 128])
        g.ident_b = sb("ident_b", [128, 128], BF16)
        g.mask_any, g.mask_q = (sb(n, [P, BT, P], BF16) for n in ("mask_any", "mask_q"))
        g.ps = ctx.enter_context(nc.psum_tensor("ps", [128, 8, 512], F32))
        g.next_tile = lambda a, i: a[:, 0:N + P].rearrange("p (t c) -> p t c", c=P)[:, i + 1, :]
        g.ctx, g.ctxT, g.key_bias = w["ctx"], w["ctxT"], w["key_bias"]
        g.tile_of = lambda a, i: a[:, 0:N].rearrange("p (t c) -> p t c", c=P)[:, i, :]
        g.sequence_of = lambda a, i: a[:, 0:N].rearrange("p (b c) -> p b c", c=S)[:, i, :]
        g.block_of = lambda a, i: a[:, 0:N].rearrange("p (b c) -> p b c", c=W)[:, i, :]
        g.tiles_of = lambda a, i: a[:].rearrange("p (b j) d -> p b j d", j=BT)[:, i, :, :]
        g.block_gate = lambda a, i: a.rearrange("p (b j) -> p b j", j=BT)[:, i, :]
        build_constants(nc, g)
        with stage(nc, "start", "x_in", "set") as (block, s):
            @block.sync
            def _(sp):
                load_all(sp, s["x_in"], [(g.x[:], w["x"].rearrange("(t a) s d -> (a s) t d", a=TB))])

            @block.gpsimd
            def _(pool):
                nc.gpsimd.memset(g.minus_half[:], -0.5).then_inc(s["set"], 1)
                for padded in (g.xnT, g.workT, g.keyT):
                    nc.gpsimd.memset(padded[:, N:N + P], 0.0).then_inc(s["set"], 1)
        for sub in SUBLAYERS[FIRST_SUBLAYER:LAST_SUBLAYER]:
            with ExitStack() as own:
                sub(nc, g, w, lambda name, shape, dt=F32: own.enter_context(nc.sbuf_tensor(name, shape, dt)))
        with stage(nc, "end", "x_out") as (block, s):
            @block.sync
            def _(sp):
                sp.dma_start(out.rearrange("(t a) s d -> (a s) t d", a=TB), g.x[:]).then_inc(s["x_out"], 16)
                sp.wait_ge(s["x_out"], 16)


def laid_out(inputs):
    import numpy as np
    w = dict(inputs)
    wqkv = w.pop("L1_attn_Wqkv")
    w["L1_attn_WqT"] = wqkv[:, 0:D].T
    w["L1_attn_Wkv"] = wqkv[:, D:3 * D]
    dirs = w.pop("L1_attn_head_dirs")
    padded = np.zeros((8, 16), dirs.dtype)
    padded[:, 0:3] = dirs
    w["L1_attn_head_dirs_row"] = padded.reshape(-1)
    w["L1_attn_head_scales_row"] = np.repeat(w.pop("L1_attn_head_scales"), 16)
    w["L2_attn_bo4"] = np.tile(w.pop("L2_attn_bo"), 4)
    w["L3_attn_bo4"] = np.tile(w.pop("L3_attn_bo"), 4)
    for name in ("wqr", "wkr", "bqr", "bkr"):
        w[f"L3_attn_{name}_swapped"] = np.roll(w[f"L3_attn_{name}"], D // 2, axis=-1)
    inv = np.float32(1.0) / np.float32(10000.0) ** (np.arange(0, D, 2, dtype=np.float32) / np.float32(D))
    angle = (np.arange(S, dtype=np.float32)[:, None] * inv[None, :]).astype(np.float32)
    angle = np.tile(np.concatenate([angle, angle], axis=1).T, (1, TB))
    sign = np.where(np.arange(D) < D // 2, -1.0, 1.0)[:, None]
    w["rotary"] = np.stack([np.cos(angle), np.sin(angle) * sign]).astype(np.float32)
    w["L0_ffn_centroidsT"] = w.pop("L0_ffn_centroids").T
    w["L0_ffn_WfcT"] = np.concatenate([w.pop("L0_ffn_Wfc_sh"), w.pop("L0_ffn_Wfc_r")]).transpose(0, 2, 1)
    w["L0_ffn_WprojT"] = np.concatenate([w.pop("L0_ffn_Wproj_sh"), w.pop("L0_ffn_Wproj_r")]).transpose(0, 2, 1)
    w["L1_ffn_rb1_cols"] = w.pop("L1_ffn_rb1").reshape(4, 128).T
    w["L1_ffn_eb1_cols"] = w.pop("L1_ffn_eb1").reshape(8, 4, 128).transpose(2, 0, 1)
    w["L2_ffn_b1_cols"] = w.pop("L2_ffn_b1").reshape(4, 128).T
    for name in ("Wg", "Wi", "Wo"):
        w[f"L3_ffn_{name}T"] = w.pop(f"L3_ffn_{name}").T
    w["L3_ffn_AT"] = w.pop("L3_ffn_A").reshape(16, D).T
    w["L3_ffn_BT"] = w.pop("L3_ffn_B").transpose(2, 0, 1).reshape(4, 4 * 512)
    ctx = w.pop("ctx_768").reshape(B, LP, LC, DC)
    w["ctx"] = np.concatenate([ctx, np.ones((B, LP, LC, 1), ctx.dtype)], axis=3)
    w["ctxT"] = w["ctx"].transpose(0, 3, 2, 1)
    w["mask_keys"] = w.pop("mask_BxS2_bf1").reshape(B, LP, LC).transpose(0, 2, 1).reshape(B, L).view(np.uint8)
    w["mask_text"] = w.pop("mask_BxS_bf1").reshape(-1).view(np.uint8)
    for name in ("Wq", "Wk"):
        w[f"L2_xattn_{name}T"] = w.pop(f"L2_xattn_{name}").T
    w["L2_xattn_film_b_cols"] = np.concatenate(
        [w.pop("L2_xattn_b_film_in").reshape(2, D), w.pop("L2_xattn_b_film_out").reshape(2, D)]).T
    w["L2_xattn_b1_cols"] = w.pop("L2_xattn_b1").reshape(4, 128).T
    w["L2_xattn_mod_gate_row"] = w.pop("L2_xattn_mod_gate").reshape(1)
    for layer in (1, 3):
        for name in ("Wq", "Wk", "Wv"):
            w[f"L{layer}_xattn_{name}T"] = w.pop(f"L{layer}_xattn_{name}").T
    w["L0_xattn_WqT"] = w.pop("L0_xattn_Wq").T
    for name in ("Wk", "Wv"):
        w[f"L0_xattn_{name}T"] = w[f"L0_xattn_{name}"].T
    for unused in ("L3_attn_wq", "L3_attn_bq", "L3_attn_wqc", "L3_attn_bqc", "L3_attn_wkc", "L3_attn_bkc"
):
        w.pop(unused)
    return {k: np.ascontiguousarray(v) for k, v in w.items()}


def kernel(**inputs):
    import numpy as np
    import concourse.bacc as bacc
    from concourse.bass_utils import run_bass_kernel_spmd as run

    nc = bacc.Bacc("TRN2", target_bir_lowering=False, num_devices=1)
    arrays, w = {}, {}
    for name, a in laid_out(inputs).items():
        arrays[f"in_{name}"] = a
        w[name] = nc.dram_tensor(f"in_{name}", a.shape, mybir.dt.from_np(a.dtype), kind="ExternalInput").ap()
    w["key_bias"] = nc.dram_tensor("key_bias", (B, 1, LC, LP), F32, kind="Internal").ap()
    out = nc.dram_tensor("out_x", (B, S, D), F32, kind="ExternalOutput").ap()
    build(nc, w, out)
    result = run(nc, [arrays], core_ids=[0])
    return result.results[0]["out_x"]
```
